# Optimizing a Trainium2 kernel written in Bass

```python
import numpy as np
import jax
import jax.numpy as jnp

def _softmax(x, axis=-1):
    return jax.nn.softmax(x, axis=axis)

def _gelu(x):
    return jax.nn.gelu(x, approximate=True)

def _silu(x):
    return jax.nn.silu(x)

def _sigmoid(x):
    return jax.nn.sigmoid(x)

def _layernorm(x, axis=-1, eps=1e-05):
    m = jnp.mean(x, axis=axis, keepdims=True)
    v = jnp.var(x, axis=axis, keepdims=True)
    return (x - m) / jnp.sqrt(v + eps)

def _scatter_add(tgt, idx, src, axis=0):
    return tgt.at[idx].add(src)

def _segment_sum(src, seg, n):
    return jax.ops.segment_sum(src, seg, n)
kernel_name = 'mk_xattn_seq_d2_seqx_r4_96f1b7'

def setup_inputs(seed: int=0):
    np.random.seed(seed)
    _w = jnp.asarray

    def _rec_inputs():
        import jax
        import jax.numpy as jnp
        _rk = jax.random.key(seed)
        x = -0.0002928 + 1 * jax.random.normal(jax.random.fold_in(_rk, 1), (8, 256, 256), jnp.float32)
        _lenS = 256 - jax.random.randint(jax.random.fold_in(_rk, 7), (8,), 0, max(1, 256 // 4) + 1, jnp.int32)
        _lenS2 = 256 - jax.random.randint(jax.random.fold_in(_rk, 8), (8,), 0, max(1, 256 // 4) + 1, jnp.int32)
        _ctx_1024P = jax.random.normal(jax.random.fold_in(_rk, 11), (8, 16, 256), jnp.float32)
        _ctx_1024c = jax.random.dirichlet(jax.random.fold_in(_rk, 511), 0.3 * jnp.ones((16,), jnp.float32), (8, 256))
        _ctx_1024t = jnp.einsum('bsk,bkd->bsd', _ctx_1024c, _ctx_1024P)
        _ctx_1024t = _ctx_1024t * jax.lax.rsqrt(jnp.mean(jnp.square(_ctx_1024t)) + 1e-12) * 0.953939
        ctx_1024 = -1.39393e-06 + 0.999914 * (_ctx_1024t + 0.3 * jax.random.normal(jax.random.fold_in(_rk, 611), (8, 256, 256), jnp.float32))
        return (x, ctx_1024)
    x, ctx_1024 = _rec_inputs()

    def _L0_xattn_setup():
        import jax, jax.numpy as jnp
        import numpy as np
        D_MODEL = 256
        N_HEAD = 16
        DK = D_MODEL // N_HEAD
        LN_EPS = 1e-05

        def _layernorm(x, g, b):
            mu = jnp.mean(x, axis=-1, keepdims=True)
            var = jnp.mean(jnp.square(x - mu), axis=-1, keepdims=True)
            return (x - mu) * jax.lax.rsqrt(var + LN_EPS) * g + b

        def _attn(x_q, x_kv, wq, bq, wk, bk, wv, bv, wo, bo, causal):
            B, Tq, D = x_q.shape
            Tk = x_kv.shape[1]
            Q = (x_q @ wq + bq).reshape(B, Tq, N_HEAD, DK)
            K = (x_kv @ wk + bk).reshape(B, Tk, N_HEAD, DK)
            V = (x_kv @ wv + bv).reshape(B, Tk, N_HEAD, DK)
            scores = jnp.einsum('bqhd,bkhd->bhqk', Q, K) / jnp.sqrt(jnp.float32(DK)).astype(x_q.dtype)
            if causal:
                mask = jnp.tril(jnp.ones((Tq, Tk), dtype=bool))
                scores = jnp.where(mask, scores, jnp.finfo(scores.dtype).min)
            a = jax.nn.softmax(scores, axis=-1)
            out = jnp.einsum('bhqk,bkhd->bqhd', a, V).reshape(B, Tq, D)
            return out @ wo + bo
        key = jax.random.key(seed)
        ks = iter(jax.random.split(key, 32))
        s = 1.0 / np.sqrt(D_MODEL)

        def lin(k, din, dout):
            return jax.random.uniform(k, (din, dout), jnp.float32, -1, 1) / np.sqrt(din)
        inp = {'x': jax.random.normal(next(ks), (2, 512, D_MODEL), jnp.float32), 'x_en': jax.random.normal(next(ks), (2, 512, D_MODEL), jnp.float32)}
        for pre in ('mmha', 'mha'):
            for nm in ('wq', 'wk', 'wv', 'wo'):
                inp[f'{pre}_{nm}'] = lin(next(ks), D_MODEL, D_MODEL)
                inp[f'{pre}_{nm}_b'] = jnp.zeros((D_MODEL,), jnp.float32)
        for i in (1, 2, 3):
            inp[f'ln{i}_g'] = jnp.ones((D_MODEL,), jnp.float32)
            inp[f'ln{i}_b'] = jnp.zeros((D_MODEL,), jnp.float32)
        inp['ffn_w1'] = lin(next(ks), D_MODEL, 4 * D_MODEL)
        inp['ffn_b1'] = jnp.zeros((4 * D_MODEL,), jnp.float32)
        inp['ffn_w2'] = lin(next(ks), 4 * D_MODEL, D_MODEL)
        inp['ffn_b2'] = jnp.zeros((D_MODEL,), jnp.float32)
        return inp
    _L0_xattn_all = _L0_xattn_setup()
    _L0_xattn_in = {k: v for k, v in _L0_xattn_all.items() if k in ('mmha_wq', 'mmha_wq_b', 'mmha_wk', 'mmha_wk_b', 'mmha_wv', 'mmha_wv_b', 'mmha_wo', 'mmha_wo_b', 'mha_wq', 'mha_wq_b', 'mha_wk', 'mha_wk_b', 'mha_wv', 'mha_wv_b', 'mha_wo', 'mha_wo_b', 'ln1_g', 'ln1_b', 'ln2_g', 'ln2_b', 'ln3_g', 'ln3_b', 'ffn_w1', 'ffn_b1', 'ffn_w2', 'ffn_b2')}
    del _L0_xattn_all

    def _L1_xattn_setup():
        import jax, jax.numpy as jnp
        import numpy as np
        B, S, SE, D, H, FF, E, K = (2, 512, 512, 256, 16, 1024, 8, 2)
        HD = D // H

        def _layernorm(x, g, b):
            m = x.mean(-1, keepdims=True)
            v = ((x - m) ** 2).mean(-1, keepdims=True)
            return (x - m) / jnp.sqrt(v + 1e-05) * g + b

        def _attn(q_in, k_in, v_in, wq, bq, wk, bk, wv, bv, wo, bo, causal):
            Bq, Sq, Dm = q_in.shape
            Sk = k_in.shape[1]
            Q = (q_in @ wq + bq).reshape(Bq, Sq, H, HD)
            Kp = (k_in @ wk + bk).reshape(Bq, Sk, H, HD)
            V = (v_in @ wv + bv).reshape(Bq, Sk, H, HD)
            scores = jnp.einsum('bqhd,bkhd->bhqk', Q, Kp) / jnp.sqrt(jnp.float32(HD))
            if causal:
                mask = jnp.tril(jnp.ones((Sq, Sk), bool))
                scores = jnp.where(mask, scores, -jnp.inf)
            a = jax.nn.softmax(scores, axis=-1)
            o = jnp.einsum('bhqk,bkhd->bqhd', a, V).reshape(Bq, Sq, Dm)
            return o @ wo + bo

        def _moe(x, rw, rb, w1, b1, w2, b2):
            T = x.shape[0] * x.shape[1]
            xf = x.reshape(T, D)
            router_weights = jax.nn.softmax(xf @ rw + rb, axis=-1)
            topw, topi = jax.lax.top_k(router_weights, K)
            topw = jax.nn.softmax(topw, axis=-1)
            combine = jnp.zeros((T, E), xf.dtype).at[jnp.arange(T)[:, None], topi].add(topw)
            h = jax.nn.gelu(jnp.einsum('td,edf->etf', xf, w1) + b1[:, None, :], approximate=False)
            eo = jnp.einsum('etf,efd->etd', h, w2) + b2[:, None, :]
            out = jnp.einsum('etd,te->td', eo, combine)
            return out.reshape(x.shape)
        key = jax.random.key(seed)
        ks = jax.random.split(key, 32)
        w = lambda k, shape: jax.random.normal(k, shape, jnp.float32) * 0.02
        inp = {'x': jax.random.normal(ks[0], (B, S, D), jnp.float32), 'encoder_output': jax.random.normal(ks[1], (B, SE, D), jnp.float32), 'sa_wq': w(ks[2], (D, D)), 'sa_bq': jnp.zeros((D,), jnp.float32), 'sa_wk': w(ks[3], (D, D)), 'sa_bk': jnp.zeros((D,), jnp.float32), 'sa_wv': w(ks[4], (D, D)), 'sa_bv': jnp.zeros((D,), jnp.float32), 'sa_wo': w(ks[5], (D, D)), 'sa_bo': jnp.zeros((D,), jnp.float32), 'ca_wq': w(ks[6], (D, D)), 'ca_bq': jnp.zeros((D,), jnp.float32), 'ca_wk': w(ks[7], (D, D)), 'ca_bk': jnp.zeros((D,), jnp.float32), 'ca_wv': w(ks[8], (D, D)), 'ca_bv': jnp.zeros((D,), jnp.float32), 'ca_wo': w(ks[9], (D, D)), 'ca_bo': jnp.zeros((D,), jnp.float32), 'ln1_g': jnp.ones((D,), jnp.float32), 'ln1_b': jnp.zeros((D,), jnp.float32), 'ln2_g': jnp.ones((D,), jnp.float32), 'ln2_b': jnp.zeros((D,), jnp.float32), 'ln3_g': jnp.ones((D,), jnp.float32), 'ln3_b': jnp.zeros((D,), jnp.float32), 'router_w': w(ks[10], (D, E)), 'router_b': jnp.zeros((E,), jnp.float32), 'e_w1': w(ks[11], (E, D, FF)), 'e_b1': jnp.zeros((E, FF), jnp.float32), 'e_w2': w(ks[12], (E, FF, D)), 'e_b2': jnp.zeros((E, D), jnp.float32)}
        return inp
    _L1_xattn_all = _L1_xattn_setup()
    _L1_xattn_in = {k: v for k, v in _L1_xattn_all.items() if k in ('sa_wq', 'sa_bq', 'sa_wk', 'sa_bk', 'sa_wv', 'sa_bv', 'sa_wo', 'sa_bo', 'ca_wq', 'ca_bq', 'ca_wk', 'ca_bk', 'ca_wv', 'ca_bv', 'ca_wo', 'ca_bo', 'ln1_g', 'ln1_b', 'ln2_g', 'ln2_b', 'ln3_g', 'ln3_b', 'router_w', 'router_b', 'e_w1', 'e_b1', 'e_w2', 'e_b2')}
    del _L1_xattn_all
    return {'x': x, 'ctx_1024': ctx_1024, 'L0_xattn_mmha_wq': _L0_xattn_in['mmha_wq'], 'L0_xattn_mmha_wq_b': _L0_xattn_in['mmha_wq_b'], 'L0_xattn_mmha_wk': _L0_xattn_in['mmha_wk'], 'L0_xattn_mmha_wk_b': _L0_xattn_in['mmha_wk_b'], 'L0_xattn_mmha_wv': _L0_xattn_in['mmha_wv'], 'L0_xattn_mmha_wv_b': _L0_xattn_in['mmha_wv_b'], 'L0_xattn_mmha_wo': _L0_xattn_in['mmha_wo'], 'L0_xattn_mmha_wo_b': _L0_xattn_in['mmha_wo_b'], 'L0_xattn_mha_wq': _L0_xattn_in['mha_wq'], 'L0_xattn_mha_wq_b': _L0_xattn_in['mha_wq_b'], 'L0_xattn_mha_wk': _L0_xattn_in['mha_wk'], 'L0_xattn_mha_wk_b': _L0_xattn_in['mha_wk_b'], 'L0_xattn_mha_wv': _L0_xattn_in['mha_wv'], 'L0_xattn_mha_wv_b': _L0_xattn_in['mha_wv_b'], 'L0_xattn_mha_wo': _L0_xattn_in['mha_wo'], 'L0_xattn_mha_wo_b': _L0_xattn_in['mha_wo_b'], 'L0_xattn_ln1_g': _L0_xattn_in['ln1_g'], 'L0_xattn_ln1_b': _L0_xattn_in['ln1_b'], 'L0_xattn_ln2_g': _L0_xattn_in['ln2_g'], 'L0_xattn_ln2_b': _L0_xattn_in['ln2_b'], 'L0_xattn_ln3_g': _L0_xattn_in['ln3_g'], 'L0_xattn_ln3_b': _L0_xattn_in['ln3_b'], 'L0_xattn_ffn_w1': _L0_xattn_in['ffn_w1'], 'L0_xattn_ffn_b1': _L0_xattn_in['ffn_b1'], 'L0_xattn_ffn_w2': _L0_xattn_in['ffn_w2'], 'L0_xattn_ffn_b2': _L0_xattn_in['ffn_b2'], 'L1_xattn_sa_wq': _L1_xattn_in['sa_wq'], 'L1_xattn_sa_bq': _L1_xattn_in['sa_bq'], 'L1_xattn_sa_wk': _L1_xattn_in['sa_wk'], 'L1_xattn_sa_bk': _L1_xattn_in['sa_bk'], 'L1_xattn_sa_wv': _L1_xattn_in['sa_wv'], 'L1_xattn_sa_bv': _L1_xattn_in['sa_bv'], 'L1_xattn_sa_wo': _L1_xattn_in['sa_wo'], 'L1_xattn_sa_bo': _L1_xattn_in['sa_bo'], 'L1_xattn_ca_wq': _L1_xattn_in['ca_wq'], 'L1_xattn_ca_bq': _L1_xattn_in['ca_bq'], 'L1_xattn_ca_wk': _L1_xattn_in['ca_wk'], 'L1_xattn_ca_bk': _L1_xattn_in['ca_bk'], 'L1_xattn_ca_wv': _L1_xattn_in['ca_wv'], 'L1_xattn_ca_bv': _L1_xattn_in['ca_bv'], 'L1_xattn_ca_wo': _L1_xattn_in['ca_wo'], 'L1_xattn_ca_bo': _L1_xattn_in['ca_bo'], 'L1_xattn_ln1_g': _L1_xattn_in['ln1_g'], 'L1_xattn_ln1_b': _L1_xattn_in['ln1_b'], 'L1_xattn_ln2_g': _L1_xattn_in['ln2_g'], 'L1_xattn_ln2_b': _L1_xattn_in['ln2_b'], 'L1_xattn_ln3_g': _L1_xattn_in['ln3_g'], 'L1_xattn_ln3_b': _L1_xattn_in['ln3_b'], 'L1_xattn_router_w': _L1_xattn_in['router_w'], 'L1_xattn_router_b': _L1_xattn_in['router_b'], 'L1_xattn_e_w1': _L1_xattn_in['e_w1'], 'L1_xattn_e_b1': _L1_xattn_in['e_b1'], 'L1_xattn_e_w2': _L1_xattn_in['e_w2'], 'L1_xattn_e_b2': _L1_xattn_in['e_b2']}

def reference(x, ctx_1024, L0_xattn_mmha_wq, L0_xattn_mmha_wq_b, L0_xattn_mmha_wk, L0_xattn_mmha_wk_b, L0_xattn_mmha_wv, L0_xattn_mmha_wv_b, L0_xattn_mmha_wo, L0_xattn_mmha_wo_b, L0_xattn_mha_wq, L0_xattn_mha_wq_b, L0_xattn_mha_wk, L0_xattn_mha_wk_b, L0_xattn_mha_wv, L0_xattn_mha_wv_b, L0_xattn_mha_wo, L0_xattn_mha_wo_b, L0_xattn_ln1_g, L0_xattn_ln1_b, L0_xattn_ln2_g, L0_xattn_ln2_b, L0_xattn_ln3_g, L0_xattn_ln3_b, L0_xattn_ffn_w1, L0_xattn_ffn_b1, L0_xattn_ffn_w2, L0_xattn_ffn_b2, L1_xattn_sa_wq, L1_xattn_sa_bq, L1_xattn_sa_wk, L1_xattn_sa_bk, L1_xattn_sa_wv, L1_xattn_sa_bv, L1_xattn_sa_wo, L1_xattn_sa_bo, L1_xattn_ca_wq, L1_xattn_ca_bq, L1_xattn_ca_wk, L1_xattn_ca_bk, L1_xattn_ca_wv, L1_xattn_ca_bv, L1_xattn_ca_wo, L1_xattn_ca_bo, L1_xattn_ln1_g, L1_xattn_ln1_b, L1_xattn_ln2_g, L1_xattn_ln2_b, L1_xattn_ln3_g, L1_xattn_ln3_b, L1_xattn_router_w, L1_xattn_router_b, L1_xattn_e_w1, L1_xattn_e_b1, L1_xattn_e_w2, L1_xattn_e_b2):
    import jax
    import jax.numpy as jnp

    def _L0_xattn_ref(x, x_en, mmha_wq, mmha_wq_b, mmha_wk, mmha_wk_b, mmha_wv, mmha_wv_b, mmha_wo, mmha_wo_b, mha_wq, mha_wq_b, mha_wk, mha_wk_b, mha_wv, mha_wv_b, mha_wo, mha_wo_b, ln1_g, ln1_b, ln2_g, ln2_b, ln3_g, ln3_b, ffn_w1, ffn_b1, ffn_w2, ffn_b2):
        import jax, jax.numpy as jnp
        import numpy as np
        D_MODEL = 256
        N_HEAD = 16
        DK = D_MODEL // N_HEAD
        LN_EPS = 1e-05

        def _layernorm(x, g, b):
            mu = jnp.mean(x, axis=-1, keepdims=True)
            var = jnp.mean(jnp.square(x - mu), axis=-1, keepdims=True)
            return (x - mu) * jax.lax.rsqrt(var + LN_EPS) * g + b

        def _attn(x_q, x_kv, wq, bq, wk, bk, wv, bv, wo, bo, causal):
            B, Tq, D = x_q.shape
            Tk = x_kv.shape[1]
            Q = (x_q @ wq + bq).reshape(B, Tq, N_HEAD, DK)
            K = (x_kv @ wk + bk).reshape(B, Tk, N_HEAD, DK)
            V = (x_kv @ wv + bv).reshape(B, Tk, N_HEAD, DK)
            scores = jnp.einsum('bqhd,bkhd->bhqk', Q, K) / jnp.sqrt(jnp.float32(DK)).astype(x_q.dtype)
            if causal:
                mask = jnp.tril(jnp.ones((Tq, Tk), dtype=bool))
                scores = jnp.where(mask, scores, jnp.finfo(scores.dtype).min)
            a = jax.nn.softmax(scores, axis=-1)
            out = jnp.einsum('bhqk,bkhd->bqhd', a, V).reshape(B, Tq, D)
            return out @ wo + bo
        h = _layernorm(x, ln1_g, ln1_b)
        x = x + _attn(h, h, mmha_wq, mmha_wq_b, mmha_wk, mmha_wk_b, mmha_wv, mmha_wv_b, mmha_wo, mmha_wo_b, causal=True)
        h = _layernorm(x, ln2_g, ln2_b)
        x = x + _attn(h, x_en, mha_wq, mha_wq_b, mha_wk, mha_wk_b, mha_wv, mha_wv_b, mha_wo, mha_wo_b, causal=False)
        h = _layernorm(x, ln3_g, ln3_b)
        x = x + (jax.nn.relu(h @ ffn_w1 + ffn_b1) @ ffn_w2 + ffn_b2)
        return x

    def _L1_xattn_ref(x, encoder_output, sa_wq, sa_bq, sa_wk, sa_bk, sa_wv, sa_bv, sa_wo, sa_bo, ca_wq, ca_bq, ca_wk, ca_bk, ca_wv, ca_bv, ca_wo, ca_bo, ln1_g, ln1_b, ln2_g, ln2_b, ln3_g, ln3_b, router_w, router_b, e_w1, e_b1, e_w2, e_b2):
        import jax, jax.numpy as jnp
        import numpy as np
        B, S, SE, D, H, FF, E, K = (2, 512, 512, 256, 16, 1024, 8, 2)
        HD = D // H

        def _layernorm(x, g, b):
            m = x.mean(-1, keepdims=True)
            v = ((x - m) ** 2).mean(-1, keepdims=True)
            return (x - m) / jnp.sqrt(v + 1e-05) * g + b

        def _attn(q_in, k_in, v_in, wq, bq, wk, bk, wv, bv, wo, bo, causal):
            Bq, Sq, Dm = q_in.shape
            Sk = k_in.shape[1]
            Q = (q_in @ wq + bq).reshape(Bq, Sq, H, HD)
            Kp = (k_in @ wk + bk).reshape(Bq, Sk, H, HD)
            V = (v_in @ wv + bv).reshape(Bq, Sk, H, HD)
            scores = jnp.einsum('bqhd,bkhd->bhqk', Q, Kp) / jnp.sqrt(jnp.float32(HD))
            if causal:
                mask = jnp.tril(jnp.ones((Sq, Sk), bool))
                scores = jnp.where(mask, scores, -jnp.inf)
            a = jax.nn.softmax(scores, axis=-1)
            o = jnp.einsum('bhqk,bkhd->bqhd', a, V).reshape(Bq, Sq, Dm)
            return o @ wo + bo

        def _moe(x, rw, rb, w1, b1, w2, b2):
            T = x.shape[0] * x.shape[1]
            xf = x.reshape(T, D)
            router_weights = jax.nn.softmax(xf @ rw + rb, axis=-1)
            topw, topi = jax.lax.top_k(router_weights, K)
            topw = jax.nn.softmax(topw, axis=-1)
            combine = jnp.zeros((T, E), xf.dtype).at[jnp.arange(T)[:, None], topi].add(topw)
            h = jax.nn.gelu(jnp.einsum('td,edf->etf', xf, w1) + b1[:, None, :], approximate=False)
            eo = jnp.einsum('etf,efd->etd', h, w2) + b2[:, None, :]
            out = jnp.einsum('etd,te->td', eo, combine)
            return out.reshape(x.shape)
        x = _layernorm(x + _attn(x, x, x, sa_wq, sa_bq, sa_wk, sa_bk, sa_wv, sa_bv, sa_wo, sa_bo, True), ln1_g, ln1_b)
        x = _layernorm(x + _attn(x, encoder_output, encoder_output, ca_wq, ca_bq, ca_wk, ca_bk, ca_wv, ca_bv, ca_wo, ca_bo, False), ln2_g, ln2_b)
        x = _layernorm(x + _moe(x, router_w, router_b, e_w1, e_b1, e_w2, e_b2), ln3_g, ln3_b)
        return x
    x = _L0_xattn_ref(x, ctx_1024, L0_xattn_mmha_wq, L0_xattn_mmha_wq_b, L0_xattn_mmha_wk, L0_xattn_mmha_wk_b, L0_xattn_mmha_wv, L0_xattn_mmha_wv_b, L0_xattn_mmha_wo, L0_xattn_mmha_wo_b, L0_xattn_mha_wq, L0_xattn_mha_wq_b, L0_xattn_mha_wk, L0_xattn_mha_wk_b, L0_xattn_mha_wv, L0_xattn_mha_wv_b, L0_xattn_mha_wo, L0_xattn_mha_wo_b, L0_xattn_ln1_g, L0_xattn_ln1_b, L0_xattn_ln2_g, L0_xattn_ln2_b, L0_xattn_ln3_g, L0_xattn_ln3_b, L0_xattn_ffn_w1, L0_xattn_ffn_b1, L0_xattn_ffn_w2, L0_xattn_ffn_b2)
    x = _L1_xattn_ref(x, ctx_1024, L1_xattn_sa_wq, L1_xattn_sa_bq, L1_xattn_sa_wk, L1_xattn_sa_bk, L1_xattn_sa_wv, L1_xattn_sa_bv, L1_xattn_sa_wo, L1_xattn_sa_bo, L1_xattn_ca_wq, L1_xattn_ca_bq, L1_xattn_ca_wk, L1_xattn_ca_bk, L1_xattn_ca_wv, L1_xattn_ca_bv, L1_xattn_ca_wo, L1_xattn_ca_bo, L1_xattn_ln1_g, L1_xattn_ln1_b, L1_xattn_ln2_g, L1_xattn_ln2_b, L1_xattn_ln3_g, L1_xattn_ln3_b, L1_xattn_router_w, L1_xattn_router_b, L1_xattn_e_w1, L1_xattn_e_b1, L1_xattn_e_w2, L1_xattn_e_b2)
    return x

_drawn_inputs = setup_inputs


def setup_inputs(seed=0):
    import zlib

    import numpy as np

    out = dict(_drawn_inputs(seed))
    spreads = {'L0_xattn_mmha_wq_b': (0.0, 0.8),
     'L0_xattn_mmha_wk_b': (0.0, 2.0),
     'L0_xattn_mmha_wv_b': (0.0, 0.1),
     'L0_xattn_mmha_wo_b': (0.0, 0.1),
     'L0_xattn_mha_wq_b': (0.0, 0.8),
     'L0_xattn_mha_wk_b': (0.0, 2.0),
     'L0_xattn_mha_wv_b': (0.0, 0.1),
     'L0_xattn_mha_wo_b': (0.0, 0.1),
     'L0_xattn_ln1_g': (1.0, 0.6),
     'L0_xattn_ln1_b': (0.0, 0.1),
     'L0_xattn_ln2_g': (1.0, 0.6),
     'L0_xattn_ln2_b': (0.0, 2.0),
     'L0_xattn_ln3_g': (1.0, 0.2),
     'L0_xattn_ln3_b': (0.0, 0.1),
     'L0_xattn_ffn_b1': (0.0, 0.1),
     'L0_xattn_ffn_b2': (0.0, 0.1),
     'L1_xattn_sa_bq': (0.0, 0.8),
     'L1_xattn_sa_bk': (0.0, 2.0),
     'L1_xattn_sa_bv': (0.0, 0.1),
     'L1_xattn_sa_bo': (0.0, 0.1),
     'L1_xattn_ca_bq': (0.0, 0.8),
     'L1_xattn_ca_bk': (0.0, 2.0),
     'L1_xattn_ca_bv': (0.0, 0.1),
     'L1_xattn_ca_bo': (0.0, 0.1),
     'L1_xattn_ln1_g': (1.0, 0.2),
     'L1_xattn_ln1_b': (0.0, 0.1),
     'L1_xattn_ln2_g': (1.0, 0.2),
     'L1_xattn_ln2_b': (0.0, 0.1),
     'L1_xattn_ln3_g': (1.0, 0.2),
     'L1_xattn_ln3_b': (0.0, 0.1),
     'L1_xattn_router_b': (0.0, 0.1),
     'L1_xattn_e_b1': (0.0, 0.364),
     'L1_xattn_e_b2': (0.0, 0.1)}
    factors = {'L0_xattn_mmha_wq': 2.728,
     'L1_xattn_sa_wq': 8.0,
     'L1_xattn_sa_wk': 8.0,
     'L1_xattn_ca_wq': 8.0,
     'L1_xattn_ca_wk': 8.0}
    for name, (base, spread) in spreads.items():
        noise = np.random.default_rng([zlib.crc32(name.encode()), seed]).standard_normal(out[name].shape)
        drawn = base * np.exp(spread * noise) if base else spread * noise
        out[name] = jnp.asarray(drawn.astype(out[name].dtype))
    for name, factor in factors.items():
        out[name] = (out[name] * factor).astype(out[name].dtype)
    return out
```

```python
from contextlib import ExitStack

import numpy as np

import concourse.bass as bass
from concourse import mybir

F32 = mybir.dt.float32
F32R = mybir.dt.float32r
BF16 = mybir.dt.bfloat16
U32 = mybir.dt.uint32
ALU = mybir.AluOpType
ACT = mybir.ActivationFunctionType
AX_X = mybir.AxisListType.X

P = 128
B, S, D = 8, 256, 256
H, DK = 16, 16
FF, E = 1024, 8
TILES = S // P
KC = D // P
FC = FF // P
HPC = H // KC
LANES = 2
TURNS = B // LANES
CALLS = 4
NCALL = CALLS * LANES
ALL_TILES = B * TILES
EPS = 1e-5
SCALE = DK ** -0.5
MASKED = -1e30
FFN, FINAL = "ffn", "final"
CAUSAL = (True, False, True, False)


def plan_slot(s):
    lane, c = s % LANES, s // LANES
    steps = []
    if c == 0:
        steps += [(0, "fetch", lane, 0), (0, "ctx", lane, 0), (0, "ln", lane, 0), (1, "T", lane, 0)]
        first = 3
    else:
        steps += [(0, "turn", lane, c - 1), (0, "out_T", lane, c - 1), (1, "wo", lane, c - 1)]
        if c == 2:
            steps += [(1, "ln", lane, FFN), (3, "T", lane, FFN)]
            steps += [(4 + j, "up", lane, j) for j in range(FC // 2)]
            steps += [(8, "down", lane, FFN), (9, "T", lane, 2)]
            first = 10
        elif c == CALLS:
            steps += [(1, "ln", lane, FINAL), (2, "store", lane, FINAL)]
        else:
            steps += [(1, "ln", lane, c), (3, "T", lane, c)]
            first = 5
    if c < CALLS:
        steps += [(first, "q", lane, c), (first, "k", lane, c), (first, "v", lane, c)]
        steps += [(min(16, first + 3 + h // 2), "max", lane, (c, h)) for h in range(H)]
        steps += [(16, "shift", lane, c)]
    return steps


SLOTS = [plan_slot(s) for s in range(NCALL + LANES)]


def count_steps():
    place, total = {}, {}
    for steps in SLOTS:
        for _, kind, lane, arg in steps:
            place[kind, lane, arg] = total.get(kind, 0)
            total[kind] = total.get(kind, 0) + 1
    return place, total


PLACE, TOTAL = count_steps()
WORK_BANKS = 2
FREE_AT_FIRST = 1
USES = {"ctx": 1, "T": 1, "q": 1, "k": 1, "v": 1, "shift": 1, "turn": 2, "out_T": 1, "wo": 1, "up": 1, "down": 1}


def count_work():
    uses, n = {}, 0
    for steps in SLOTS:
        for _, kind, lane, arg in steps:
            for j in range(USES.get(kind, 0)):
                uses[kind, lane, arg, j] = (n, n % WORK_BANKS, n // WORK_BANKS)
                n += 1
    return uses, n, [len(range(b, n, WORK_BANKS)) for b in range(WORK_BANKS)]


WORK, WORK_TOTAL, WORK_PER_BANK = count_work()


def build(nc, t, out):
    with ExitStack() as ctx:
        sb = lambda name, shape, dt=F32: ctx.enter_context(nc.sbuf_tensor(name, shape, dt))
        sem = lambda name: ctx.enter_context(nc.semaphore(name))
        x_all = sb("x_all", [P, ALL_TILES, D])
        ident = sb("ident", [P, P])
        minus_half = sb("minus_half", [P, TILES])
        attention_part(nc, t, x_all, ident, minus_half)
        moe_part(nc, t, out, x_all, ident, minus_half)


def attention_part(nc, t, x_all, ident, minus_half):
    with ExitStack() as ctx:
        def sb(name, shape, dt=F32):
            return ctx.enter_context(nc.sbuf_tensor(name, shape, dt))

        def per_lane(name, shape, dt=F32):
            return [sb(f"{name}{lane}", shape, dt) for lane in range(LANES)]

        def psum(name):
            return ctx.enter_context(nc.psum_tensor(name, [P, 512], F32))

        def sem(name):
            return ctx.enter_context(nc.semaphore(name))

        wq = [sb(f"wq{c}", [P, KC, D]) for c in range(CALLS)]
        wk = [sb(f"wk{c}", [P, KC, D]) for c in range(CALLS)]
        wv = [sb(f"wv{c}", [P, KC, D]) for c in range(CALLS)]
        wo = [sb(f"wo{c}", [P, KC, D]) for c in range(CALLS)]
        w1 = sb("w1", [P, KC, FF])
        w2 = sb("w2", [P, FC, D])
        bq = sb("bq", [P, CALLS, KC])
        bk = sb("bk", [P, CALLS, KC])
        b1 = sb("b1", [P, FC])
        bv = sb("bv", [P, CALLS, D])
        bo = sb("bo", [P, CALLS, D])
        b2 = sb("b2", [P, D])
        stages = {0: "L0_xattn_ln1", 1: "L0_xattn_ln2", FFN: "L0_xattn_ln3", 3: "L1_xattn_ln1", FINAL: "L1_xattn_ln2"}
        gain = {k: sb(f"gain_{k}", [P, D]) for k in stages}
        shift = {k: sb(f"shift_{k}", [P, D]) for k in stages}
        ident_b = sb("ident_b", [P, P], BF16)
        mask_qk = sb("mask_qk", [P, P], BF16)
        mask_kq = sb("mask_kq", [P, P], BF16)
        x_in = per_lane("x_in", [P, TILES, D])
        ctx_in = per_lane("ctx_in", [P, TILES, D])
        x = per_lane("x", [P, TILES, D])
        h = per_lane("h", [P, TILES, D])
        hT = per_lane("hT", [P, KC, S])
        cT = per_lane("cT", [P, KC, S])
        q_stack = per_lane("q_stack", [P, HPC, S], F32R)
        k_stack = per_lane("k_stack", [P, HPC, S], F32R)
        v = per_lane("v", [P, TILES, H, 2 * DK])
        u = per_lane("u", [P, H // 4, S])
        q_hi, q_lo, k_hi, k_lo = (sb(n, [P, KC, S], F32R) for n in ("q_hi", "q_lo", "k_hi", "k_lo"))
        neg_max = sb("neg_max", [P, TILES, H])
        neg_max_T = sb("neg_max_T", [H, S], F32R)
        probs = [sb(f"probs{i}", [P, TILES * S]) for i in range(2)]
        inv_sum = sb("inv_sum", [P, TILES, H])
        o = sb("o", [P, TILES, D])
        oT = sb("oT", [P, KC, S])
        hidden = sb("hidden", [P, FC, S])
        stats = sb("stats", [P, TILES, 6])
        mean_var = sb("mean_var", [P, TILES, 2])
        var_eps = sb("var_eps", [P, TILES])
        rstd = sb("rstd", [P, TILES])
        centred = sb("centred", [P, TILES, D])
        raw_q = [hidden[:, 2 * c:2 * c + 2, :] for c in range(CALLS)]
        raw_k = [u[c // 2][:, 2 * (c % 2):2 * (c % 2) + 2, :] for c in range(CALLS)]
        work = [psum(f"work{i}") for i in range(WORK_BANKS)]
        s1 = [psum(f"s1_{i}") for i in range(2)]
        s2 = [psum(f"s2_{i}") for i in range(2)]
        pv = [psum(f"pv{i}") for i in range(2)]
        consts = sem("consts")
        loaded = [sem(f"loaded{c}") for c in range(CALLS)]
        loaded_ffn = sem("loaded_ffn")
        reordered = sem("reordered")
        loaded_rows = sem("loaded_rows")
        seq_in = [sem(f"seq_in{i}") for i in range(LANES)]
        x_taken = sem("x_taken")
        work_full = sem("work_full")
        work_free = [sem(f"work_free{i}") for i in range(WORK_BANKS)]
        var_ready = sem("var_ready")
        rstd_ready = sem("rstd_ready")
        h_ready = sem("h_ready")
        ctx_T_ready = sem("ctx_T_ready")
        hT_ready = sem("hT_ready")
        q_hi_ready = sem("q_hi_ready")
        k_hi_ready = sem("k_hi_ready")
        q_lo_ready = sem("q_lo_ready")
        k_lo_ready = sem("k_lo_ready")
        v_ready = sem("v_ready")
        stacked = sem("stacked")
        shift_T_ready = sem("shift_T_ready")
        shift_stacked = sem("shift_stacked")
        s1_full = sem("s1_full")
        s1_free = [sem(f"s1_free{i}") for i in range(2)]
        s2_full = sem("s2_full")
        probs_ready = sem("probs_ready")
        probs_used = [sem(f"probs_used{i}") for i in range(2)]
        u_ready = [sem(f"u_ready{i}") for i in range(2)]
        o_ready = sem("o_ready")
        oT_ready = sem("oT_ready")
        x_biased = sem("x_biased")
        x_ready = sem("x_ready")
        hidden_ready = sem("hidden_ready")
        stored = sem("stored")

        def nth(it, kind, lane, arg):
            return it * TOTAL[kind] + PLACE[kind, lane, arg] + 1

        def filled(it, kind, lane, arg, j=0):
            return it * WORK_TOTAL + WORK[kind, lane, arg, j][0] + 1

        def bank(kind, lane, arg, j=0):
            return work[WORK[kind, lane, arg, j][1]]

        def freed(kind, lane, arg, j=0):
            return work_free[WORK[kind, lane, arg, j][1]]

        def bank_uses(it, kind, lane, arg, j=0):
            _, b, k = WORK[kind, lane, arg, j]
            return it * WORK_PER_BANK[b] + k + FREE_AT_FIRST

        def call(it, n):
            return it * NCALL + n

        def run(engine, it, step, head):
            for s, steps in enumerate(SLOTS):
                n = s - 1
                heads = 0 <= n < NCALL
                for pos in range(H + 1):
                    for at, kind, lane, arg in steps:
                        if at == pos and kind in step:
                            step[kind](it, lane, arg)
                    if heads:
                        head(it, n, pos)

        layers = ["L0_xattn_mmha_w{}", "L0_xattn_mha_w{}", "L1_xattn_sa_w{}", "L1_xattn_ca_w{}"]
        biases = ["L0_xattn_mmha_w{}_b", "L0_xattn_mha_w{}_b", "L1_xattn_sa_b{}", "L1_xattn_ca_b{}"]
        ROW_LOADS = 2 * CALLS + 1 + 2 * len(stages)
        BIAS_LOADS = 2 * CALLS * KC + 1

        block = ctx.enter_context(nc.Block())

        @block.sync
        def _(sp):
            def load_sequence(it, lane):
                for src, dst in ((t["x"], x_in[lane]), (t["ctx_1024"], ctx_in[lane])):
                    rows = src.rearrange("b (t p) d -> p (b t) d", p=P)
                    sp.dma_start(dst[:], rows[:, bass.ds((it * LANES + lane) * TILES, TILES), :]).then_inc(seq_in[lane], 16)

            load_sequence(0, 0)
            for c in range(CALLS):
                for w, key in ((raw_q, "q"), (raw_k, "k"), (wv, "v"), (wo, "o")):
                    sp.dma_start(w[c][:], t[layers[c].format(key)].rearrange("(k p) n -> p k n", p=P)).then_inc(loaded[c], 16)
                if c == 0:
                    load_sequence(0, 1)
            for w, name in ((w1, "L0_xattn_ffn_w1"), (w2, "L0_xattn_ffn_w2")):
                sp.dma_start(w[:], t[name].rearrange("(k p) n -> p k n", p=P)).then_inc(loaded_ffn, 16)

            def stack_q(it, lane, c):
                sp.wait_ge(q_hi_ready, nth(it, "q", lane, c))
                for half in range(KC):
                    for row in (0, 2 * DK):
                        at = half * 64 + row
                        sp.dma_start(q_stack[lane][at:at + DK].bitcast(F32), q_hi[:, half, :].bitcast(F32)).then_inc(stacked, 16)
                sp.wait_ge(q_lo_ready, nth(it, "q", lane, c))
                for half in range(KC):
                    at = half * 64 + DK
                    sp.dma_start(q_stack[lane][at:at + DK].bitcast(F32), q_lo[:, half, :].bitcast(F32)).then_inc(stacked, 16)

            def stack_k(it, lane, c):
                sp.wait_ge(k_hi_ready, nth(it, "k", lane, c))
                for half in range(KC):
                    for row in (0, DK):
                        at = half * 64 + row
                        sp.dma_start(k_stack[lane][at:at + DK].bitcast(F32), k_hi[:, half, :].bitcast(F32)).then_inc(stacked, 16)
                sp.wait_ge(k_lo_ready, nth(it, "k", lane, c))
                for half in range(KC):
                    at = half * 64 + 2 * DK
                    sp.dma_start(k_stack[lane][at:at + DK].bitcast(F32), k_lo[:, half, :].bitcast(F32)).then_inc(stacked, 16)

            def stack_shift(it, lane, c):
                sp.wait_ge(shift_T_ready, nth(it, "shift", lane, c))
                for half in range(KC):
                    at = half * 64 + 3 * DK
                    sp.dma_start(q_stack[lane][at:at + 1].bitcast(F32), neg_max_T[half * HPC:(half + 1) * HPC, :].bitcast(F32)).then_inc(shift_stacked, 16)

            def next_sequence(it, lane, c):
                if c == 0:
                    sp.wait_ge(x_taken, nth(it, "fetch", lane, 0))
                    sp.wait_ge(ctx_T_ready, nth(it, "ctx", lane, 0))
                    load_sequence((it + 1) % TURNS, lane)

            def shift_and_next(it, lane, c):
                stack_shift(it, lane, c)
                next_sequence(it, lane, c)

            with sp.Fori(0, TURNS) as it:
                run(sp, it, {"q": stack_q, "k": stack_k, "shift": shift_and_next}, lambda it, n, pos: None)
            for lane in range(LANES):
                sp.wait_ge(seq_in[lane], 32 * (TURNS + 1))

        @block.gpsimd
        def _(pool):
            pool.memset(ident[:], 0.0)
            pool.memset(minus_half[:], -0.5)
            pool.memset(mask_qk[:], 0.0)
            pool.memset(mask_kq[:], 0.0)
            pool.memset(ident_b[:], 0.0)
            for lane in range(LANES):
                pool.memset(v[lane][:], 1.0)
            pool.drain()
            for m in (ident, ident_b):
                pool.affine_select(out=m[:], in_=m[:], compare_op=ALU.not_equal, fill=1.0, base=0, pattern=[[-1, P]], channel_multiplier=1)
            pool.affine_select(out=mask_qk[:], in_=mask_qk[:], compare_op=ALU.is_ge, fill=MASKED, base=0, pattern=[[-1, P]], channel_multiplier=1)
            pool.affine_select(out=mask_kq[:], in_=mask_kq[:], compare_op=ALU.is_ge, fill=MASKED, base=0, pattern=[[1, P]], channel_multiplier=-1)
            pool.drain()
            pool.sem_inc(consts, 1)
            for c in range(CALLS):
                for dst, key in ((bq, "q"), (bk, "k")):
                    for half in range(KC):
                        src = t[biases[c].format(key)].rearrange("(c i d) -> c d i", c=KC, d=DK)[half]
                        with nc.allow_non_contiguous_dma(reason="128 biases"):
                            pool.dma_start(dst[:, c, half:half + 1], src.rearrange("d (i a) -> d i a", a=1)).then_inc(loaded_rows, 16)
                for dst, key in ((bv, "v"), (bo, "o")):
                    pool.dma_start(dst[:, c, :], t[biases[c].format(key)].partition_broadcast(P)).then_inc(loaded_rows, 16)
            with nc.allow_non_contiguous_dma(reason="1024 biases"):
                pool.dma_start(b1[:], t["L0_xattn_ffn_b1"].rearrange("(f p) -> p f", p=P)).then_inc(loaded_rows, 16)
            pool.dma_start(b2[:], t["L0_xattn_ffn_b2"].partition_broadcast(P)).then_inc(loaded_rows, 16)
            for k, name in stages.items():
                pool.dma_start(gain[k][:], t[name + "_g"].partition_broadcast(P)).then_inc(loaded_rows, 16)
                pool.dma_start(shift[k][:], t[name + "_b"].partition_broadcast(P)).then_inc(loaded_rows, 16)
            pool.wait_ge(loaded_rows, 16 * (ROW_LOADS + BIAS_LOADS))

            def inverse_root(it, lane, stage):
                pool.wait_ge(var_ready, nth(it, "ln", lane, stage))
                pool.tensor_tensor(rstd[:], var_eps[:], minus_half[:], ALU.pow).then_inc(rstd_ready, 1)

            def add_bias(it, lane, stage):
                pool.wait_ge(work_full, filled(it, "T", lane, stage))
                row = b2[:] if stage == FFN else bo[:, stage, :]
                pool.tensor_tensor(x[lane][:], x[lane][:], row.unsqueeze(1).to_broadcast([P, TILES, D]), ALU.add).then_inc(x_biased, 1)

            def store(it, lane, _):
                pool.wait_ge(h_ready, nth(it, "ln", lane, FINAL))
                pool.wait_ge(consts, 1)
                pool.tensor_copy(x_all[:, bass.ds((it * LANES + lane) * TILES, TILES), :], x[lane][:]).then_inc(stored, 1)

            with pool.Fori(0, TURNS) as it:
                run(pool, it, {"ln": inverse_root, "T": add_bias, "store": store}, lambda it, n, pos: None)

        @block.tensor
        def _(pe):
            for free in (*work_free, *s1_free, *u_ready, *probs_used, stored):
                pe.sem_inc(free, FREE_AT_FIRST)
            pe.wait_ge(consts, 1)

            def take(it, kind, lane, arg, j=0):
                pe.wait_ge(freed(kind, lane, arg, j), bank_uses(it, kind, lane, arg, j))
                return bank(kind, lane, arg, j)

            def transpose_rows(dst, src):
                for k in range(KC):
                    for i in range(TILES):
                        last = pe.transpose(dst[:, k * S + i * P:k * S + (i + 1) * P], src[:, i, k * P:(k + 1) * P], ident[:])
                return last

            def ctx_T(it, lane, _):
                pe.wait_ge(seq_in[lane], 32 * (it + 1))
                transpose_rows(take(it, "ctx", lane, 0), ctx_in[lane]).then_inc(work_full, 1)

            def rows_T(it, lane, stage):
                if stage == 2:
                    pe.wait_ge(x_ready, it * (TOTAL["wo"] + TOTAL["down"]) + X_PLACE["down", lane, FFN] + 1)
                    src = x[lane]
                else:
                    pe.wait_ge(h_ready, nth(it, "ln", lane, stage))
                    src = x[lane] if stage == 3 else h[lane]
                transpose_rows(take(it, "T", lane, stage), src).then_inc(work_full, 1)

            def project(it, kind, lane, c, w, src):
                dst = take(it, kind, lane, c)
                for half in range(KC):
                    for k in range(KC):
                        last = pe.matmul(dst[:, half * S:(half + 1) * S], w[c][:, k, half * P:(half + 1) * P], src[:, k, :], start=(k == 0), stop=(k == KC - 1))
                last.then_inc(work_full, 1)

            def project_q(it, lane, c):
                pe.wait_ge(reordered, c + 1)
                pe.wait_ge(hT_ready, nth(it, "T", lane, c))
                project(it, "q", lane, c, wq, hT[lane])

            def project_k(it, lane, c):
                if not CAUSAL[c]:
                    pe.wait_ge(ctx_T_ready, nth(it, "ctx", lane, 0))
                project(it, "k", lane, c, wk, hT[lane] if CAUSAL[c] else cT[lane])

            def project_rows(it, kind, lane, arg, w, src, chunks):
                dst = take(it, kind, lane, arg)
                for i in range(TILES):
                    for k in range(chunks):
                        last = pe.matmul(dst[:, i * D:(i + 1) * D], src[:, k, i * P:(i + 1) * P], w[:, k, :], start=(k == 0), stop=(k == chunks - 1))
                last.then_inc(work_full, 1)

            def project_v(it, lane, c):
                project_rows(it, "v", lane, c, wv[c], hT[lane] if CAUSAL[c] else cT[lane], KC)

            def scores_for_max(it, lane, arg):
                c, hd = arg
                n = c * LANES + lane
                if hd == 0:
                    pe.wait_ge(stacked, 16 * 12 * (call(it, n) + 1))
                pe.wait_ge(s1_free[hd % 2], call(it, n) * (H // 2) + hd // 2 + FREE_AT_FIRST)
                i, r = hd % HPC, 64 * (hd // HPC)
                dst = s1[hd % 2]
                for qt in range(TILES):
                    keys = (qt + 1) * P if CAUSAL[c] else S
                    last = pe.matmul(dst[:, qt * S:qt * S + keys], q_stack[lane][r:r + 3 * DK, i, qt * P:(qt + 1) * P],
                                     k_stack[lane][r:r + 3 * DK, i, 0:keys], start=True, stop=not CAUSAL[c])
                    if CAUSAL[c]:
                        last = pe.matmul(dst[:, qt * S + qt * P:qt * S + keys], ident_b[:], mask_qk[:], start=False, stop=True)
                last.then_inc(s1_full, 1)

            def shift_T(it, lane, c):
                n = c * LANES + lane
                for i in range(2):
                    pe.wait_ge(s1_free[i], (call(it, n) + 1) * (H // 2) + FREE_AT_FIRST)
                dst = take(it, "shift", lane, c)
                for qt in range(TILES):
                    last = pe.transpose(dst[0:H, qt * P:(qt + 1) * P], neg_max[:, qt, :], ident[:])
                last.then_inc(work_full, 1)

            def scores(it, n, hd):
                lane, c = n % LANES, n // LANES
                if hd == 0:
                    pe.wait_ge(shift_stacked, 16 * 2 * (call(it, n) + 1))
                i, r = hd % HPC, 64 * (hd // HPC)
                dst = s2[hd % 2]
                for kt in range(TILES):
                    q0 = kt * P if CAUSAL[c] else 0
                    last = pe.matmul(dst[:, kt * S:kt * S + S - q0], k_stack[lane][r:r + 3 * DK + 1, i, kt * P:(kt + 1) * P],
                                     q_stack[lane][r:r + 3 * DK + 1, i, q0:S], start=True, stop=not CAUSAL[c])
                    if CAUSAL[c]:
                        last = pe.matmul(dst[:, kt * S:kt * S + P], ident_b[:], mask_kq[:], start=False, stop=True)
                last.then_inc(s2_full, 1)

            def weigh_values(it, n, hd):
                lane, c = n % LANES, n // LANES
                half = (hd // 4) % 2
                dst = pv[hd // 8]
                if hd == 0:
                    pe.wait_ge(v_ready, nth(it, "v", lane, c))
                if hd % 8 == 0:
                    pe.wait_ge(u_ready[hd // 8], call(it, n) + FREE_AT_FIRST)
                pe.wait_ge(probs_ready, call(it, n) * H + hd + 1)
                rows = slice(32 * (hd % 4), 32 * (hd % 4) + 32)
                for kt in range(TILES):
                    q0 = kt * P if CAUSAL[c] else 0
                    last = pe.matmul(dst[rows, half * S + q0:(half + 1) * S], v[lane][:, kt, hd, :],
                                     probs[hd % 2][:, kt * S:kt * S + S - q0], start=(kt == 0), stop=(kt == TILES - 1))
                last.then_inc(probs_used[hd % 2], 1)

            def head(it, n, pos):
                if pos == 0:
                    scores(it, n, 0)
                if pos + 1 < H:
                    scores(it, n, pos + 1)
                if pos < H:
                    weigh_values(it, n, pos)

            def turn(it, lane, c):
                n = c * LANES + lane
                for i in range(2):
                    pe.wait_ge(u_ready[i], call(it, n) + 1 + FREE_AT_FIRST)
                for qt in range(TILES):
                    dst = take(it, "turn", lane, c, qt)
                    for g in range(H // 4):
                        last = pe.transpose(dst[:, g * P:(g + 1) * P], u[lane][:, g, qt * P:(qt + 1) * P], ident[:])
                    last.then_inc(work_full, 1)

            def out_T(it, lane, c):
                pe.wait_ge(o_ready, nth(it, "turn", lane, c))
                transpose_rows(take(it, "out_T", lane, c), o).then_inc(work_full, 1)

            def out_project(it, lane, c):
                pe.wait_ge(oT_ready, nth(it, "out_T", lane, c))
                project_rows(it, "wo", lane, c, wo[c], oT, KC)

            def up(it, lane, j):
                if j == 0:
                    pe.wait_ge(loaded_ffn, 16 * 2)
                    pe.wait_ge(hT_ready, nth(it, "T", lane, FFN))
                dst = take(it, "up", lane, j)
                for m in range(2):
                    f = 2 * j + m
                    for k in range(KC):
                        last = pe.matmul(dst[:, m * S:(m + 1) * S], w1[:, k, f * P:(f + 1) * P], hT[lane][:, k, :], start=(k == 0), stop=(k == KC - 1))
                last.then_inc(work_full, 1)

            def down(it, lane, _):
                pe.wait_ge(hidden_ready, nth(it, "up", lane, FC // 2 - 1))
                project_rows(it, "down", lane, FFN, w2, hidden, FC)

            with pe.Fori(0, TURNS) as it:
                run(pe, it, {"ctx": ctx_T, "T": rows_T, "q": project_q, "k": project_k, "v": project_v, "max": scores_for_max,
                             "shift": shift_T, "turn": turn, "out_T": out_T, "wo": out_project, "up": up, "down": down}, head)

        @block.scalar
        def _(act):
            act.wait_ge(loaded_rows, 16 * (ROW_LOADS + BIAS_LOADS))

            def fetch(it, lane, _):
                act.wait_ge(seq_in[lane], 32 * (it + 1))
                act.wait_ge(stored, it * LANES + FREE_AT_FIRST)
                act.activation(x[lane][:], x_in[lane][:], ACT.Copy).then_inc(x_taken, 1)

            def ctx_T(it, lane, _):
                act.wait_ge(work_full, filled(it, "ctx", lane, 0))
                act.activation(cT[lane][:].rearrange("p k s -> p (k s)"), bank("ctx", lane, 0)[:], ACT.Copy).then_inc(freed("ctx", lane, 0), 1)
                act.drain()
                act.sem_inc(ctx_T_ready, 1)

            def rows_T(it, lane, stage):
                act.wait_ge(work_full, filled(it, "T", lane, stage))
                act.activation(hT[lane][:].rearrange("p k s -> p (k s)"), bank("T", lane, stage)[:], ACT.Copy).then_inc(freed("T", lane, stage), 1)
                act.drain()
                act.sem_inc(hT_ready, 1)

            def hi_part(kind, dst, bias, ready):
                def step(it, lane, c):
                    act.wait_ge(work_full, filled(it, kind, lane, c))
                    for half in range(KC):
                        last = act.activation(dst[:, half, :], bank(kind, lane, c)[:, half * S:(half + 1) * S], ACT.Identity, bias=bias[:, c, half:half + 1])
                    last.then_inc(ready, 1)
                return step

            def shift_T(it, lane, c):
                act.wait_ge(work_full, filled(it, "shift", lane, c))
                act.activation(neg_max_T[:], bank("shift", lane, c)[0:H, 0:S], ACT.Copy).then_inc(shift_T_ready, 1)
                act.drain()
                act.sem_inc(freed("shift", lane, c), 1)

            def out_T(it, lane, c):
                act.wait_ge(work_full, filled(it, "out_T", lane, c))
                act.activation(oT[:].rearrange("p k s -> p (k s)"), bank("out_T", lane, c)[:], ACT.Copy).then_inc(oT_ready, 1)
                act.drain()
                act.sem_inc(freed("out_T", lane, c), 1)

            def up(it, lane, j):
                act.wait_ge(work_full, filled(it, "up", lane, j))
                for m in range(2):
                    f = 2 * j + m
                    act.activation(hidden[:, f, :], bank("up", lane, j)[:, m * S:(m + 1) * S], ACT.Relu, bias=b1[:, f:f + 1])
                act.drain()
                act.sem_inc(freed("up", lane, j), 1)
                act.sem_inc(hidden_ready, 1)

            def head(it, n, pos):
                if pos == H:
                    return
                width = S + P if CAUSAL[n // LANES] else TILES * S
                act.wait_ge(s2_full, call(it, n) * H + pos + 1)
                act.wait_ge(probs_used[pos % 2], call(it, n) * (H // 2) + pos // 2 + FREE_AT_FIRST)
                act.activation(probs[pos % 2][:, 0:width], s2[pos % 2][:, 0:width], ACT.Exp, scale=SCALE).then_inc(probs_ready, 1)

            with act.Fori(0, TURNS) as it:
                run(act, it, {"fetch": fetch, "ctx": ctx_T, "T": rows_T, "q": hi_part("q", q_hi, bq, q_hi_ready), "k": hi_part("k", k_hi, bk, k_hi_ready),
                              "shift": shift_T, "out_T": out_T, "up": up}, head)

        @block.vector
        def _(dve):
            for lane in range(LANES):
                for r in (32, 96):
                    dve.memset(k_stack[lane][r:r + 32].bitcast(F32), 1.0)
            dve.drain()
            for c in range(CALLS):
                dve.wait_ge(loaded[c], 16 * 4)
                for w, raw in ((wq, raw_q), (wk, raw_k)):
                    for k in range(KC):
                        for half in range(KC):
                            last = dve.tensor_copy(w[c][:, k, half * P:(half + 1) * P].rearrange("p (d i) -> p d i", d=DK),
                                                   raw[c][:, k, half * P:(half + 1) * P].rearrange("p (i d) -> p d i", d=DK))
                last.then_inc(reordered, 1)
            dve.drain()
            dve.wait_ge(loaded_rows, 16 * (ROW_LOADS + BIAS_LOADS))
            dve.wait_ge(consts, 1)

            def norm(it, lane, stage):
                if stage == 0:
                    dve.wait_ge(x_taken, nth(it, "fetch", lane, 0))
                src, dst = x[lane], (x[lane] if stage in (3, FINAL) else h[lane])
                for i in range(TILES):
                    dve.bn_stats(stats[:, i, :], src[:, i, :])
                dve.drain()
                for i in range(TILES):
                    dve.bn_aggr(mean_var[:, i, :], stats[:, i, :])
                dve.drain()
                dve.tensor_scalar(var_eps[:], mean_var[:, :, 1], EPS, None, ALU.add).then_inc(var_ready, 1)
                for i in range(TILES):
                    dve.scalar_tensor_tensor(out=centred[:, i, :], in0=src[:, i, :], scalar=mean_var[:, i, 0:1], in1=gain[stage][:], op0=ALU.subtract, op1=ALU.mult)
                dve.drain()
                dve.wait_ge(rstd_ready, nth(it, "ln", lane, stage))
                for i in range(TILES):
                    last = dve.scalar_tensor_tensor(out=dst[:, i, :], in0=centred[:, i, :], scalar=rstd[:, i:i + 1], in1=shift[stage][:], op0=ALU.mult, op1=ALU.add)
                last.then_inc(h_ready, 1)
                dve.drain()

            def lo_part(kind, hi, dst, bias, hi_ready, ready):
                def step(it, lane, c):
                    dve.wait_ge(hi_ready, nth(it, kind, lane, c))
                    for half in range(KC):
                        dve.scalar_tensor_tensor(out=dst[:, half, :], in0=bank(kind, lane, c)[:, half * S:(half + 1) * S], scalar=bias[:, c, half:half + 1],
                                                 in1=hi[:, half, :].bitcast(F32), op0=ALU.add, op1=ALU.subtract)
                    dve.drain()
                    dve.sem_inc(ready, 1)
                    dve.sem_inc(freed(kind, lane, c), 1)
                return step

            def values(it, lane, c):
                dve.wait_ge(work_full, filled(it, "v", lane, c))
                for i in range(TILES):
                    dve.tensor_tensor(v[lane][:, i, :, 0:DK], bank("v", lane, c)[:, i * D:(i + 1) * D].rearrange("p (h d) -> p h d", d=DK),
                                      bv[:, c, :].rearrange("p (h d) -> p h d", d=DK), ALU.add)
                dve.drain()
                dve.sem_inc(v_ready, 1)
                dve.sem_inc(freed("v", lane, c), 1)

            def row_max(it, lane, arg):
                c, hd = arg
                n = c * LANES + lane
                dve.wait_ge(s1_full, call(it, n) * H + hd + 1)
                src = s1[hd % 2]
                if CAUSAL[c]:
                    dve.tensor_reduce(neg_max[:, 0, hd:hd + 1], src[:, 0:P], AX_X, ALU.max, negate=True)
                    last = dve.tensor_reduce(neg_max[:, 1, hd:hd + 1], src[:, S:2 * S], AX_X, ALU.max, negate=True)
                else:
                    last = dve.tensor_reduce(neg_max[:, :, hd], src[:].rearrange("p (t s) -> p t s", t=TILES), AX_X, ALU.max, negate=True)
                last.then_inc(s1_free[hd % 2], 1)

            def copy_out(it, n, i):
                dve.wait_ge(probs_used[1], call(it, n) * (H // 2) + 4 * (i + 1) + FREE_AT_FIRST)
                dve.tensor_copy(u[n % LANES][:, 2 * i:2 * i + 2, :].rearrange("p g s -> p (g s)"), pv[i][:]).then_inc(u_ready[i], 1)

            def head(it, n, pos):
                if pos == 9:
                    copy_out(it, n, 0)
                if pos == H:
                    copy_out(it, n, 1)

            def normalise(it, lane, c):
                for qt in range(TILES):
                    dve.wait_ge(work_full, filled(it, "turn", lane, c, qt))
                    src = bank("turn", lane, c, qt)[:].rearrange("p (h e) -> p h e", e=2 * DK)
                    dve.reciprocal(inv_sum[:, qt, :], src[:, :, DK])
                    dve.drain()
                    dve.tensor_tensor(o[:, qt, :].rearrange("p (h d) -> p h d", d=DK), src[:, :, 0:DK],
                                      inv_sum[:, qt, :].unsqueeze(2).to_broadcast([P, H, DK]), ALU.mult).then_inc(freed("turn", lane, c, qt), 1)
                dve.drain()
                dve.sem_inc(o_ready, 1)

            def residual(it, kind, lane, arg, stage):
                dve.wait_ge(work_full, filled(it, kind, lane, arg))
                dve.wait_ge(x_biased, nth(it, "T", lane, stage))
                dve.tensor_tensor(x[lane][:], x[lane][:], bank(kind, lane, arg)[:].rearrange("p (t d) -> p t d", t=TILES), ALU.add).then_inc(x_ready, 1)
                dve.drain()
                dve.sem_inc(freed(kind, lane, arg), 1)

            with dve.Fori(0, TURNS) as it:
                run(dve, it, {"ln": norm, "q": lo_part("q", q_hi, q_lo, bq, q_hi_ready, q_lo_ready), "k": lo_part("k", k_hi, k_lo, bk, k_hi_ready, k_lo_ready),
                              "v": values, "max": row_max, "turn": normalise,
                              "wo": lambda it, lane, c: residual(it, "wo", lane, c, c),
                              "down": lambda it, lane, _: residual(it, "down", lane, FFN, FFN)}, head)


def count_residuals():
    place, n = {}, 0
    for steps in SLOTS:
        for _, kind, lane, arg in steps:
            if kind in ("wo", "down"):
                place[kind, lane, arg] = n
                n += 1
    return place


X_PLACE = count_residuals()

BLOCK = 512
BLOCKS = B * S // BLOCK
BT = BLOCK // P


def moe_part(nc, t, out, x_all, ident, minus_half):
    with ExitStack() as ctx:
        def sb(name, shape, dt=F32):
            return ctx.enter_context(nc.sbuf_tensor(name, shape, dt))

        def sem(name):
            return ctx.enter_context(nc.semaphore(name))

        xT = sb("moe_xT", [P, KC, B * S])
        rw = sb("rw", [P, KC, E])
        rb = sb("rb", [P, E])
        w1 = [sb(f"e_w1_{i}", [P, KC, FF]) for i in range(2)]
        w2 = [sb(f"e_w2_{i}", [P, FC, D]) for i in range(2)]
        b1 = sb("e_b1", [P, E, FC])
        b1_e = [sb(f"e_b1_{i}", [P, FC]) for i in range(2)]
        b2 = sb("e_b2", [E, D])
        gain = sb("ln3_gain", [P, D])
        shift = sb("ln3_shift", [P, D])
        logits = sb("logits", [P, ALL_TILES, E])
        top = sb("top", [P, ALL_TILES, 8])
        index = sb("index", [P, ALL_TILES, 8], U32)
        index_f = sb("index_f", [P, ALL_TILES, 2])
        iota_e = sb("iota_e", [P, E])
        gap = sb("gap", [P, ALL_TILES, E])
        total = sb("total", [P, ALL_TILES])
        share = sb("share", [P, ALL_TILES, 2])
        combine = sb("combine", [P, ALL_TILES, E])
        picked = sb("picked", [P, ALL_TILES, E])
        combine_T = sb("combine_T", [E, B * S])
        acc = x_all
        hidden = [sb(f"e_hidden{i}", [P, FC, BLOCK]) for i in range(2)]
        stats = sb("e_stats", [P, TILES, 6])
        mean_var = sb("e_mean_var", [P, TILES, 2])
        var_eps = sb("e_var_eps", [P, TILES])
        rstd = sb("e_rstd", [P, TILES])
        centred = sb("e_centred", [P, TILES, D])
        y = [sb(f"e_y{i}", [P, TILES, D]) for i in range(2)]
        up_bank = [ctx.enter_context(nc.psum_tensor(f"up{i}", [P, 512], F32)) for i in range(4)]
        down_bank = [ctx.enter_context(nc.psum_tensor(f"down{i}", [P, 512], F32)) for i in range(4)]

        small = sem("small_loaded")
        w_loaded = [sem(f"w_loaded{i}") for i in range(2)]
        w_used = [sem(f"w_used{i}") for i in range(2)]
        up_full = sem("up_full")
        up_free = [sem(f"up_free{i}") for i in range(4)]
        hidden_ready = sem("e_hidden_ready")
        b1_ready = sem("e_b1_ready")
        down_full = sem("down_full")
        down_free = [sem(f"down_free{i}") for i in range(4)]
        xT_full = sem("xT_full")
        xT_free = sem("xT_free")
        routed = sem("routed")
        exps = sem("exps")
        gaps = sem("gaps")
        combined = sem("combined")
        cT_full = sem("cT_full")
        cT_done = sem("cT_done")
        bias_full = sem("bias_full")
        bias_added = sem("bias_added")
        var_ready = sem("e_var_ready")
        rstd_ready = sem("e_rstd_ready")
        y_ready = sem("y_ready")
        iota_ready = sem("iota_ready")
        y_out = [sem(f"y_out{i}") for i in range(2)]

        block = ctx.enter_context(nc.Block())

        @block.sync
        def _(sp):
            sp.dma_start(rw[:], t["L1_xattn_router_w"].rearrange("(k p) n -> p k n", p=P)).then_inc(small, 16)
            sp.dma_start(rb[:], t["L1_xattn_router_b"].partition_broadcast(P)).then_inc(small, 16)
            sp.dma_start(b2[:], t["L1_xattn_e_b2"]).then_inc(small, 16)
            sp.dma_start(gain[:], t["L1_xattn_ln3_g"].partition_broadcast(P)).then_inc(small, 16)
            sp.dma_start(shift[:], t["L1_xattn_ln3_b"].partition_broadcast(P)).then_inc(small, 16)
            with nc.allow_non_contiguous_dma(reason="biases"):
                sp.dma_start(b1[:], t["L1_xattn_e_b1"].rearrange("e (f p) -> p e f", p=P)).then_inc(small, 16)
            with sp.Fori(0, E // 2) as j:
                for i in range(2):
                    e = j * 2 + i
                    sp.wait_ge(w_used[i], j + FREE_AT_FIRST)
                    sp.dma_start(w1[i][:], t["L1_xattn_e_w1"].rearrange("e (k p) n -> p e k n", p=P)[:, bass.ds(e, 1)].rearrange("p a k n -> p (a k) n")).then_inc(w_loaded[i], 16)
                    sp.dma_start(w2[i][:], t["L1_xattn_e_w2"].rearrange("e (k p) n -> p e k n", p=P)[:, bass.ds(e, 1)].rearrange("p a k n -> p (a k) n")).then_inc(w_loaded[i], 16)
            rows = out.rearrange("b (t p) d -> p (b t) d", p=P)
            with sp.Fori(0, B // 2) as j:
                for i in range(2):
                    sp.wait_ge(y_ready, j * 2 + i + 1)
                    sp.dma_start(rows[:, bass.ds((j * 2 + i) * TILES, TILES), :], y[i][:]).then_inc(y_out[i], 16)
            for i in range(2):
                sp.wait_ge(y_out[i], 16 * (B // 2 + 1))

        @block.gpsimd
        def _(pool):
            pool.iota(iota_e[:], pattern=[[1, E]], base=0, channel_multiplier=0, allow_small_or_imprecise_dtypes=True).then_inc(iota_ready, 1)
            with pool.Fori(0, B) as j:
                pool.wait_ge(var_ready, j + 1)
                pool.tensor_tensor(rstd[:], var_eps[:], minus_half[:], ALU.pow).then_inc(rstd_ready, 1)

        @block.tensor
        def _(pe):
            for free in (*w_used, *up_free, *down_free):
                pe.sem_inc(free, FREE_AT_FIRST)
            for g in range(KC * ALL_TILES // 4):
                k, t0 = g % KC, 4 * (g // KC)
                if g >= 4:
                    pe.wait_ge(xT_free, g - 3)
                for i in range(4):
                    last = pe.transpose(up_bank[g % 4][:, i * P:(i + 1) * P], x_all[:, t0 + i, k * P:(k + 1) * P], ident[:])
                last.then_inc(xT_full, 1)
            pe.wait_ge(small, 16 * 6)
            pe.wait_ge(xT_free, KC * ALL_TILES // 4)
            for i in range(ALL_TILES):
                for k in range(KC):
                    last = pe.matmul(down_bank[0][:, i * E:(i + 1) * E], xT[:, k, i * P:(i + 1) * P], rw[:, k, :], start=(k == 0), stop=(k == KC - 1))
            last.then_inc(routed, 1)
            pe.wait_ge(combined, 1)
            for g in range(ALL_TILES // 4):
                for i in range(4):
                    last = pe.transpose(up_bank[g][0:E, i * P:(i + 1) * P], combine[:, 4 * g + i, :], ident[:])
                last.then_inc(cT_full, 1)
            pe.wait_ge(cT_done, ALL_TILES // 4)
            for i in range(ALL_TILES // 2):
                if i >= 4:
                    pe.wait_ge(bias_added, i - 3)
                for m in range(2):
                    tile = 2 * i + m
                    last = pe.matmul(down_bank[i % 4][:, m * D:(m + 1) * D], combine_T[:, tile * P:(tile + 1) * P], b2[:], start=True, stop=True)
                last.then_inc(bias_full, 1)
            pe.wait_ge(bias_added, ALL_TILES // 2)

            with pe.Fori(0, E // 2) as j:
                for i in range(2):
                    pe.wait_ge(w_loaded[i], (j + 1) * 32)
                    for b in range(BLOCKS):
                        nb = (j * 2 + i) * BLOCKS + b
                        for f in range(FC):
                            pe.wait_ge(up_free[f % 4], nb * 2 + f // 4 + FREE_AT_FIRST)
                            for k in range(KC):
                                last = pe.matmul(up_bank[f % 4][:], w1[i][:, k, f * P:(f + 1) * P], xT[:, k, b * BLOCK:(b + 1) * BLOCK], start=(k == 0), stop=(k == KC - 1))
                            last.then_inc(up_full, 1)
                        for m in range(BT):
                            pe.wait_ge(down_free[m], nb + FREE_AT_FIRST)
                            for f in range(FC):
                                if m == 0:
                                    pe.wait_ge(hidden_ready, nb * FC + f + 1)
                                last = pe.matmul(down_bank[m][:, 0:D], hidden[b % 2][:, f, m * P:(m + 1) * P], w2[i][:, f, :], start=(f == 0), stop=(f == FC - 1))
                            last.then_inc(down_full, 1)
                    pe.drain()
                    pe.sem_inc(w_used[i], 1)

        @block.scalar
        def _(act):
            for g in range(KC * ALL_TILES // 4):
                k, t0 = g % KC, 4 * (g // KC)
                act.wait_ge(xT_full, g + 1)
                act.activation(xT[:, k, t0 * P:(t0 + 4) * P], up_bank[g % 4][:], ACT.Copy).then_inc(xT_free, 1)
            act.wait_ge(gaps, 1)
            act.activation(gap[:].rearrange("p t e -> p (t e)"), gap[:].rearrange("p t e -> p (t e)"), ACT.Exp).then_inc(exps, 1)
            act.wait_ge(gaps, 2)
            act.activation(share[:, :, 0], share[:, :, 0], ACT.Exp).then_inc(exps, 1)
            act.wait_ge(small, 16 * 6)
            for g in range(ALL_TILES // 4):
                act.wait_ge(cT_full, g + 1)
                act.activation(combine_T[:, g * 512:(g + 1) * 512], up_bank[g][0:E, :], ACT.Copy).then_inc(cT_done, 1)
            with act.Fori(0, E // 2) as j:
                for i in range(2):
                    act.wait_ge(b1_ready, j * 2 + i + 1)
                    for b in range(BLOCKS):
                        nb = (j * 2 + i) * BLOCKS + b
                        for f in range(FC):
                            act.wait_ge(up_full, nb * FC + f + 1)
                            act.activation(hidden[b % 2][:, f, :], up_bank[f % 4][:], ACT.Gelu, bias=b1_e[i][:, f:f + 1]).then_inc(hidden_ready, 1)
                            act.drain()
                            act.sem_inc(up_free[f % 4], 1)

        @block.vector
        def _(dve):
            dve.wait_ge(small, 16 * 6)
            dve.wait_ge(iota_ready, 1)
            dve.wait_ge(routed, 1)
            dve.tensor_tensor(logits[:], down_bank[0][:, 0:ALL_TILES * E].rearrange("p (t e) -> p t e", e=E), rb[:].unsqueeze(1).to_broadcast([P, ALL_TILES, E]), ALU.add)
            dve.drain()
            for i in range(ALL_TILES):
                dve.max(top[:, i, :], logits[:, i, :])
            dve.drain()
            for i in range(ALL_TILES):
                dve.max_index(index[:, i, :], top[:, i, :], logits[:, i, :])
            dve.tensor_tensor(gap[:], top[:], top[:, :, 0:1].to_broadcast([P, ALL_TILES, E]), ALU.subtract).then_inc(gaps, 1)
            dve.drain()
            dve.tensor_copy(index_f[:], index[:, :, 0:2])
            dve.wait_ge(exps, 1)
            dve.tensor_reduce(total[:], gap[:], AX_X, ALU.add)
            dve.drain()
            dve.reciprocal(total[:], total[:])
            dve.drain()
            dve.tensor_tensor(gap[:, :, 0:2], gap[:, :, 0:2], total[:].unsqueeze(2).to_broadcast([P, ALL_TILES, 2]), ALU.mult)
            dve.drain()
            dve.tensor_tensor(share[:, :, 0], gap[:, :, 1], gap[:, :, 0], ALU.subtract).then_inc(gaps, 1)
            dve.wait_ge(exps, 2)
            dve.tensor_scalar(share[:, :, 1], share[:, :, 0], 1.0, None, ALU.add)
            dve.drain()
            dve.reciprocal(total[:], share[:, :, 1])
            dve.drain()
            dve.tensor_tensor(share[:, :, 1], share[:, :, 0], total[:], ALU.mult)
            dve.drain()
            dve.tensor_copy(share[:, :, 0], total[:])
            dve.drain()
            lanes_e = iota_e[:].unsqueeze(1).to_broadcast([P, ALL_TILES, E])
            for i, dst in ((0, combine), (1, picked)):
                dve.tensor_tensor(dst[:], lanes_e, index_f[:, :, i:i + 1].to_broadcast([P, ALL_TILES, E]), ALU.is_equal)
                dve.drain()
                dve.tensor_tensor(dst[:], dst[:], share[:, :, i:i + 1].to_broadcast([P, ALL_TILES, E]), ALU.mult)
                dve.drain()
            dve.tensor_tensor(combine[:], combine[:], picked[:], ALU.add).then_inc(combined, 1)
            for i in range(ALL_TILES // 2):
                dve.wait_ge(bias_full, i + 1)
                dve.tensor_tensor(acc[:, 2 * i:2 * i + 2, :], acc[:, 2 * i:2 * i + 2, :], down_bank[i % 4][:].rearrange("p (t d) -> p t d", t=2), ALU.add).then_inc(bias_added, 1)
            dve.tensor_copy(b1_e[0][:], b1[:, 0, :]).then_inc(b1_ready, 1)
            dve.drain()
            with dve.Fori(0, E // 2) as j:
                for i in range(2):
                    for b in range(BLOCKS):
                        if b == 1:
                            dve.tensor_copy(b1_e[1 - i][:].unsqueeze(1), b1[:, bass.ds((j * 2 + i + 1) % E, 1), :]).then_inc(b1_ready, 1)
                        nb = (j * 2 + i) * BLOCKS + b
                        for m in range(BT):
                            tile = b * BT + m
                            dve.wait_ge(down_full, nb * BT + m + 1)
                            dve.scalar_tensor_tensor(out=acc[:, tile, :], in0=down_bank[m][:, 0:D], scalar=combine[:, tile, bass.ds(j * 2 + i, 1)], in1=acc[:, tile, :], op0=ALU.mult, op1=ALU.add).then_inc(down_free[m], 1)
            dve.drain()
            for i in range(2):
                dve.sem_inc(y_out[i], 16)
            with dve.Fori(0, B // 2) as j:
                for i in range(2):
                    at = (j * 2 + i) * TILES
                    for m in range(TILES):
                        dve.bn_stats(stats[:, m, :], acc[:, bass.ds(at + m, 1), :].rearrange("p a d -> p (a d)"))
                    dve.drain()
                    for m in range(TILES):
                        dve.bn_aggr(mean_var[:, m, :], stats[:, m, :])
                    dve.drain()
                    dve.tensor_scalar(var_eps[:], mean_var[:, :, 1], EPS, None, ALU.add).then_inc(var_ready, 1)
                    for m in range(TILES):
                        dve.scalar_tensor_tensor(out=centred[:, m, :], in0=acc[:, bass.ds(at + m, 1), :].rearrange("p a d -> p (a d)"), scalar=mean_var[:, m, 0:1], in1=gain[:], op0=ALU.subtract, op1=ALU.mult)
                    dve.drain()
                    dve.wait_ge(rstd_ready, j * 2 + i + 1)
                    dve.wait_ge(y_out[i], (j + 1) * 16)
                    for m in range(TILES):
                        last = dve.scalar_tensor_tensor(out=y[i][:, m, :], in0=centred[:, m, :], scalar=rstd[:, m:m + 1], in1=shift[:], op0=ALU.mult, op1=ALU.add)
                    last.then_inc(y_ready, 1)
                    dve.drain()


_OUT = ((B, S, D), "float32")


def kernel(**inputs):
    from concourse import bacc
    from concourse.bass_utils import run_bass_kernel_spmd

    nc = bacc.Bacc("TRN2", target_bir_lowering=False, num_devices=1)
    arrays, tensors = {}, {}
    for name, value in inputs.items():
        a = np.ascontiguousarray(value)
        arrays[f"in_{name}"] = a
        tensors[name] = nc.dram_tensor(f"in_{name}", a.shape, mybir.dt.from_np(a.dtype), kind="ExternalInput").ap()
    out = nc.dram_tensor("out_0", _OUT[0], F32, kind="ExternalOutput").ap()
    build(nc, tensors, out)
    r = run_bass_kernel_spmd(nc, [arrays], core_ids=[0])
    return r.results[0]["out_0"]
```

```python
from contextlib import ExitStack

import numpy as np

import concourse.bass as bass
from concourse import mybir

F32 = mybir.dt.float32
F32R = mybir.dt.float32r
BF16 = mybir.dt.bfloat16
U32 = mybir.dt.uint32
I32 = mybir.dt.int32
ALU = mybir.AluOpType
ACT = mybir.ActivationFunctionType
AX_X = mybir.AxisListType.X

P = 128
B, S, D = 8, 256, 256
H, DK = 16, 16
FF, E = 1024, 8
TILES = S // P
KC = D // P
FC = FF // P
HPC = H // KC
LANES = 4
TURNS = B // LANES
CALLS = 4
NCALL = CALLS * LANES
ALL_TILES = B * TILES
EPS = 1e-5
SCALE = DK ** -0.5
MASKED = -1e30
FFN, FINAL = "ffn", "final"
CAUSAL = (True, False, True, False)


def plan_slot(s):
    steps = []
    if 0 <= s - 3 < NCALL:
        c, lane = divmod(s - 3, LANES)
        steps += [(0, "turn", lane, c), (2, "out_T", lane, c), (4, "wo", lane, c)]
        if c == 1:
            steps += [(5, "ln", lane, FFN), (7, "T", lane, FFN)]
            steps += [(8 + j, "up", lane, j) for j in range(FC // 2)]
            steps += [(13, "down", lane, FFN)]
        elif c == CALLS - 1:
            steps += [(6, "ln", lane, FINAL), (9, "store", lane, FINAL)]
    if s < NCALL:
        c, lane = divmod(s, LANES)
        if c == 0:
            steps += [(0, "ctx", lane, 0)]
        if c != 2:
            steps += [(0, "ln", lane, c)]
        steps += [(1, "T", lane, c), (3, "q", lane, c), (4, "k", lane, c), (6, "v", lane, c)]
    if 0 <= s - 1 < NCALL:
        c, lane = divmod(s - 1, LANES)
        steps += [(h, "max", lane, (c, h)) for h in range(H)]
        steps += [(H, "shift", lane, c)]
    return sorted(steps, key=lambda step: step[0])


SLOTS = [plan_slot(s) for s in range(NCALL + 3)]


def count_steps():
    place, total = {}, {}
    for steps in SLOTS:
        for _, kind, lane, arg in steps:
            place[kind, lane, arg] = total.get(kind, 0)
            total[kind] = total.get(kind, 0) + 1
    return place, total


PLACE, TOTAL = count_steps()
WORK_BANKS = 2
FREE_AT_FIRST = 1
USES = {"ctx": 1, "T": 1, "q": 1, "k": 1, "v": 1, "shift": 1, "turn": 2, "out_T": 1, "wo": 1, "up": 1, "down": 1}


def count_work():
    uses, n = {}, 0
    for steps in SLOTS:
        for _, kind, lane, arg in steps:
            for j in range(USES.get(kind, 0)):
                uses[kind, lane, arg, j] = (n, n % WORK_BANKS, n // WORK_BANKS)
                n += 1
    return uses, n, [len(range(b, n, WORK_BANKS)) for b in range(WORK_BANKS)]


WORK, WORK_TOTAL, WORK_PER_BANK = count_work()


def build(nc, t, out):
    with ExitStack() as ctx:
        sb = lambda name, shape, dt=F32: ctx.enter_context(nc.sbuf_tensor(name, shape, dt))
        sem = lambda name: ctx.enter_context(nc.semaphore(name))
        x_rows = nc.dram_tensor("x_rows", [B, S, D], F32).ap()
        ident = sb("ident", [P, P])
        minus_half = sb("minus_half", [P, TILES])
        attention_part(nc, t, x_rows, ident, minus_half)
        moe_part(nc, t, out, x_rows, ident, minus_half)


def attention_part(nc, t, x_rows, ident, minus_half):
    with ExitStack() as ctx:
        def sb(name, shape, dt=F32):
            return ctx.enter_context(nc.sbuf_tensor(name, shape, dt))

        def ring(n, name, shape, dt=F32):
            return [sb(f"{name}{i}", shape, dt) for i in range(n)]

        def psum(name):
            return ctx.enter_context(nc.psum_tensor(name, [P, 512], F32))

        def sem(name):
            return ctx.enter_context(nc.semaphore(name))

        wq = [sb(f"wq{c}", [P, KC, D]) for c in range(CALLS)]
        wk = [sb(f"wk{c}", [P, KC, D]) for c in range(CALLS)]
        wv = [sb(f"wv{c}", [P, KC, D]) for c in range(CALLS)]
        wo = [sb(f"wo{c}", [P, KC, D]) for c in range(CALLS)]
        w1 = sb("w1", [P, KC, FF])
        w2 = sb("w2", [P, FC, D])
        bq = sb("bq", [P, CALLS, KC])
        bk = sb("bk", [P, CALLS, KC])
        b1 = sb("b1", [P, FC])
        bv = sb("bv", [P, CALLS, KC])
        bo = sb("bo", [P, CALLS, D])
        b2 = sb("b2", [P, D])
        pre = {0: "L0_xattn_ln1", 1: "L0_xattn_ln2", FFN: "L0_xattn_ln3"}
        pre_gain = {k: sb(f"pre_gain_{k}", [P, KC]) for k in pre}
        pre_shift = {k: sb(f"pre_shift_{k}", [P, KC]) for k in pre}
        post = {3: "L1_xattn_ln1", FINAL: "L1_xattn_ln2"}
        gain = {k: sb(f"gain_{k}", [P, D]) for k in post}
        shift = {k: sb(f"shift_{k}", [P, D]) for k in post}
        ident_b = sb("ident_b", [P, P], BF16)
        mask_qk = sb("mask_qk", [P, P], BF16)
        mask_kq = sb("mask_kq", [P, P], BF16)
        x = ring(LANES, "x", [P, TILES, D])
        cT = ring(LANES, "cT", [P, KC, S])
        q_stack = ring(3, "q_stack", [P, HPC, S], F32R)
        k_stack = ring(3, "k_stack", [P, HPC, S], F32R)
        v = ring(3, "v", [P, TILES, H, 2 * DK])
        ctx_in = ring(2, "ctx_in", [P, TILES, D])
        h = ring(2, "h", [P, TILES, D])
        hT = ring(2, "hT", [P, KC, S])
        u = ring(2, "u", [P, H // 4, S])
        q_hi, q_lo, k_hi, k_lo = (sb(n, [P, KC, S], F32R) for n in ("q_hi", "q_lo", "k_hi", "k_lo"))
        zeros = sb("zeros", [2, S])
        neg_max = sb("neg_max", [P, TILES, H])
        neg_max_T = sb("neg_max_T", [H, S], F32R)
        probs = ring(8, "probs", [P, TILES * S])
        inv_sum = sb("inv_sum", [P, TILES, H])
        o = sb("o", [P, TILES, D])
        oT = sb("oT", [P, KC, S])
        hidden = sb("hidden", [P, FC, S])
        stats = sb("stats", [P, TILES, 6])
        mean_var = sb("mean_var", [P, TILES, 2])
        var_eps = sb("var_eps", [P, TILES])
        rstd = sb("rstd", [P, TILES])
        centred = sb("centred", [P, TILES, D])
        raw_q = [hidden[:, 2 * c:2 * c + 2, :] for c in range(CALLS)]
        raw_k = [u[c // 2][:, 2 * (c % 2):2 * (c % 2) + 2, :] for c in range(CALLS)]
        work = [psum(f"work{i}") for i in range(WORK_BANKS)]
        s1 = [psum(f"s1_{i}") for i in range(2)]
        s2 = [psum(f"s2_{i}") for i in range(2)]
        pv = [psum(f"pv{i}") for i in range(2)]
        consts = sem("consts")
        loaded = [sem(f"loaded{c}") for c in range(CALLS)]
        loaded_ffn = sem("loaded_ffn")
        reordered = sem("reordered")
        loaded_rows = sem("loaded_rows")
        x_in = [sem(f"x_in{i}") for i in range(LANES)]
        ctx_loaded = [sem(f"ctx_loaded{i}") for i in range(2)]
        work_full = sem("work_full")
        work_free = [sem(f"work_free{i}") for i in range(WORK_BANKS)]
        var_ready = sem("var_ready")
        rstd_ready = sem("rstd_ready")
        h_ready = sem("h_ready")
        ctx_T_ready = sem("ctx_T_ready")
        hT_ready = sem("hT_ready")
        q_hi_ready = sem("q_hi_ready")
        k_hi_ready = sem("k_hi_ready")
        q_lo_ready = sem("q_lo_ready")
        k_lo_ready = sem("k_lo_ready")
        v_ready = sem("v_ready")
        stacked = sem("stacked")
        shift_T_ready = sem("shift_T_ready")
        shift_stacked = sem("shift_stacked")
        s1_full = sem("s1_full")
        s1_free = [sem(f"s1_free{i}") for i in range(2)]
        s2_full = sem("s2_full")
        probs_ready = sem("probs_ready")
        weighed = [sem(f"weighed{i}") for i in range(2)]
        u_ready = [sem(f"u_ready{i}") for i in range(2)]
        o_ready = sem("o_ready")
        oT_ready = sem("oT_ready")
        x_biased = sem("x_biased")
        x_ready = sem("x_ready")
        hidden_ready = sem("hidden_ready")
        stored = [sem(f"stored{i}") for i in range(LANES)]

        def nth(it, kind, lane, arg):
            return it * TOTAL[kind] + PLACE[kind, lane, arg] + 1

        def filled(it, kind, lane, arg, j=0):
            return it * WORK_TOTAL + WORK[kind, lane, arg, j][0] + 1

        def bank(kind, lane, arg, j=0):
            return work[WORK[kind, lane, arg, j][1]]

        def freed(kind, lane, arg, j=0):
            return work_free[WORK[kind, lane, arg, j][1]]

        def bank_uses(it, kind, lane, arg, j=0):
            _, b, k = WORK[kind, lane, arg, j]
            return it * WORK_PER_BANK[b] + k + FREE_AT_FIRST

        def call(it, n):
            return it * NCALL + n

        def run(engine, it, step, head):
            for s, steps in enumerate(SLOTS):
                n = s - 2
                for pos in range(H + 1):
                    if 0 <= n < NCALL and pos == H:
                        head(it, n, pos)
                    for at, kind, lane, arg in steps:
                        if at == pos and kind in step:
                            step[kind](it, lane, arg)
                    if 0 <= n < NCALL and pos < H:
                        head(it, n, pos)

        layers = ["L0_xattn_mmha_w{}", "L0_xattn_mha_w{}", "L1_xattn_sa_w{}", "L1_xattn_ca_w{}"]
        biases = ["L0_xattn_mmha_w{}_b", "L0_xattn_mha_w{}_b", "L1_xattn_sa_b{}", "L1_xattn_ca_b{}"]
        ROW_LOADS = 2 * CALLS + 1 + 2 * len(pre) + 2 * len(post)
        BIAS_LOADS = 2 * CALLS * KC + 1

        block = ctx.enter_context(nc.Block())

        @block.sync
        def _(sp):
            def rows_of(src, it, lane):
                return src.rearrange("b (t p) d -> p (b t) d", p=P)[:, bass.ds((it * LANES + lane) * TILES, TILES), :]

            def load_x(it, lane):
                sp.dma_start(x[lane][:], rows_of(t["x"], it, lane)).then_inc(x_in[lane], 16)

            def load_context(it, lane):
                sp.dma_start(ctx_in[lane % 2][:], rows_of(t["ctx_1024"], it, lane)).then_inc(ctx_loaded[lane % 2], 16)

            load_x(0, 0)
            load_context(0, 0)
            for c in range(CALLS):
                for w, key in ((raw_q, "q"), (raw_k, "k"), (wv, "v"), (wo, "o")):
                    sp.dma_start(w[c][:], t[layers[c].format(key)].rearrange("(k p) n -> p k n", p=P)).then_inc(loaded[c], 16)
                if c == 0:
                    load_x(0, 1)
                    load_context(0, 1)
                    for lane in range(2, LANES):
                        load_x(0, lane)
            for w, name in ((w1, "L0_xattn_ffn_w1"), (w2, "L0_xattn_ffn_w2")):
                sp.dma_start(w[:], t[name].rearrange("(k p) n -> p k n", p=P)).then_inc(loaded_ffn, 16)

            def stack_q(it, lane, c):
                buf = call(0, c * LANES + lane) % 3
                sp.wait_ge(q_hi_ready, nth(it, "q", lane, c))
                for half in range(KC):
                    for row in (0, 2 * DK):
                        at = half * 64 + row
                        sp.dma_start(q_stack[buf][at:at + DK].bitcast(F32), q_hi[:, half, :].bitcast(F32)).then_inc(stacked, 16)
                rows = q_stack[buf][3 * DK:3 * DK + 65:64].bitcast(F32)
                sp.dma_start(rows, zeros[:].unsqueeze(1).to_broadcast([2, HPC, S])).then_inc(stacked, 16)
                sp.wait_ge(q_lo_ready, nth(it, "q", lane, c))
                for half in range(KC):
                    at = half * 64 + DK
                    sp.dma_start(q_stack[buf][at:at + DK].bitcast(F32), q_lo[:, half, :].bitcast(F32)).then_inc(stacked, 16)

            def stack_k(it, lane, c):
                buf = call(0, c * LANES + lane) % 3
                sp.wait_ge(k_hi_ready, nth(it, "k", lane, c))
                for half in range(KC):
                    for row in (0, DK):
                        at = half * 64 + row
                        sp.dma_start(k_stack[buf][at:at + DK].bitcast(F32), k_hi[:, half, :].bitcast(F32)).then_inc(stacked, 16)
                sp.wait_ge(k_lo_ready, nth(it, "k", lane, c))
                for half in range(KC):
                    at = half * 64 + 2 * DK
                    sp.dma_start(k_stack[buf][at:at + DK].bitcast(F32), k_lo[:, half, :].bitcast(F32)).then_inc(stacked, 16)

            def stack_shift(it, lane, c):
                sp.wait_ge(shift_T_ready, nth(it, "shift", lane, c))
                buf = call(0, c * LANES + lane) % 3
                rows = q_stack[buf][3 * DK:3 * DK + 65:64].bitcast(F32)
                sp.dma_start(rows, neg_max_T[:].bitcast(F32)).then_inc(shift_stacked, 16)

            def next_context(it, lane, _):
                sp.wait_ge(ctx_T_ready, nth(it, "ctx", lane, 0))
                if lane < 2:
                    load_context(it, lane + 2)
                else:
                    load_context((it + 1) % TURNS, lane - 2)

            def store(it, lane, _):
                sp.wait_ge(h_ready, nth(it, "ln", lane, FINAL))
                sp.dma_start(rows_of(x_rows, it, lane), x[lane][:]).then_inc(stored[lane], 16)
                sp.wait_ge(stored[lane], 16 * (it + 1))
                load_x((it + 1) % TURNS, lane)

            with sp.Fori(0, TURNS) as it:
                run(sp, it, {"ctx": next_context, "q": stack_q, "k": stack_k, "shift": stack_shift, "store": store}, lambda it, n, pos: None)
            for lane in range(LANES):
                sp.wait_ge(x_in[lane], 16 * (TURNS + 1))
            for i in range(2):
                sp.wait_ge(ctx_loaded[i], 16 * (2 * TURNS + 1))

        @block.gpsimd
        def _(pool):
            pool.memset(ident[:], 0.0)
            pool.memset(minus_half[:], -0.5)
            pool.memset(mask_qk[:], 0.0)
            pool.memset(mask_kq[:], 0.0)
            pool.memset(ident_b[:], 0.0)
            pool.memset(zeros[:], 0.0)
            for buf in v:
                pool.memset(buf[:], 1.0)
            pool.drain()
            for m in (ident, ident_b):
                pool.affine_select(out=m[:], in_=m[:], compare_op=ALU.not_equal, fill=1.0, base=0, pattern=[[-1, P]], channel_multiplier=1)
            pool.affine_select(out=mask_qk[:], in_=mask_qk[:], compare_op=ALU.is_ge, fill=MASKED, base=0, pattern=[[-1, P]], channel_multiplier=1)
            pool.affine_select(out=mask_kq[:], in_=mask_kq[:], compare_op=ALU.is_ge, fill=MASKED, base=0, pattern=[[1, P]], channel_multiplier=-1)
            pool.drain()
            pool.sem_inc(consts, 1)
            for c in range(CALLS):
                for dst, key in ((bq, "q"), (bk, "k")):
                    for half in range(KC):
                        src = t[biases[c].format(key)].rearrange("(c i d) -> c d i", c=KC, d=DK)[half]
                        with nc.allow_non_contiguous_dma(reason="128 biases"):
                            pool.dma_start(dst[:, c, half:half + 1], src.rearrange("d (i a) -> d i a", a=1)).then_inc(loaded_rows, 16)
                with nc.allow_non_contiguous_dma(reason="256 biases"):
                    pool.dma_start(bv[:, c, :], t[biases[c].format("v")].rearrange("(k p) -> p k", p=P)).then_inc(loaded_rows, 16)
                pool.dma_start(bo[:, c, :], t[biases[c].format("o")].partition_broadcast(P)).then_inc(loaded_rows, 16)
            with nc.allow_non_contiguous_dma(reason="1024 biases"):
                pool.dma_start(b1[:], t["L0_xattn_ffn_b1"].rearrange("(f p) -> p f", p=P)).then_inc(loaded_rows, 16)
            pool.dma_start(b2[:], t["L0_xattn_ffn_b2"].partition_broadcast(P)).then_inc(loaded_rows, 16)
            for k, name in pre.items():
                with nc.allow_non_contiguous_dma(reason="256 gains"):
                    pool.dma_start(pre_gain[k][:], t[name + "_g"].rearrange("(k p) -> p k", p=P)).then_inc(loaded_rows, 16)
                    pool.dma_start(pre_shift[k][:], t[name + "_b"].rearrange("(k p) -> p k", p=P)).then_inc(loaded_rows, 16)
            for k, name in post.items():
                pool.dma_start(gain[k][:], t[name + "_g"].partition_broadcast(P)).then_inc(loaded_rows, 16)
                pool.dma_start(shift[k][:], t[name + "_b"].partition_broadcast(P)).then_inc(loaded_rows, 16)
            pool.wait_ge(loaded_rows, 16 * (ROW_LOADS + BIAS_LOADS))

            def inverse_root(it, lane, stage):
                pool.wait_ge(var_ready, nth(it, "ln", lane, stage))
                pool.tensor_tensor(rstd[:], var_eps[:], minus_half[:], ALU.pow).then_inc(rstd_ready, 1)

            def add_bias(it, lane, stage):
                pool.wait_ge(work_full, filled(it, "T", lane, stage))
                row = b2[:] if stage == FFN else bo[:, stage, :]
                pool.tensor_tensor(x[lane][:], x[lane][:], row.unsqueeze(1).to_broadcast([P, TILES, D]), ALU.add).then_inc(x_biased, 1)

            with pool.Fori(0, TURNS) as it:
                run(pool, it, {"ln": inverse_root, "T": add_bias}, lambda it, n, pos: None)

        @block.tensor
        def _(pe):
            for free in (*work_free, *s1_free, *u_ready, *weighed):
                pe.sem_inc(free, FREE_AT_FIRST)
            pe.wait_ge(consts, 1)

            def take(it, kind, lane, arg, j=0):
                pe.wait_ge(freed(kind, lane, arg, j), bank_uses(it, kind, lane, arg, j))
                return bank(kind, lane, arg, j)

            def transpose_rows(dst, src):
                for k in range(KC):
                    for i in range(TILES):
                        last = pe.transpose(dst[:, k * S + i * P:k * S + (i + 1) * P], src[:, i, k * P:(k + 1) * P], ident[:])
                return last

            def ctx_T(it, lane, _):
                pe.wait_ge(ctx_loaded[lane % 2], 16 * (it * 2 + lane // 2 + 1))
                transpose_rows(take(it, "ctx", lane, 0), ctx_in[lane % 2]).then_inc(work_full, 1)

            def rows_T(it, lane, stage):
                if stage == 2:
                    pe.wait_ge(x_ready, it * (TOTAL["wo"] + TOTAL["down"]) + X_PLACE["down", lane, FFN] + 1)
                    src = x[lane]
                else:
                    pe.wait_ge(h_ready, nth(it, "ln", lane, stage))
                    src = x[lane] if stage == 3 else h[lane % 2]
                transpose_rows(take(it, "T", lane, stage), src).then_inc(work_full, 1)

            def project(it, kind, lane, c, w, src):
                dst = take(it, kind, lane, c)
                for half in range(KC):
                    for k in range(KC):
                        last = pe.matmul(dst[:, half * S:(half + 1) * S], w[c][:, k, half * P:(half + 1) * P], src[:, k, :], start=(k == 0), stop=(k == KC - 1))
                last.then_inc(work_full, 1)

            def project_q(it, lane, c):
                pe.wait_ge(reordered, c + 1)
                pe.wait_ge(hT_ready, nth(it, "T", lane, c))
                project(it, "q", lane, c, wq, hT[lane % 2])

            def project_k(it, lane, c):
                if not CAUSAL[c]:
                    pe.wait_ge(ctx_T_ready, nth(it, "ctx", lane, 0))
                project(it, "k", lane, c, wk, hT[lane % 2] if CAUSAL[c] else cT[lane])

            def project_rows(it, kind, lane, arg, w, src, chunks):
                dst = take(it, kind, lane, arg)
                for i in range(TILES):
                    for k in range(chunks):
                        last = pe.matmul(dst[:, i * D:(i + 1) * D], src[:, k, i * P:(i + 1) * P], w[:, k, :], start=(k == 0), stop=(k == chunks - 1))
                last.then_inc(work_full, 1)

            def project_v(it, lane, c):
                project_rows(it, "v", lane, c, wv[c], hT[lane % 2] if CAUSAL[c] else cT[lane], KC)

            def scores_for_max(it, lane, arg):
                c, hd = arg
                n = c * LANES + lane
                if hd == 0:
                    pe.wait_ge(stacked, 16 * 13 * (call(it, n) + 1))
                pe.wait_ge(s1_free[hd % 2], call(it, n) * (H // 2) + hd // 2 + FREE_AT_FIRST)
                i, r = hd % HPC, 64 * (hd // HPC)
                dst = s1[hd % 2]
                for qt in range(TILES):
                    keys = (qt + 1) * P if CAUSAL[c] else S
                    last = pe.matmul(dst[:, qt * S:qt * S + keys], q_stack[n % 3][r:r + 4 * DK, i, qt * P:(qt + 1) * P],
                                     k_stack[n % 3][r:r + 4 * DK, i, 0:keys], start=True, stop=not CAUSAL[c])
                    if CAUSAL[c]:
                        last = pe.matmul(dst[:, qt * S + qt * P:qt * S + keys], ident_b[:], mask_qk[:], start=False, stop=True)
                last.then_inc(s1_full, 1)

            def shift_T(it, lane, c):
                n = c * LANES + lane
                for i in range(2):
                    pe.wait_ge(s1_free[i], (call(it, n) + 1) * (H // 2) + FREE_AT_FIRST)
                dst = take(it, "shift", lane, c)
                for qt in range(TILES):
                    last = pe.transpose(dst[0:H, qt * P:(qt + 1) * P], neg_max[:, qt, :], ident[:])
                last.then_inc(work_full, 1)

            def scores(it, n, hd):
                lane, c = n % LANES, n // LANES
                if hd == 0:
                    pe.wait_ge(shift_stacked, 16 * (call(it, n) + 1))
                if hd >= 2:
                    pe.wait_ge(probs_ready, call(it, n) * H + hd - 1)
                i, r = hd % HPC, 64 * (hd // HPC)
                dst = s2[hd % 2]
                for kt in range(TILES):
                    q0 = kt * P if CAUSAL[c] else 0
                    last = pe.matmul(dst[:, kt * S:kt * S + S - q0], k_stack[n % 3][r:r + 4 * DK, i, kt * P:(kt + 1) * P],
                                     q_stack[n % 3][r:r + 4 * DK, i, q0:S], start=True, stop=not CAUSAL[c])
                    if CAUSAL[c]:
                        last = pe.matmul(dst[:, kt * S:kt * S + P], ident_b[:], mask_kq[:], start=False, stop=True)
                last.then_inc(s2_full, 1)

            def weigh_values(it, n, g):
                lane, c = n % LANES, n // LANES
                dst, at = pv[g // 2], (g % 2) * S
                if g == 0:
                    pe.wait_ge(v_ready, nth(it, "v", lane, c))
                if g % 2 == 0:
                    pe.wait_ge(u_ready[g // 2], call(it, n) + FREE_AT_FIRST)
                pe.wait_ge(probs_ready, call(it, n) * H + 4 * g + 4)
                for kt in range(TILES):
                    q0 = kt * P if CAUSAL[c] else 0
                    for j in range(4):
                        hd = 4 * g + j
                        last = pe.matmul(dst[32 * j:32 * j + 32, at + q0:at + S], v[n % 3][:, kt, hd, :],
                                         probs[hd % 8][:, kt * S:kt * S + S - q0], start=(kt == 0), stop=(kt == TILES - 1))
                last.then_inc(weighed[g % 2], 1)

            def head(it, n, pos):
                if pos < H:
                    scores(it, n, pos)
                if pos in (5, 9, 13):
                    weigh_values(it, n, pos // 4 - 1)
                if pos == H:
                    weigh_values(it, n, 3)

            def turn(it, lane, c):
                n = c * LANES + lane
                for i in range(2):
                    pe.wait_ge(u_ready[i], call(it, n) + 1 + FREE_AT_FIRST)
                for qt in range(TILES):
                    dst = take(it, "turn", lane, c, qt)
                    for g in range(H // 4):
                        last = pe.transpose(dst[:, g * P:(g + 1) * P], u[n % 2][:, g, qt * P:(qt + 1) * P], ident[:])
                    last.then_inc(work_full, 1)

            def out_T(it, lane, c):
                pe.wait_ge(o_ready, nth(it, "turn", lane, c))
                transpose_rows(take(it, "out_T", lane, c), o).then_inc(work_full, 1)

            def out_project(it, lane, c):
                pe.wait_ge(oT_ready, nth(it, "out_T", lane, c))
                project_rows(it, "wo", lane, c, wo[c], oT, KC)

            def up(it, lane, j):
                if j == 0:
                    pe.wait_ge(loaded_ffn, 16 * 2)
                    pe.wait_ge(hT_ready, nth(it, "T", lane, FFN))
                dst = take(it, "up", lane, j)
                for m in range(2):
                    f = 2 * j + m
                    for k in range(KC):
                        last = pe.matmul(dst[:, m * S:(m + 1) * S], w1[:, k, f * P:(f + 1) * P], hT[lane % 2][:, k, :], start=(k == 0), stop=(k == KC - 1))
                last.then_inc(work_full, 1)

            def down(it, lane, _):
                pe.wait_ge(hidden_ready, nth(it, "up", lane, FC // 2 - 1))
                project_rows(it, "down", lane, FFN, w2, hidden, FC)

            with pe.Fori(0, TURNS) as it:
                run(pe, it, {"ctx": ctx_T, "T": rows_T, "q": project_q, "k": project_k, "v": project_v, "max": scores_for_max,
                             "shift": shift_T, "turn": turn, "out_T": out_T, "wo": out_project, "up": up, "down": down}, head)

        @block.scalar
        def _(act):
            act.wait_ge(loaded_rows, 16 * (ROW_LOADS + BIAS_LOADS))

            def ctx_T(it, lane, _):
                act.wait_ge(work_full, filled(it, "ctx", lane, 0))
                act.activation(cT[lane][:].rearrange("p k s -> p (k s)"), bank("ctx", lane, 0)[:], ACT.Copy).then_inc(freed("ctx", lane, 0), 1)
                act.drain()
                act.sem_inc(ctx_T_ready, 1)

            def rows_T(it, lane, stage):
                act.wait_ge(work_full, filled(it, "T", lane, stage))
                for k in range(KC):
                    dst, src = hT[lane % 2][:, k, :], bank("T", lane, stage)[:, k * S:(k + 1) * S]
                    if stage in pre:
                        last = act.activation(dst, src, ACT.Identity, bias=pre_shift[stage][:, k:k + 1], scale=pre_gain[stage][:, k:k + 1])
                    else:
                        last = act.activation(dst, src, ACT.Copy)
                last.then_inc(freed("T", lane, stage), 1)
                act.drain()
                act.sem_inc(hT_ready, 1)

            def hi_part(kind, dst, bias, ready):
                def step(it, lane, c):
                    act.wait_ge(work_full, filled(it, kind, lane, c))
                    for half in range(KC):
                        last = act.activation(dst[:, half, :], bank(kind, lane, c)[:, half * S:(half + 1) * S], ACT.Identity, bias=bias[:, c, half:half + 1])
                    last.then_inc(ready, 1)
                return step

            def shift_T(it, lane, c):
                act.wait_ge(work_full, filled(it, "shift", lane, c))
                act.activation(neg_max_T[:], bank("shift", lane, c)[0:H, 0:S], ACT.Copy).then_inc(shift_T_ready, 1)
                act.drain()
                act.sem_inc(freed("shift", lane, c), 1)

            def values(it, lane, c):
                act.wait_ge(work_full, filled(it, "v", lane, c))
                act.activation(v[(c * LANES + lane) % 3][:, :, :, 0:DK], bank("v", lane, c)[:].rearrange("p (t h d) -> p t h d", t=TILES, d=DK), ACT.Copy).then_inc(freed("v", lane, c), 1)
                act.drain()
                act.sem_inc(v_ready, 1)

            def out_T(it, lane, c):
                act.wait_ge(work_full, filled(it, "out_T", lane, c))
                for k in range(KC):
                    last = act.activation(oT[:, k, :], bank("out_T", lane, c)[:, k * S:(k + 1) * S], ACT.Identity, bias=bv[:, c, k:k + 1])
                last.then_inc(oT_ready, 1)
                act.drain()
                act.sem_inc(freed("out_T", lane, c), 1)

            def up(it, lane, j):
                act.wait_ge(work_full, filled(it, "up", lane, j))
                for m in range(2):
                    f = 2 * j + m
                    act.activation(hidden[:, f, :], bank("up", lane, j)[:, m * S:(m + 1) * S], ACT.Relu, bias=b1[:, f:f + 1])
                act.drain()
                act.sem_inc(freed("up", lane, j), 1)
                act.sem_inc(hidden_ready, 1)

            def head(it, n, pos):
                if pos == H:
                    return
                width = S + P if CAUSAL[n // LANES] else TILES * S
                act.wait_ge(s2_full, call(it, n) * H + pos + 1)
                if pos % 4 == 0:
                    act.wait_ge(weighed[pos // 4 % 2], call(it, n) * 2 + pos // 8 + FREE_AT_FIRST)
                act.activation(probs[pos % 8][:, 0:width], s2[pos % 2][:, 0:width], ACT.Exp, scale=SCALE).then_inc(probs_ready, 1)

            with act.Fori(0, TURNS) as it:
                run(act, it, {"ctx": ctx_T, "v": values, "T": rows_T, "q": hi_part("q", q_hi, bq, q_hi_ready), "k": hi_part("k", k_hi, bk, k_hi_ready),
                              "shift": shift_T, "out_T": out_T, "up": up}, head)

        @block.vector
        def _(dve):
            for i in range(3):
                for r in (32, 96):
                    dve.memset(k_stack[i][r:r + 32].bitcast(F32), 1.0)
                    dve.memset(q_stack[i][r:r + 32].bitcast(F32), 0.0)
            dve.drain()
            for c in range(CALLS):
                dve.wait_ge(loaded[c], 16 * 4)
                for w, raw in ((wq, raw_q), (wk, raw_k)):
                    for k in range(KC):
                        for half in range(KC):
                            last = dve.tensor_copy(w[c][:, k, half * P:(half + 1) * P].rearrange("p (d i) -> p d i", d=DK),
                                                   raw[c][:, k, half * P:(half + 1) * P].rearrange("p (i d) -> p d i", d=DK))
                last.then_inc(reordered, 1)
            dve.drain()
            dve.wait_ge(loaded_rows, 16 * (ROW_LOADS + BIAS_LOADS))
            dve.wait_ge(consts, 1)

            def norm(it, lane, stage):
                if stage == 0:
                    dve.wait_ge(x_in[lane], 16 * (it + 1))
                src = x[lane]
                for i in range(TILES):
                    dve.bn_stats(stats[:, i, :], src[:, i, :])
                dve.drain()
                for i in range(TILES):
                    dve.bn_aggr(mean_var[:, i, :], stats[:, i, :])
                dve.drain()
                dve.tensor_scalar(var_eps[:], mean_var[:, :, 1], EPS, None, ALU.add).then_inc(var_ready, 1)
                if stage in post:
                    for i in range(TILES):
                        dve.scalar_tensor_tensor(out=centred[:, i, :], in0=src[:, i, :], scalar=mean_var[:, i, 0:1], in1=gain[stage][:], op0=ALU.subtract, op1=ALU.mult)
                    dve.drain()
                dve.wait_ge(rstd_ready, nth(it, "ln", lane, stage))
                for i in range(TILES):
                    if stage in post:
                        last = dve.scalar_tensor_tensor(out=src[:, i, :], in0=centred[:, i, :], scalar=rstd[:, i:i + 1], in1=shift[stage][:], op0=ALU.mult, op1=ALU.add)
                    else:
                        last = dve.tensor_scalar(h[lane % 2][:, i, :], src[:, i, :], mean_var[:, i, 0:1], rstd[:, i:i + 1], ALU.subtract, ALU.mult)
                last.then_inc(h_ready, 1)
                dve.drain()

            def lo_part(kind, hi, dst, bias, hi_ready, ready):
                def step(it, lane, c):
                    dve.wait_ge(hi_ready, nth(it, kind, lane, c))
                    for half in range(KC):
                        dve.scalar_tensor_tensor(out=dst[:, half, :], in0=bank(kind, lane, c)[:, half * S:(half + 1) * S], scalar=bias[:, c, half:half + 1],
                                                 in1=hi[:, half, :].bitcast(F32), op0=ALU.add, op1=ALU.subtract)
                    dve.drain()
                    dve.sem_inc(ready, 1)
                    dve.sem_inc(freed(kind, lane, c), 1)
                return step

            def row_max(it, lane, arg):
                c, hd = arg
                n = c * LANES + lane
                dve.wait_ge(s1_full, call(it, n) * H + hd + 1)
                src = s1[hd % 2]
                if CAUSAL[c]:
                    dve.tensor_reduce(neg_max[:, 0, hd:hd + 1], src[:, 0:P], AX_X, ALU.max, negate=True)
                    last = dve.tensor_reduce(neg_max[:, 1, hd:hd + 1], src[:, S:2 * S], AX_X, ALU.max, negate=True)
                else:
                    last = dve.tensor_reduce(neg_max[:, :, hd], src[:].rearrange("p (t s) -> p t s", t=TILES), AX_X, ALU.max, negate=True)
                last.then_inc(s1_free[hd % 2], 1)

            def copy_out(it, n, i):
                dve.wait_ge(weighed[1], call(it, n) * 2 + i + 1 + FREE_AT_FIRST)
                dve.tensor_copy(u[n % 2][:, 2 * i:2 * i + 2, :].rearrange("p g s -> p (g s)"), pv[i][:]).then_inc(u_ready[i], 1)

            def head(it, n, pos):
                if pos == 11:
                    copy_out(it, n, 0)
                if pos == H:
                    copy_out(it, n, 1)

            def normalise(it, lane, c):
                for qt in range(TILES):
                    dve.wait_ge(work_full, filled(it, "turn", lane, c, qt))
                    src = bank("turn", lane, c, qt)[:].rearrange("p (h e) -> p h e", e=2 * DK)
                    dve.reciprocal(inv_sum[:, qt, :], src[:, :, DK])
                    dve.drain()
                    dve.tensor_tensor(o[:, qt, :].rearrange("p (h d) -> p h d", d=DK), src[:, :, 0:DK],
                                      inv_sum[:, qt, :].unsqueeze(2).to_broadcast([P, H, DK]), ALU.mult).then_inc(freed("turn", lane, c, qt), 1)
                dve.drain()
                dve.sem_inc(o_ready, 1)

            def residual(it, kind, lane, arg, stage):
                dve.wait_ge(work_full, filled(it, kind, lane, arg))
                dve.wait_ge(x_biased, nth(it, "T", lane, stage))
                dve.tensor_tensor(x[lane][:], x[lane][:], bank(kind, lane, arg)[:].rearrange("p (t d) -> p t d", t=TILES), ALU.add).then_inc(x_ready, 1)
                dve.drain()
                dve.sem_inc(freed(kind, lane, arg), 1)

            with dve.Fori(0, TURNS) as it:
                run(dve, it, {"ln": norm, "q": lo_part("q", q_hi, q_lo, bq, q_hi_ready, q_lo_ready), "k": lo_part("k", k_hi, k_lo, bk, k_hi_ready, k_lo_ready),
                              "max": row_max, "turn": normalise,
                              "wo": lambda it, lane, c: residual(it, "wo", lane, c, c),
                              "down": lambda it, lane, _: residual(it, "down", lane, FFN, FFN)}, head)


def count_residuals():
    place, n = {}, 0
    for steps in SLOTS:
        for _, kind, lane, arg in steps:
            if kind in ("wo", "down"):
                place[kind, lane, arg] = n
                n += 1
    return place


X_PLACE = count_residuals()

GROUP = 256
GT = GROUP // P
TOP = 2
SLOT_TILES = (TOP * B * S + E * (GROUP - 1)) // GROUP
assert SLOT_TILES % 2 == 1
PAIRS = SLOT_TILES // 2
PLACES = SLOT_TILES + 1
WRITTEN_AT_FIRST = 16


def moe_part(nc, t, out, x_rows, ident, minus_half):
    with ExitStack() as ctx:
        def sb(name, shape, dt=F32):
            return ctx.enter_context(nc.sbuf_tensor(name, shape, dt))

        def sem(name):
            return ctx.enter_context(nc.semaphore(name))

        x_all = sb("x_all", [P, ALL_TILES, D])
        rw = sb("rw", [P, KC, E])
        rb = sb("rb", [P, E])
        b1 = sb("e_b1", [P, E, FC])
        b2 = sb("e_b2", [E, D])
        gain = sb("ln3_gain", [P, D])
        shift = sb("ln3_shift", [P, D])
        xT = sb("moe_xT", [P, KC, B * S])
        logits = sb("logits", [P, ALL_TILES, E])
        top = sb("top", [P, ALL_TILES, 8])
        index = sb("index", [P, ALL_TILES, 8], U32)
        index_f = sb("index_f", [P, ALL_TILES, TOP])
        iota_e = sb("iota_e", [P, E])
        iota_s = sb("iota_s", [P, PLACES])
        before = sb("before", [P, P], BF16)
        ones = sb("ones", [P, P], BF16)
        gap = sb("gap", [P, ALL_TILES, E])
        total = sb("total", [P, ALL_TILES])
        ratio = sb("ratio", [P, ALL_TILES])
        share = sb("share", [P, ALL_TILES, TOP])
        chosen = [sb(f"chosen{i}", [P, ALL_TILES, E]) for i in range(TOP)]
        weighed = [sb(f"weighed{i}", [P, ALL_TILES, E]) for i in range(TOP)]
        combine = sb("combine", [P, ALL_TILES, E])
        combine_T = sb("combine_T", [E, B * S])
        both = sb("both", [P, ALL_TILES * E], BF16)
        counts = [sb(f"counts{i}", [P, ALL_TILES, E]) for i in range(2)]
        slot = sb("slot", [P, ALL_TILES, E])
        tiles_i = sb("tiles_i", [P, E], I32)
        tiles_f = sb("tiles_f", [P, E])
        ends = [sb(f"ends{i}", [P, E]) for i in range(2)]
        starts = sb("starts", [P, E])
        past = sb("past", [P, PLACES, E])
        tile_expert_f = sb("tile_expert_f", [P, PLACES])
        tile_expert = sb("tile_expert", [P, PLACES], I32)
        slot_f = sb("slot_f", [P, TOP, ALL_TILES])
        slot_of = sb("slot_of", [P, TOP, ALL_TILES], U32)
        def two(name, shape, dt=F32):
            return [sb(f"{name}{i}", shape, dt) for i in range(2)]

        w1 = two("e_w1_", [P, KC, FF])
        w2 = two("e_w2_", [P, FC, D])
        b1_e = two("e_b1_", [P, FC])
        rows = two("rows", [P, GT, D])
        rows_T = two("rows_T", [P, KC, GROUP])
        hidden = two("e_hidden", [P, FC, GROUP])
        result = two("result", [P, GT, D])
        acc = sb("acc", [P, ALL_TILES, D])
        got = [sb(f"got{i}", [P, ALL_TILES, D]) for i in range(TOP)]
        stats = sb("e_stats", [P, TILES, 6])
        mean_var = sb("e_mean_var", [P, TILES, 2])
        var_eps = sb("e_var_eps", [P, TILES])
        rstd = sb("e_rstd", [P, TILES])
        centred = sb("centred_e", [P, TILES, D])
        y = two("e_y", [P, TILES, D])
        bank = [ctx.enter_context(nc.psum_tensor(f"moe{i}", [P, 512], F32)) for i in range(8)]
        up_bank, down_bank, turn_bank = bank[0:4], bank[4:6], bank[6:8]
        slots_x = nc.dram_tensor("slots_x", [PLACES * GROUP, D], F32).ap()
        slots_y = nc.dram_tensor("slots_y", [SLOT_TILES * GROUP, D], F32).ap()
        x_tiles = slots_x.rearrange("(s g p) d -> p (s g) d", p=P, g=GT)
        y_tiles = slots_y.rearrange("(s g p) d -> p (s g) d", p=P, g=GT)

        x_loaded = [sem(f"x_loaded{g}") for g in range(ALL_TILES // 4)]
        small = sem("small_loaded")
        made = sem("made")
        zero_made = sem("zero_made")
        zeroed = sem("zeroed")
        xT_full, xT_free = sem("xT_full"), sem("xT_free")
        routed = sem("routed")
        gaps, exps = sem("gaps"), sem("exps")
        both_ready = sem("both_ready")
        ranked = sem("ranked")
        slots_ready = sem("slots_ready")
        scattered = sem("scattered")
        combined = sem("combined")
        cT_full, cT_done = sem("cT_full"), sem("cT_done")
        bias_full, bias_added = sem("bias_full"), sem("bias_added")
        w1_loaded = [sem(f"w1_loaded{i}") for i in range(2)]
        w2_loaded = [sem(f"w2_loaded{i}") for i in range(2)]
        rows_loaded = [sem(f"rows_loaded{i}") for i in range(2)]
        rows_T_full = sem("rows_T_full")
        rows_T_ready = sem("rows_T_ready")
        up_full = sem("up_full")
        hidden_ready = sem("e_hidden_ready")
        b1_ready = sem("e_b1_ready")
        down_full = sem("down_full")
        result_ready = sem("result_ready")
        written = [sem(f"written{i}") for i in range(2)]
        gathered = [sem(f"gathered{b}") for b in range(B)]
        var_ready, rstd_ready = sem("e_var_ready"), sem("e_rstd_ready")
        y_ready = sem("y_ready")
        y_out = [sem(f"y_out{i}") for i in range(2)]

        ZERO_LOADS = PLACES * GT // ALL_TILES
        assert ZERO_LOADS * ALL_TILES == PLACES * GT
        block = ctx.enter_context(nc.Block())

        @block.sync
        def _(sp):
            for g in range(ALL_TILES // 4):
                sp.dma_start(x_all[:, 4 * g:4 * g + 4, :], x_rows.rearrange("b (t p) d -> p (b t) d", p=P)[:, 4 * g:4 * g + 4, :]).then_inc(x_loaded[g], 16)
            sp.dma_start(rw[:], t["L1_xattn_router_w"].rearrange("(k p) n -> p k n", p=P)).then_inc(small, 16)
            sp.dma_start(rb[:], t["L1_xattn_router_b"].partition_broadcast(P)).then_inc(small, 16)
            sp.dma_start(b2[:], t["L1_xattn_e_b2"]).then_inc(small, 16)
            sp.dma_start(gain[:], t["L1_xattn_ln3_g"].partition_broadcast(P)).then_inc(small, 16)
            sp.dma_start(shift[:], t["L1_xattn_ln3_b"].partition_broadcast(P)).then_inc(small, 16)
            with nc.allow_non_contiguous_dma(reason="biases"):
                sp.dma_start(b1[:], t["L1_xattn_e_b1"].rearrange("e (f p) -> p e f", p=P)).then_inc(small, 16)
            sp.wait_ge(zero_made, 1)
            flat = slots_x.rearrange("(p r) d -> p r d", p=P)
            for r in range(ZERO_LOADS):
                sp.dma_start(flat[:, r * ALL_TILES:(r + 1) * ALL_TILES, :], got[0][:]).then_inc(zeroed, 16)

            w1_rows = t["L1_xattn_e_w1"].rearrange("e (k p) n -> p (e k) n", p=P)
            w2_rows = t["L1_xattn_e_w2"].rearrange("e (k p) n -> p (e k) n", p=P)

            def expert(s):
                return sp.value_load(tile_expert[0:1, bass.ds(s, 1)], min_val=0, max_val=E - 1)

            def fetch_first(i, e):
                sp.dma_start(w1[i][:], w1_rows[:, bass.ds(e * KC, KC), :]).then_inc(w1_loaded[i], 16)

            def fetch_second(i, e):
                sp.dma_start(w2[i][:], w2_rows[:, bass.ds(e * FC, FC), :]).then_inc(w2_loaded[i], 16)

            def fetch_rows(s, i):
                sp.dma_start(rows[i][:], x_tiles[:, bass.ds(s * GT, GT), :]).then_inc(rows_loaded[i], 16)

            def write(s, i):
                sp.wait_ge(result_ready, s + 1)
                sp.dma_start(y_tiles[:, bass.ds(s * GT, GT), :], result[i][:]).then_inc(written[i], 16)

            sp.wait_ge(slots_ready, 1)
            for s in range(2):
                e = expert(s)
                fetch_first(s, e)
                fetch_second(s, e)
            sp.wait_ge(scattered, 16 * TOP * ALL_TILES)
            for s in range(2):
                fetch_rows(s, s)
            with sp.Fori(0, PAIRS) as j:
                for i in range(2):
                    s = j * 2 + i
                    e = expert(s + 2)
                    sp.wait_ge(up_full, (s + 1) * (FC // 2))
                    fetch_first(i, e)
                    sp.wait_ge(rows_T_full, s + 1)
                    fetch_rows(s + 2, i)
                    sp.wait_ge(down_full, s + 1)
                    write(s, i)
                    fetch_second(i, e)
            write(SLOT_TILES - 1, 0)
            for i in range(2):
                sp.wait_ge(w1_loaded[i], 16 * (PAIRS + 1))
                sp.wait_ge(w2_loaded[i], 16 * (PAIRS + 1))
                sp.wait_ge(rows_loaded[i], 16 * (PAIRS + 1))
            out_rows = out.rearrange("b (t p) d -> p (b t) d", p=P)
            for b in range(B):
                sp.wait_ge(y_ready, b + 1)
                sp.dma_start(out_rows[:, b * TILES:(b + 1) * TILES, :], y[b % 2][:]).then_inc(y_out[b % 2], 16)
            for i in range(2):
                sp.wait_ge(y_out[i], 16 * (B // 2))

        @block.gpsimd
        def _(pool):
            pool.iota(iota_e[:], pattern=[[1, E]], base=0, channel_multiplier=0, allow_small_or_imprecise_dtypes=True)
            pool.iota(iota_s[:], pattern=[[1, PLACES]], base=0, channel_multiplier=0, allow_small_or_imprecise_dtypes=True)
            pool.memset(ones[:], 1.0)
            pool.drain()
            pool.affine_select(out=before[:], in_=ones[:], compare_op=ALU.is_gt, fill=0.0, base=0, pattern=[[1, P]], channel_multiplier=-1)
            pool.drain()
            pool.sem_inc(made, 1)
            pool.wait_ge(zeroed, 16 * ZERO_LOADS)
            pool.wait_ge(slots_ready, 1)
            for i in range(ALL_TILES):
                for j in range(TOP):
                    pool.indirect_dma_start(slots_x, bass.IndirectOffsetOnAxis(ap=slot_of[:, j, i:i + 1], axis=0), x_all[:, i, :], None).then_inc(scattered, 16)
            for i in range(2):
                pool.wait_ge(written[i], 16 * (PAIRS + 1 - i) + WRITTEN_AT_FIRST)

            def inverse_root(b):
                pool.wait_ge(var_ready, b + 1)
                pool.tensor_tensor(rstd[:], var_eps[:], minus_half[:], ALU.pow).then_inc(rstd_ready, 1)

            for b in range(B):
                for i in range(b * TILES, (b + 1) * TILES):
                    for j in range(TOP):
                        pool.indirect_dma_start(got[j][:, i, :], None, slots_y, bass.IndirectOffsetOnAxis(ap=slot_of[:, j, i:i + 1], axis=0)).then_inc(gathered[b], 16)
                if b >= 2:
                    inverse_root(b - 2)
            for b in range(B - 2, B):
                inverse_root(b)

        @block.tensor
        def _(pe):
            for g in range(KC * ALL_TILES // 4):
                k, t0 = g % KC, 4 * (g // KC)
                pe.wait_ge(x_loaded[g // KC], 16)
                if g >= 4:
                    pe.wait_ge(xT_free, g - 3)
                for i in range(4):
                    last = pe.transpose(up_bank[g % 4][:, i * P:(i + 1) * P], x_all[:, t0 + i, k * P:(k + 1) * P], ident[:])
                last.then_inc(xT_full, 1)
            pe.wait_ge(small, 16 * 6)
            pe.wait_ge(xT_free, KC * ALL_TILES // 4)
            for i in range(ALL_TILES):
                for k in range(KC):
                    last = pe.matmul(down_bank[0][:, i * E:(i + 1) * E], xT[:, k, i * P:(i + 1) * P], rw[:, k, :], start=(k == 0), stop=(k == KC - 1))
            last.then_inc(routed, 1)
            pe.wait_ge(both_ready, 1)
            pe.matmul(down_bank[0][:, 0:ALL_TILES * E], before[:], both[:], start=True, stop=True)
            pe.matmul(down_bank[1][:, 0:ALL_TILES * E], ones[:], both[:], start=True, stop=True).then_inc(ranked, 1)
            pe.wait_ge(combined, 1)
            for g in range(ALL_TILES // 4):
                for i in range(4):
                    last = pe.transpose(up_bank[g][0:E, i * P:(i + 1) * P], combine[:, 4 * g + i, :], ident[:])
                last.then_inc(cT_full, 1)
            pe.wait_ge(cT_done, ALL_TILES // 4)
            for i in range(ALL_TILES // 2):
                if i >= 2:
                    pe.wait_ge(bias_added, i - 1)
                for m in range(2):
                    tile = 2 * i + m
                    last = pe.matmul(turn_bank[i % 2][:, m * D:(m + 1) * D], combine_T[:, tile * P:(tile + 1) * P], b2[:], start=True, stop=True)
                last.then_inc(bias_full, 1)
            pe.wait_ge(bias_added, ALL_TILES // 2)

            def turn(s, i, n):
                pe.wait_ge(rows_loaded[i], 16 * n)
                for k in range(KC):
                    for m in range(GT):
                        last = pe.transpose(turn_bank[i][:, k * GROUP + m * P:k * GROUP + (m + 1) * P], rows[i][:, m, k * P:(k + 1) * P], ident[:])
                last.then_inc(rows_T_full, 1)

            def up(s, i, n):
                pe.wait_ge(w1_loaded[i], 16 * n)
                pe.wait_ge(rows_T_ready, s + 1)
                for q in range(FC // 2):
                    if not isinstance(s, int):
                        pe.wait_ge(hidden_ready, (s - 1) * (FC // 2) + q + 1)
                    for m in range(2):
                        f = 2 * q + m
                        for k in range(KC):
                            last = pe.matmul(up_bank[q][:, m * GROUP:(m + 1) * GROUP], w1[i][:, k, f * P:(f + 1) * P], rows_T[i][:, k, :], start=(k == 0), stop=(k == KC - 1))
                    last.then_inc(up_full, 1)

            def down(s, i, n):
                pe.wait_ge(w2_loaded[i], 16 * n)
                for m in range(GT):
                    for f in range(FC):
                        if m == 0 and f % 2 == 0:
                            pe.wait_ge(hidden_ready, s * (FC // 2) + f // 2 + 1)
                        last = pe.matmul(down_bank[i][:, m * D:(m + 1) * D], hidden[i][:, f, m * P:(m + 1) * P], w2[i][:, f, :], start=(f == 0), stop=(f == FC - 1))
                last.then_inc(down_full, 1)

            turn(0, 0, 1)
            up(0, 0, 1)
            with pe.Fori(0, PAIRS) as j:
                turn(j * 2 + 1, 1, j + 1)
                up(j * 2 + 1, 1, j + 1)
                down(j * 2, 0, j + 1)
                turn(j * 2 + 2, 0, j + 2)
                up(j * 2 + 2, 0, j + 2)
                down(j * 2 + 1, 1, j + 1)
            down(SLOT_TILES - 1, 0, PAIRS + 1)

        @block.scalar
        def _(act):
            for g in range(KC * ALL_TILES // 4):
                k, t0 = g % KC, 4 * (g // KC)
                act.wait_ge(xT_full, g + 1)
                act.activation(xT[:, k, t0 * P:(t0 + 4) * P], up_bank[g % 4][:], ACT.Copy).then_inc(xT_free, 1)
            act.wait_ge(gaps, 1)
            act.activation(gap[:].rearrange("p t e -> p (t e)"), gap[:].rearrange("p t e -> p (t e)"), ACT.Exp).then_inc(exps, 1)
            act.wait_ge(gaps, 2)
            act.activation(ratio[:], ratio[:], ACT.Exp).then_inc(exps, 1)
            for g in range(ALL_TILES // 4):
                act.wait_ge(cT_full, g + 1)
                act.activation(combine_T[:, g * 512:(g + 1) * 512], up_bank[g][0:E, :], ACT.Copy).then_inc(cT_done, 1)

            def turn(s, i):
                act.wait_ge(rows_T_full, s + 1)
                act.activation(rows_T[i][:].rearrange("p k g -> p (k g)"), turn_bank[i][:], ACT.Copy).then_inc(rows_T_ready, 1)

            def gelu(s, i):
                act.wait_ge(b1_ready, s + 1)
                for q in range(FC // 2):
                    act.wait_ge(up_full, s * (FC // 2) + q + 1)
                    for m in range(2):
                        f = 2 * q + m
                        last = act.activation(hidden[i][:, f, :], up_bank[q][:, m * GROUP:(m + 1) * GROUP], ACT.Gelu, bias=b1_e[i][:, f:f + 1])
                    last.then_inc(hidden_ready, 1)

            turn(0, 0)
            gelu(0, 0)
            with act.Fori(0, PAIRS) as j:
                for i in (1, 0):
                    turn(j * 2 + 2 - i, i)
                    gelu(j * 2 + 2 - i, i)

        @block.vector
        def _(dve):
            dve.memset(got[0][:], 0.0).then_inc(zero_made, 1)
            dve.wait_ge(small, 16 * 6)
            dve.wait_ge(made, 1)
            dve.wait_ge(routed, 1)
            wide = [P, ALL_TILES, E]

            def then(_):
                dve.drain()

            then(dve.tensor_tensor(logits[:], down_bank[0][:, 0:ALL_TILES * E].rearrange("p (t e) -> p t e", e=E), rb[:].unsqueeze(1).to_broadcast(wide), ALU.add))
            for i in range(ALL_TILES):
                last = dve.max(top[:, i, :], logits[:, i, :])
            then(last)
            dve.tensor_tensor(gap[:], top[:], top[:, :, 0:1].to_broadcast(wide), ALU.subtract).then_inc(gaps, 1)
            for i in range(ALL_TILES):
                last = dve.max_index(index[:, i, :], top[:, i, :], logits[:, i, :])
            then(last)
            then(dve.tensor_copy(index_f[:], index[:, :, 0:TOP]))
            experts = iota_e[:].unsqueeze(1).to_broadcast(wide)
            for i in range(TOP):
                last = dve.tensor_tensor(chosen[i][:], experts, index_f[:, :, i:i + 1].to_broadcast(wide), ALU.is_equal)
            then(last)
            dve.tensor_tensor(both[:].rearrange("p (t e) -> p t e", e=E), chosen[0][:], chosen[1][:], ALU.add).then_inc(both_ready, 1)

            dve.wait_ge(ranked, 1)
            in_tile = down_bank[0][:, 0:ALL_TILES * E].rearrange("p (t e) -> p t e", e=E)
            tile_count = down_bank[1][:, 0:ALL_TILES * E].rearrange("p (t e) -> p t e", e=E)
            then(dve.tensor_copy(counts[0][:], tile_count))
            now = 0
            for step in (1, 2, 4, 8):
                dve.tensor_copy(counts[1 - now][:, 0:step, :], counts[now][:, 0:step, :])
                then(dve.tensor_tensor(counts[1 - now][:, step:, :], counts[now][:, step:, :], counts[now][:, :-step, :], ALU.add))
                now = 1 - now
            running = counts[now]
            then(dve.tensor_scalar(tiles_i[:], running[:, ALL_TILES - 1, :], float(GROUP - 1), None, ALU.add))
            then(dve.tensor_scalar(tiles_i[:], tiles_i[:], GROUP.bit_length() - 1, None, ALU.logical_shift_right))
            dve.tensor_copy(tiles_f[:], tiles_i[:])
            then(dve.tensor_copy(ends[0][:], tiles_i[:]))
            at = 0
            for step in (1, 2, 4):
                dve.tensor_copy(ends[1 - at][:, 0:step], ends[at][:, 0:step])
                then(dve.tensor_tensor(ends[1 - at][:, step:], ends[at][:, step:], ends[at][:, :-step], ALU.add))
                at = 1 - at
            end = ends[at]
            dve.tensor_tensor(past[:], end[:].unsqueeze(1).to_broadcast([P, PLACES, E]), iota_s[:].unsqueeze(2).to_broadcast([P, PLACES, E]), ALU.is_le)
            then(dve.tensor_tensor(starts[:], end[:], tiles_f[:], ALU.subtract))
            dve.tensor_scalar(starts[:], starts[:], float(GROUP), None, ALU.mult)
            then(dve.tensor_reduce(tile_expert_f[:], past[:], AX_X, ALU.add))
            dve.tensor_scalar(tile_expert[:], tile_expert_f[:], float(E - 1), None, ALU.min)
            then(dve.tensor_tensor(slot[:], running[:], tile_count, ALU.subtract))
            then(dve.tensor_tensor(slot[:], slot[:], in_tile, ALU.add))
            then(dve.tensor_tensor(slot[:], slot[:], starts[:].unsqueeze(1).to_broadcast(wide), ALU.add))
            for i in range(TOP):
                then(dve.tensor_tensor(weighed[i][:], chosen[i][:], slot[:], ALU.mult))
                then(dve.tensor_reduce(slot_f[:, i, :], weighed[i][:], AX_X, ALU.add))
            dve.tensor_copy(slot_of[:], slot_f[:]).then_inc(slots_ready, 1)

            dve.wait_ge(exps, 1)
            then(dve.tensor_reduce(total[:], gap[:], AX_X, ALU.add))
            then(dve.reciprocal(total[:], total[:]))
            then(dve.tensor_tensor(gap[:, :, 0:TOP], gap[:, :, 0:TOP], total[:].unsqueeze(2).to_broadcast([P, ALL_TILES, TOP]), ALU.mult))
            dve.tensor_tensor(ratio[:], gap[:, :, 1], gap[:, :, 0], ALU.subtract).then_inc(gaps, 1)
            dve.wait_ge(exps, 2)
            then(dve.tensor_scalar(total[:], ratio[:], 1.0, None, ALU.add))
            then(dve.reciprocal(share[:, :, 0], total[:]))
            then(dve.tensor_tensor(share[:, :, 1], ratio[:], share[:, :, 0], ALU.mult))
            for i in range(TOP):
                last = dve.tensor_tensor(weighed[i][:], chosen[i][:], share[:, :, i:i + 1].to_broadcast(wide), ALU.mult)
            then(last)
            dve.tensor_tensor(combine[:], weighed[0][:], weighed[1][:], ALU.add).then_inc(combined, 1)
            for i in range(ALL_TILES // 2):
                dve.wait_ge(bias_full, i + 1)
                dve.tensor_tensor(acc[:, 2 * i:2 * i + 2, :], x_all[:, 2 * i:2 * i + 2, :], turn_bank[i % 2][:].rearrange("p (t d) -> p t d", t=2), ALU.add).then_inc(bias_added, 1)

            def fetch_bias(s, i):
                e = dve.value_load(tile_expert[0:1, bass.ds(s, 1)], min_val=0, max_val=E - 1)
                dve.tensor_copy(b1_e[i][:].unsqueeze(1), b1[:, bass.ds(e, 1), :]).then_inc(b1_ready, 1)

            def copy_out(s, i, n):
                dve.wait_ge(down_full, s + 1)
                dve.wait_ge(written[i], 16 * n)
                dve.tensor_copy(result[i][:].rearrange("p g d -> p (g d)"), down_bank[i][:]).then_inc(result_ready, 1)

            for i in range(2):
                dve.sem_inc(written[i], WRITTEN_AT_FIRST)
            fetch_bias(0, 0)
            fetch_bias(1, 1)
            with dve.Fori(0, PAIRS) as j:
                copy_out(j * 2, 0, j + 1)
                fetch_bias(j * 2 + 2, 0)
                copy_out(j * 2 + 1, 1, j + 1)
                fetch_bias(j * 2 + 3, 1)
            copy_out(SLOT_TILES - 1, 0, PAIRS + 1)

            for b in range(B):
                rows_b = range(b * TILES, (b + 1) * TILES)
                dve.wait_ge(gathered[b], 16 * TOP * TILES)
                for j in range(TOP):
                    for m in rows_b:
                        last = dve.scalar_tensor_tensor(out=acc[:, m, :], in0=got[j][:, m, :], scalar=share[:, m, j:j + 1], in1=acc[:, m, :], op0=ALU.mult, op1=ALU.add)
                    then(last)
                for m in rows_b:
                    last = dve.bn_stats(stats[:, m - b * TILES, :], acc[:, m, :])
                then(last)
                for m in range(TILES):
                    last = dve.bn_aggr(mean_var[:, m, :], stats[:, m, :])
                then(last)
                dve.tensor_scalar(var_eps[:], mean_var[:, :, 1], EPS, None, ALU.add).then_inc(var_ready, 1)
                for m in rows_b:
                    last = dve.scalar_tensor_tensor(out=centred[:, m - b * TILES, :], in0=acc[:, m, :], scalar=mean_var[:, m - b * TILES, 0:1], in1=gain[:], op0=ALU.subtract, op1=ALU.mult)
                then(last)
                dve.wait_ge(rstd_ready, b + 1)
                if b >= 2:
                    dve.wait_ge(y_out[b % 2], 16 * (b // 2))
                for m in range(TILES):
                    last = dve.scalar_tensor_tensor(out=y[b % 2][:, m, :], in0=centred[:, m, :], scalar=rstd[:, m:m + 1], in1=shift[:], op0=ALU.mult, op1=ALU.add)
                last.then_inc(y_ready, 1)
                then(last)


_OUT = ((B, S, D), "float32")


def kernel(**inputs):
    from concourse import bacc
    from concourse.bass_utils import run_bass_kernel_spmd

    nc = bacc.Bacc("TRN2", target_bir_lowering=False, num_devices=1)
    arrays, tensors = {}, {}
    for name, value in inputs.items():
        a = np.ascontiguousarray(value)
        arrays[f"in_{name}"] = a
        tensors[name] = nc.dram_tensor(f"in_{name}", a.shape, mybir.dt.from_np(a.dtype), kind="ExternalInput").ap()
    out = nc.dram_tensor("out_0", _OUT[0], F32, kind="ExternalOutput").ap()
    build(nc, tensors, out)
    r = run_bass_kernel_spmd(nc, [arrays], core_ids=[0])
    return r.results[0]["out_0"]
```

```python
from contextlib import ExitStack

import numpy as np

import concourse.bass as bass
from concourse import mybir

F32 = mybir.dt.float32
F32R = mybir.dt.float32r
BF16 = mybir.dt.bfloat16
U32 = mybir.dt.uint32
I32 = mybir.dt.int32
ALU = mybir.AluOpType
ACT = mybir.ActivationFunctionType
AX_X = mybir.AxisListType.X

P = 128
B, S, D = 8, 256, 256
H, DK = 16, 16
FF, E = 1024, 8
TILES = S // P
KC = D // P
FC = FF // P
HPC = H // KC
LANES = 4
TURNS = B // LANES
CALLS = 4
NCALL = CALLS * LANES
ALL_TILES = B * TILES
EPS = 1e-5
SCALE = DK ** -0.5
MASKED = -1e30
GROUP = 256
GT = GROUP // P
TOP = 2
REGION = 2 * B * S
EXPERT_TILES = REGION // GROUP
SLOT_TILES = (TOP * B * S + E * (GROUP - 1)) // GROUP
assert SLOT_TILES % 2 == 1
PAIRS = SLOT_TILES // 2
PLACES = SLOT_TILES + 2
X_TILES = E * EXPERT_TILES + 1
WRITTEN_AT_FIRST = 16
FFN, FINAL = "ffn", "final"
LAG = {"scalar": {"ctx": 0, "T": 0.0, "q": 1.3, "k": 0, "v": 1.0, "out_T": 0.5, "up": 0.7, "head": 0.3, "shift": 0.5, "final_T": 0.5},
       "vector": {"max": 0.5, "q": 1.7, "k": 1.7, "wo": 0.7, "down": 0.0, "turn": 0.5, "out": 0.6, "ln": 1.6, "centre": 1.8, "apply": 3.0, "router": 0.0},
       "gpsimd": {"mask": 0.6, "T": 1.0, "ln": 1.4},
       "sync": {"ctx": 4.0, "q": 3.0, "k": 2.0, "shift": 0, "store": 0.5}}
MAX_PACE = 0.75
CAUSAL = (True, False, True, False)


def plan_slot(s):
    steps = []
    if 0 <= s - 3 < NCALL:
        c, lane = divmod(s - 3, LANES)
        steps += [(0.9, "weigh", lane, (c, 3)), (1.3, "out", lane, (c, 1)), (2.2, "turn", lane, c), (3.2, "out_T", lane, c), (5.0, "wo", lane, c)]
        if c == 1:
            steps += [(5.8, "ln", lane, FFN), (5.5, "apply", lane, FFN), (9.2, "T", lane, FFN)]
            steps += [(10.2 + j, "up", lane, j) for j in range(FC // 2)]
            steps += [(13.9, "down", lane, FFN)]
        elif c == CALLS - 1:
            steps += [(6.5, "ln", lane, FINAL), (6.7, "apply", lane, FINAL), (6.5, "centre", lane, FINAL), (14.0, "store", lane, FINAL), (11.0, "final_T", lane, FINAL),
                      (14.4, "router", lane, FINAL), (18.7, "rank", lane, FINAL), (21.0, "scatter", lane, FINAL)]
    if s in (0, 1):
        steps += [(10.0, "load", s + 2, "late")]
    if s == NCALL + 2:
        steps += [(25.0, "free", lane, "late") for lane in (2, 3)]
        steps += [(1.0, "load", lane, "early") for lane in (0, 1)]
    if s < NCALL:
        c, lane = divmod(s, LANES)
        if c == 0:
            steps += [(1.0, "ctx", lane, 0)]
        if s == 0:
            steps += [(0.0, "ln", lane, c), (0.0, "apply", lane, c)]
        steps += [(0.5, "T", lane, c), (3.7, "q", lane, c), (6.2, "k", lane, c), (9.0, "v", lane, c)]
    if s + 1 < NCALL and (s + 1) // LANES != 2:
        c, lane = divmod(s + 1, LANES)
        steps += [(5.5, "ln", lane, c), (5.8, "apply", lane, c)]
        if c == CALLS - 1:
            steps += [(5.8, "centre", lane, c)]
    if 0 <= s - 1 < NCALL:
        c, lane = divmod(s - 1, LANES)
        steps += [(MAX_PACE * h, "max", lane, (c, h)) for h in range(H)]
        steps += [(MAX_PACE * H + 1.4, "shift", lane, c)]
    if 0 <= s - 2 < NCALL:
        c, lane = divmod(s - 2, LANES)
        steps += [(h + 0.1, "head", lane, (c, h)) for h in range(H)]
        if CAUSAL[c]:
            steps += [(h + 0.1, "mask", lane, (c, h)) for h in range(H)]
        steps += [(4 * g + 5.6, "weigh", lane, (c, g)) for g in range(3)]
        steps += [(11.2, "out", lane, (c, 0))]
    return [(s * H + at, kind, lane, arg) for at, kind, lane, arg in steps]


STEPS = sorted((step for s in range(NCALL + 3) for step in plan_slot(s)), key=lambda step: step[0])


def count_steps():
    place, total = {}, {}
    for _, kind, lane, arg in STEPS:
        place[kind, lane, arg] = total.get(kind, 0)
        total[kind] = total.get(kind, 0) + 1
    return place, total


PLACE, TOTAL = count_steps()
WORK_BANKS = 2
FREE_AT_FIRST = 1
USES = {"ctx": 1, "T": 1, "q": 1, "k": 1, "v": 1, "shift": 1, "turn": 2, "out_T": 1, "wo": 1, "up": 1, "down": 1, "final_T": 1, "router": 1, "rank": 1}


def count_work():
    uses, n = {}, 0
    for _, kind, lane, arg in STEPS:
        for j in range(USES.get(kind, 0)):
            uses[kind, lane, arg, j] = (n, n % WORK_BANKS, n // WORK_BANKS)
            n += 1
    return uses, n, [len(range(b, n, WORK_BANKS)) for b in range(WORK_BANKS)]


WORK, WORK_TOTAL, WORK_PER_BANK = count_work()


def build(nc, t, out):
    with ExitStack() as ctx:
        def sb(name, shape, dt=F32):
            return ctx.enter_context(nc.sbuf_tensor(name, shape, dt))

        x_rows = nc.dram_tensor("x_rows", [B, S, D], F32).ap()
        slots_x = nc.dram_tensor("slots_x", [X_TILES * GROUP, D], F32).ap()
        ident = sb("ident", [P, P])
        minus_half = sb("minus_half", [P, TILES])
        eps = sb("eps", [P, TILES])
        top = sb("top", [P, ALL_TILES, E])
        slot_of = sb("slot_of", [P, TOP, ALL_TILES], U32)
        next_slot = sb("next_slot", [P, E])
        zeros = sb("zeros", [P, S])
        attention_part(nc, t, x_rows, slots_x, zeros, ident, minus_half, eps, top, slot_of, next_slot)
        moe_part(nc, t, out, x_rows, slots_x, zeros, ident, minus_half, top, slot_of, next_slot)


def attention_part(nc, t, x_rows, slots_x, zeros, ident, minus_half, eps, top, slot_of, next_slot):
    with ExitStack() as ctx:
        def sb(name, shape, dt=F32):
            return ctx.enter_context(nc.sbuf_tensor(name, shape, dt))

        def ring(n, name, shape, dt=F32):
            return [sb(f"{name}{i}", shape, dt) for i in range(n)]

        def psum(name):
            return ctx.enter_context(nc.psum_tensor(name, [P, 512], F32))

        def sem(name):
            return ctx.enter_context(nc.semaphore(name))

        wq = [sb(f"wq{c}", [P, KC, D]) for c in range(CALLS)]
        wk = [sb(f"wk{c}", [P, KC, D]) for c in range(CALLS)]
        wv = [sb(f"wv{c}", [P, KC, D]) for c in range(CALLS)]
        wo = [sb(f"wo{c}", [P, KC, D]) for c in range(CALLS)]
        w1 = sb("w1", [P, KC, FF])
        w2 = sb("w2", [P, FC, D])
        bq = sb("bq", [P, CALLS, KC])
        bk = sb("bk", [P, CALLS, KC])
        b1 = sb("b1", [P, FC])
        bv = sb("bv", [P, CALLS, KC])
        bo = sb("bo", [P, CALLS, D])
        b2 = sb("b2", [P, D])
        pre = {0: "L0_xattn_ln1", 1: "L0_xattn_ln2", FFN: "L0_xattn_ln3"}
        pre_gain = {k: sb(f"pre_gain_{k}", [P, KC]) for k in pre}
        pre_shift = {k: sb(f"pre_shift_{k}", [P, KC]) for k in pre}
        post = {3: "L1_xattn_ln1", FINAL: "L1_xattn_ln2"}
        gain = {k: sb(f"gain_{k}", [P, D]) for k in post}
        shift = {k: sb(f"shift_{k}", [P, D]) for k in post}
        ident_b = sb("ident_b", [P, P], BF16)
        mask_qk = sb("mask_qk", [P, P], BF16)
        x = ring(LANES, "x", [P, TILES, D])
        cT = ring(LANES, "cT", [P, KC, S])
        q_stack = ring(3, "q_stack", [P, HPC, S], F32R)
        k_stack = ring(3, "k_stack", [P, HPC, S], F32R)
        v = ring(3, "v", [P, TILES, H, 2 * DK])
        ctx_in = ring(2, "ctx_in", [P, TILES, D])
        h = ring(2, "h", [P, TILES, D])
        hT = ring(2, "hT", [P, KC, S])
        u = ring(2, "u", [P, H // 4, S])
        q_hi, q_lo, k_hi, k_lo = (sb(n, [P, KC, S], F32R) for n in ("q_hi", "q_lo", "k_hi", "k_lo"))
        router_w = sb("router_w", [P, KC, E])
        router_b = sb("router_b", [P, E])
        iota_e = sb("router_iota", [P, E])
        before = sb("before", [P, P], BF16)
        ones = sb("ones", [P, P], BF16)
        logits = sb("logits", [P, TILES, E])
        ordered = sb("ordered", [P, TILES, E])
        index = sb("index", [P, TILES, E], U32)
        index_f = sb("index_f", [P, TILES, TOP])
        chosen = [sb(f"chosen{i}", [P, TILES, E]) for i in range(TOP)]
        both = sb("both", [P, TILES * E], BF16)
        slot_e = sb("slot_e", [P, TILES, E])
        slot_chosen = [sb(f"slot_chosen{i}", [P, TILES, E]) for i in range(TOP)]
        slot_f = sb("slot_f", [P, TOP, TILES])
        slots = [sb(f"slots{i}", [P, TOP, TILES], U32) for i in range(LANES)]
        neg_max = sb("neg_max", [P, TILES, H])
        neg_max_T = sb("neg_max_T", [H, S], F32R)
        probs = ring(8, "probs", [P, TILES * S])
        inv_sum = sb("inv_sum", [P, TILES, H])
        o = sb("o", [P, TILES, D])
        oT = sb("oT", [P, KC, S])
        hidden = sb("hidden", [P, FC, S])
        stats = sb("stats", [P, TILES, 6])
        mean_var = sb("mean_var", [P, TILES, 2])
        var_eps = sb("var_eps", [P, TILES])
        rstd = sb("rstd", [P, TILES])
        centred = sb("centred", [P, TILES, D])
        raw_q = [hidden[:, 2 * c:2 * c + 2, :] for c in range(CALLS)]
        raw_k = [u[c // 2][:, 2 * (c % 2):2 * (c % 2) + 2, :] for c in range(CALLS)]
        work = [psum(f"work{i}") for i in range(WORK_BANKS)]
        s1 = [psum(f"s1_{i}") for i in range(2)]
        s2 = [psum(f"s2_{i}") for i in range(2)]
        pv = [psum(f"pv{i}") for i in range(2)]
        consts = sem("consts")
        loaded_qk = [sem(f"loaded_qk{c}") for c in range(CALLS)]
        loaded_vo = [sem(f"loaded_vo{c}") for c in range(CALLS)]
        loaded_ffn = sem("loaded_ffn")
        reordered = sem("reordered")
        loaded_rows = sem("loaded_rows")
        loaded_rest = sem("loaded_rest")
        x_in = [sem(f"x_in{i}") for i in range(LANES)]
        ctx_loaded = [sem(f"ctx_loaded{i}") for i in range(2)]
        work_full = sem("work_full")
        work_free = [sem(f"work_free{i}") for i in range(WORK_BANKS)]
        var_ready = sem("var_ready")
        rstd_ready = sem("rstd_ready")
        h_ready = sem("h_ready")
        ctx_T_ready = sem("ctx_T_ready")
        hT_ready = sem("hT_ready")
        q_hi_ready = sem("q_hi_ready")
        k_hi_ready = sem("k_hi_ready")
        q_lo_ready = sem("q_lo_ready")
        k_lo_ready = sem("k_lo_ready")
        v_ready = sem("v_ready")
        stacked = [sem(f"stacked{i}") for i in range(3)]
        shift_T_ready = sem("shift_T_ready")
        shift_stacked = [sem(f"shift_stacked{i}") for i in range(3)]
        s1_full = sem("s1_full")
        s1_free = [sem(f"s1_free{i}") for i in range(2)]
        s2_full = sem("s2_full")
        probs_ready = sem("probs_ready")
        weighed = [sem(f"weighed{i}") for i in range(2)]
        u_ready = [sem(f"u_ready{i}") for i in range(2)]
        o_ready = sem("o_ready")
        oT_ready = sem("oT_ready")
        x_biased = sem("x_biased")
        x_ready = sem("x_ready")
        hidden_ready = sem("hidden_ready")
        final_T_ready = sem("final_T_ready")
        both_ready = sem("both_ready")
        slots_ready = sem("slots_ready")
        scattered = [sem(f"scattered{i}") for i in range(LANES)]
        x_free = [sem(f"x_free{i}") for i in range(2)]
        zeroed = sem("zeroed")
        gate = sem("scatter_gate")
        masked = sem("masked")
        stored = sem("stored")

        def nth(it, kind, lane, arg):
            return it * TOTAL[kind] + PLACE[kind, lane, arg] + 1

        def filled(it, kind, lane, arg, j=0):
            return it * WORK_TOTAL + WORK[kind, lane, arg, j][0] + 1

        def bank(kind, lane, arg, j=0):
            return work[WORK[kind, lane, arg, j][1]]

        def freed(kind, lane, arg, j=0):
            return work_free[WORK[kind, lane, arg, j][1]]

        def bank_uses(it, kind, lane, arg, j=0):
            _, b, k = WORK[kind, lane, arg, j]
            return it * WORK_PER_BANK[b] + k + FREE_AT_FIRST

        def call(it, n):
            return it * NCALL + n

        def run(it, step, lag):
            own = [(at + lag.get(kind, 0), kind, lane, arg) for at, kind, lane, arg in STEPS if kind in step]
            for _, kind, lane, arg in sorted(own, key=lambda one: one[0]):
                step[kind](it, lane, arg)

        def exps_done(it, n, hd):
            return call(it, n) * H + hd + 1 + len(s2)

        def buffer_uses(it, n):
            return it * len(range(n % 3, NCALL, 3)) + n // 3 + 1

        STACK_LOADS = 13
        SCATTER = 16 * TOP * TILES
        layers = ["L0_xattn_mmha_w{}", "L0_xattn_mha_w{}", "L1_xattn_sa_w{}", "L1_xattn_ca_w{}"]
        biases = ["L0_xattn_mmha_w{}_b", "L0_xattn_mha_w{}_b", "L1_xattn_sa_b{}", "L1_xattn_ca_b{}"]
        CALL_ROWS = 2 * KC + 2
        FIRST_ROWS = CALL_ROWS + 2
        REST_ROWS = (CALLS - 1) * CALL_ROWS + 2 + 2 * (len(pre) - 1) + 2 * len(post) + 2

        def load_biases(engine, c, done):
            with nc.allow_non_contiguous_dma(reason="biases, one for each partition"):
                for dst, key in ((bq, "q"), (bk, "k")):
                    for half in range(KC):
                        src = t[biases[c].format(key)].rearrange("(c i d) -> c d i", c=KC, d=DK)[half]
                        engine.dma_start(dst[:, c, half:half + 1], src.rearrange("d (i a) -> d i a", a=1)).then_inc(done, 16)
                engine.dma_start(bv[:, c, :], t[biases[c].format("v")].rearrange("(k p) -> p k", p=P)).then_inc(done, 16)
            engine.dma_start(bo[:, c, :], t[biases[c].format("o")].partition_broadcast(P)).then_inc(done, 16)

        def load_pre(engine, k, done):
            with nc.allow_non_contiguous_dma(reason="gains and shifts, one for each partition"):
                engine.dma_start(pre_gain[k][:], t[pre[k] + "_g"].rearrange("(k p) -> p k", p=P)).then_inc(done, 16)
                engine.dma_start(pre_shift[k][:], t[pre[k] + "_b"].rearrange("(k p) -> p k", p=P)).then_inc(done, 16)

        block = ctx.enter_context(nc.Block())

        @block.sync
        def _(sp):
            def rows_of(src, it, lane):
                return src.rearrange("b (t p) d -> p (b t) d", p=P)[:, bass.ds((it * LANES + lane) * TILES, TILES), :]

            def load_x(it, lane):
                sp.dma_start(x[lane][:], rows_of(t["x"], it, lane)).then_inc(x_in[lane], 16)

            def load_context(it, lane):
                sp.dma_start(ctx_in[lane % 2][:], rows_of(t["ctx_1024"], it, lane)).then_inc(ctx_loaded[lane % 2], 16)

            load_x(0, 0)
            for c in range(CALLS):
                for w, key in ((raw_q, "q"), (raw_k, "k")):
                    sp.dma_start(w[c][:], t[layers[c].format(key)].rearrange("(k p) n -> p k n", p=P)).then_inc(loaded_qk[c], 16)
                if c == 0:
                    load_context(0, 0)
            for c in range(CALLS):
                for w, key in ((wv, "v"), (wo, "o")):
                    sp.dma_start(w[c][:], t[layers[c].format(key)].rearrange("(k p) n -> p k n", p=P)).then_inc(loaded_vo[c], 16)
                if c == 0:
                    load_x(0, 1)
                    load_context(0, 1)
            for w, name in ((w1, "L0_xattn_ffn_w1"), (w2, "L0_xattn_ffn_w2")):
                sp.dma_start(w[:], t[name].rearrange("(k p) n -> p k n", p=P)).then_inc(loaded_ffn, 16)

            for k in (1, FFN):
                load_pre(sp, k, loaded_rest)
            for c in range(1, CALLS):
                load_biases(sp, c, loaded_rest)
            for k, name in post.items():
                sp.dma_start(gain[k][:], t[name + "_g"].partition_broadcast(P)).then_inc(loaded_rest, 16)
                sp.dma_start(shift[k][:], t[name + "_b"].partition_broadcast(P)).then_inc(loaded_rest, 16)
            with nc.allow_non_contiguous_dma(reason="1024 biases"):
                sp.dma_start(b1[:], t["L0_xattn_ffn_b1"].rearrange("(f p) -> p f", p=P)).then_inc(loaded_rest, 16)
            sp.dma_start(b2[:], t["L0_xattn_ffn_b2"].partition_broadcast(P)).then_inc(loaded_rest, 16)
            sp.dma_start(router_w[:], t["L1_xattn_router_w"].rearrange("(k p) n -> p k n", p=P)).then_inc(loaded_rest, 16)
            sp.dma_start(router_b[:], t["L1_xattn_router_b"].partition_broadcast(P)).then_inc(loaded_rest, 16)
            sp.wait_ge(consts, 1)
            sp.dma_start(slots_x[E * REGION:E * REGION + GROUP, :].rearrange("(g p) d -> p g d", p=P), zeros[:].unsqueeze(1).to_broadcast([P, GT, D])).then_inc(zeroed, 16)

            def stack_q(it, lane, c):
                buf = (c * LANES + lane) % 3
                sp.wait_ge(q_hi_ready, nth(it, "q", lane, c))
                for half in range(KC):
                    for row in (0, 2 * DK):
                        at = half * 64 + row
                        sp.dma_start(q_stack[buf][at:at + DK].bitcast(F32), q_hi[:, half, :].bitcast(F32)).then_inc(stacked[buf], 16)
                rows = q_stack[buf][3 * DK:3 * DK + 65:64].bitcast(F32)
                sp.dma_start(rows, zeros[0:2].unsqueeze(1).to_broadcast([2, HPC, S])).then_inc(stacked[buf], 16)
                sp.wait_ge(q_lo_ready, nth(it, "q", lane, c))
                for half in range(KC):
                    at = half * 64 + DK
                    sp.dma_start(q_stack[buf][at:at + DK].bitcast(F32), q_lo[:, half, :].bitcast(F32)).then_inc(stacked[buf], 16)

            def stack_k(it, lane, c):
                buf = (c * LANES + lane) % 3
                sp.wait_ge(k_hi_ready, nth(it, "k", lane, c))
                for half in range(KC):
                    for row in (0, DK):
                        at = half * 64 + row
                        sp.dma_start(k_stack[buf][at:at + DK].bitcast(F32), k_hi[:, half, :].bitcast(F32)).then_inc(stacked[buf], 16)
                sp.wait_ge(k_lo_ready, nth(it, "k", lane, c))
                for half in range(KC):
                    at = half * 64 + 2 * DK
                    sp.dma_start(k_stack[buf][at:at + DK].bitcast(F32), k_lo[:, half, :].bitcast(F32)).then_inc(stacked[buf], 16)

            def stack_shift(it, lane, c):
                sp.wait_ge(shift_T_ready, nth(it, "shift", lane, c))
                buf = (c * LANES + lane) % 3
                rows = q_stack[buf][3 * DK:3 * DK + 65:64].bitcast(F32)
                sp.dma_start(rows, neg_max_T[:].bitcast(F32)).then_inc(shift_stacked[buf], 16)

            def next_context(it, lane, _):
                sp.wait_ge(ctx_T_ready, nth(it, "ctx", lane, 0))
                if lane < 2:
                    load_context(it, lane + 2)
                else:
                    load_context((it + 1) % TURNS, lane - 2)

            def store(it, lane, _):
                sp.wait_ge(work_full, filled(it, "final_T", lane, FINAL))
                sp.dma_start(rows_of(x_rows, it, lane), x[lane][:]).then_inc(stored, 16)

            def load(it, lane, when):
                if when == "late":
                    sp.wait_ge(x_free[lane - 2], it + FREE_AT_FIRST)
                    load_x(it, lane)
                else:
                    sp.wait_ge(scattered[lane], SCATTER * (it + 1))
                    load_x((it + 1) % TURNS, lane)

            with sp.Fori(0, TURNS) as it:
                run(it, {"ctx": next_context, "q": stack_q, "k": stack_k, "shift": stack_shift, "store": store, "load": load}, LAG["sync"])
            sp.wait_ge(zeroed, 16)
            sp.wait_ge(stored, 16 * B)
            for lane in (0, 1):
                sp.wait_ge(x_in[lane], 16 * (TURNS + 1))
            for lane in range(LANES):
                sp.wait_ge(scattered[lane], SCATTER * TURNS)
            for i in range(2):
                sp.wait_ge(ctx_loaded[i], 16 * (2 * TURNS + 1))

        @block.gpsimd
        def _(pool):
            pool.memset(ident[:], 0.0)
            pool.memset(minus_half[:], -0.5)
            pool.memset(eps[:], EPS)
            pool.memset(mask_qk[:], 0.0)
            pool.memset(ident_b[:], 0.0)
            pool.memset(zeros[:], 0.0)
            pool.memset(ones[:], 1.0)
            pool.iota(iota_e[:], pattern=[[1, E]], base=0, channel_multiplier=0, allow_small_or_imprecise_dtypes=True)
            pool.iota(next_slot[:], pattern=[[REGION, E]], base=0, channel_multiplier=0, allow_small_or_imprecise_dtypes=True)
            for buf in v:
                pool.memset(buf[:], 1.0)
            pool.memset(k_stack[2][:].bitcast(F32), 1.0)
            pool.memset(q_stack[2][:].bitcast(F32), 0.0)
            pool.drain()
            for m in (ident, ident_b):
                pool.affine_select(out=m[:], in_=m[:], compare_op=ALU.not_equal, fill=1.0, base=0, pattern=[[-1, P]], channel_multiplier=1)
            pool.affine_select(out=before[:], in_=ones[:], compare_op=ALU.is_gt, fill=0.0, base=0, pattern=[[1, P]], channel_multiplier=-1)
            pool.affine_select(out=mask_qk[:], in_=mask_qk[:], compare_op=ALU.is_ge, fill=MASKED, base=0, pattern=[[-1, P]], channel_multiplier=1)
            pool.drain()
            pool.sem_inc(consts, 1)
            def inverse_root(it, lane, stage):
                pool.wait_ge(var_ready, nth(it, "ln", lane, stage))
                pool.tensor_tensor(var_eps[:], mean_var[:, :, 1], eps[:], ALU.add)
                pool.drain()
                pool.tensor_tensor(rstd[:], var_eps[:], minus_half[:], ALU.pow).then_inc(rstd_ready, 1)

            pool.wait_ge(loaded_rows, 16 * FIRST_ROWS)

            def add_bias(it, lane, stage):
                if stage == 1 and lane == 0:
                    pool.wait_ge(loaded_rest, 16 * REST_ROWS)
                pool.wait_ge(work_full, filled(it, "T", lane, stage))
                row = b2[:] if stage == FFN else bo[:, stage, :]
                pool.tensor_tensor(x[lane][:], x[lane][:], row.unsqueeze(1).to_broadcast([P, TILES, D]), ALU.add).then_inc(x_biased, 1)

            def mask(it, lane, arg):
                c, hd = arg
                pool.wait_ge(probs_ready, exps_done(it, c * LANES + lane, hd))
                pool.sem_inc(gate, 1)
                blocks = probs[hd % 8][:].rearrange("p (k s) -> p k s", k=TILES)[:, :, 0:P]
                pool.affine_select(out=blocks, in_=blocks, compare_op=ALU.is_ge, fill=0.0, base=0, pattern=[[0, TILES], [1, P]], channel_multiplier=-1).then_inc(masked, 1)

            def scatter(it, lane, stage):
                pool.wait_ge(slots_ready, nth(it, "rank", lane, stage))
                pool.sem_inc(gate, 1)
                for i in range(TILES):
                    for j in range(TOP):
                        pool.indirect_dma_start(slots_x, bass.IndirectOffsetOnAxis(ap=slots[lane][:, j, i:i + 1], axis=0), x[lane][:, i, :], None).then_inc(scattered[lane], 16)

            def free_x(it, lane, _):
                pool.wait_ge(scattered[lane], SCATTER * (it + 1))
                pool.sem_inc(x_free[lane - 2], 1)

            with pool.Fori(0, TURNS) as it:
                run(it, {"ln": inverse_root, "T": add_bias, "mask": mask, "scatter": scatter, "free": free_x}, LAG["gpsimd"])

        @block.tensor
        def _(pe):
            for free in (*x_free, *work_free, *s1_free, *u_ready, *weighed):
                pe.sem_inc(free, FREE_AT_FIRST)
            pe.sem_inc(probs_ready, len(s2))
            pe.wait_ge(consts, 1)

            def take(it, kind, lane, arg, j=0):
                pe.wait_ge(freed(kind, lane, arg, j), bank_uses(it, kind, lane, arg, j))
                return bank(kind, lane, arg, j)

            def transpose_rows(dst, src):
                for k in range(KC):
                    for i in range(TILES):
                        last = pe.transpose(dst[:, k * S + i * P:k * S + (i + 1) * P], src[:, i, k * P:(k + 1) * P], ident[:])
                return last

            def ctx_T(it, lane, _):
                pe.wait_ge(ctx_loaded[lane % 2], 16 * (it * 2 + lane // 2 + 1))
                transpose_rows(take(it, "ctx", lane, 0), ctx_in[lane % 2]).then_inc(work_full, 1)

            def rows_T(it, lane, stage):
                if stage == 2:
                    pe.wait_ge(x_ready, it * (TOTAL["wo"] + TOTAL["down"]) + X_PLACE["down", lane, FFN] + 1)
                    src = x[lane]
                else:
                    pe.wait_ge(h_ready, nth(it, "ln", lane, stage))
                    src = x[lane] if stage == 3 else h[lane % 2]
                transpose_rows(take(it, "T", lane, stage), src).then_inc(work_full, 1)

            def project(it, kind, lane, c, w, src):
                dst = take(it, kind, lane, c)
                for half in range(KC):
                    for k in range(KC):
                        last = pe.matmul(dst[:, half * S:(half + 1) * S], w[c][:, k, half * P:(half + 1) * P], src[:, k, :], start=(k == 0), stop=(k == KC - 1))
                last.then_inc(work_full, 1)

            def project_q(it, lane, c):
                pe.wait_ge(reordered, c + 1)
                pe.wait_ge(hT_ready, nth(it, "T", lane, c))
                project(it, "q", lane, c, wq, hT[lane % 2])

            def project_k(it, lane, c):
                if not CAUSAL[c]:
                    pe.wait_ge(ctx_T_ready, nth(it, "ctx", lane, 0))
                project(it, "k", lane, c, wk, hT[lane % 2] if CAUSAL[c] else cT[lane])

            def project_rows(it, kind, lane, arg, w, src, chunks):
                dst = take(it, kind, lane, arg)
                for i in range(TILES):
                    for k in range(chunks):
                        last = pe.matmul(dst[:, i * D:(i + 1) * D], src[:, k, i * P:(i + 1) * P], w[:, k, :], start=(k == 0), stop=(k == chunks - 1))
                last.then_inc(work_full, 1)

            def project_v(it, lane, c):
                if lane == 0:
                    pe.wait_ge(loaded_vo[c], 16 * 2)
                project_rows(it, "v", lane, c, wv[c], hT[lane % 2] if CAUSAL[c] else cT[lane], KC)

            def scores_for_max(it, lane, arg):
                c, hd = arg
                n = c * LANES + lane
                if hd == 0:
                    pe.wait_ge(stacked[n % 3], 16 * STACK_LOADS * buffer_uses(it, n))
                pe.wait_ge(s1_free[hd % 2], call(it, n) * (H // 2) + hd // 2 + FREE_AT_FIRST)
                i, r = hd % HPC, 64 * (hd // HPC)
                dst = s1[hd % 2]
                for qt in range(TILES):
                    keys = (qt + 1) * P if CAUSAL[c] else S
                    last = pe.matmul(dst[:, qt * S:qt * S + keys], q_stack[n % 3][r:r + 4 * DK, i, qt * P:(qt + 1) * P],
                                     k_stack[n % 3][r:r + 4 * DK, i, 0:keys], start=True, stop=not CAUSAL[c])
                    if CAUSAL[c]:
                        last = pe.matmul(dst[:, qt * S + qt * P:qt * S + keys], ident_b[:], mask_qk[:], start=False, stop=True)
                last.then_inc(s1_full, 1)

            def shift_T(it, lane, c):
                n = c * LANES + lane
                for i in range(2):
                    pe.wait_ge(s1_free[i], (call(it, n) + 1) * (H // 2) + FREE_AT_FIRST)
                dst = take(it, "shift", lane, c)
                for qt in range(TILES):
                    last = pe.transpose(dst[0:H, qt * P:(qt + 1) * P], neg_max[:, qt, :], ident[:])
                last.then_inc(work_full, 1)

            def scores(it, lane, arg):
                c, hd = arg
                n = c * LANES + lane
                if hd == 0:
                    pe.wait_ge(shift_stacked[n % 3], 16 * buffer_uses(it, n))
                pe.wait_ge(probs_ready, exps_done(it, n, hd - len(s2)))
                i, r = hd % HPC, 64 * (hd // HPC)
                dst = s2[hd % 2]
                for kt in range(TILES):
                    q0 = kt * P if CAUSAL[c] else 0
                    last = pe.matmul(dst[:, kt * S:kt * S + S - q0], k_stack[n % 3][r:r + 4 * DK, i, kt * P:(kt + 1) * P],
                                     q_stack[n % 3][r:r + 4 * DK, i, q0:S], start=True, stop=True)
                last.then_inc(s2_full, 1)

            def weigh_values(it, lane, arg):
                c, g = arg
                n = c * LANES + lane
                dst, at = pv[g // 2], (g % 2) * S
                if g == 0:
                    pe.wait_ge(v_ready, nth(it, "v", lane, c))
                if g % 2 == 0:
                    pe.wait_ge(u_ready[g // 2], call(it, n) + FREE_AT_FIRST)
                if CAUSAL[c]:
                    pe.wait_ge(masked, nth(it, "mask", lane, (c, 4 * g + 3)))
                else:
                    pe.wait_ge(probs_ready, exps_done(it, n, 4 * g + 3))
                for kt in range(TILES):
                    q0 = kt * P if CAUSAL[c] else 0
                    for j in range(4):
                        hd = 4 * g + j
                        last = pe.matmul(dst[32 * j:32 * j + 32, at + q0:at + S], v[n % 3][:, kt, hd, :],
                                         probs[hd % 8][:, kt * S:kt * S + S - q0], start=(kt == 0), stop=(kt == TILES - 1))
                last.then_inc(weighed[g % 2], 1)

            def turn(it, lane, c):
                n = c * LANES + lane
                for i in range(2):
                    pe.wait_ge(u_ready[i], call(it, n) + 1 + FREE_AT_FIRST)
                for qt in range(TILES):
                    dst = take(it, "turn", lane, c, qt)
                    for g in range(H // 4):
                        last = pe.transpose(dst[:, g * P:(g + 1) * P], u[n % 2][:, g, qt * P:(qt + 1) * P], ident[:])
                    last.then_inc(work_full, 1)

            def out_T(it, lane, c):
                pe.wait_ge(o_ready, nth(it, "turn", lane, c))
                transpose_rows(take(it, "out_T", lane, c), o).then_inc(work_full, 1)

            def out_project(it, lane, c):
                pe.wait_ge(oT_ready, nth(it, "out_T", lane, c))
                project_rows(it, "wo", lane, c, wo[c], oT, KC)

            def final_T(it, lane, stage):
                pe.wait_ge(h_ready, nth(it, "ln", lane, stage))
                transpose_rows(take(it, "final_T", lane, stage), x[lane]).then_inc(work_full, 1)

            def router(it, lane, stage):
                pe.wait_ge(final_T_ready, nth(it, "final_T", lane, stage))
                dst = take(it, "router", lane, stage)
                for i in range(TILES):
                    for k in range(KC):
                        last = pe.matmul(dst[:, i * E:(i + 1) * E], hT[lane % 2][:, k, i * P:(i + 1) * P], router_w[:, k, :], start=(k == 0), stop=(k == KC - 1))
                last.then_inc(work_full, 1)

            def rank(it, lane, stage):
                pe.wait_ge(both_ready, nth(it, "router", lane, stage))
                dst = take(it, "rank", lane, stage)
                pe.matmul(dst[:, 0:TILES * E], before[:], both[:], start=True, stop=True)
                pe.matmul(dst[:, TILES * E:2 * TILES * E], ones[:], both[:], start=True, stop=True).then_inc(work_full, 1)

            def up(it, lane, j):
                if j == 0:
                    pe.wait_ge(loaded_ffn, 16 * 2)
                    pe.wait_ge(hT_ready, nth(it, "T", lane, FFN))
                dst = take(it, "up", lane, j)
                for m in range(2):
                    f = 2 * j + m
                    for k in range(KC):
                        last = pe.matmul(dst[:, m * S:(m + 1) * S], w1[:, k, f * P:(f + 1) * P], hT[lane % 2][:, k, :], start=(k == 0), stop=(k == KC - 1))
                last.then_inc(work_full, 1)

            def down(it, lane, _):
                pe.wait_ge(hidden_ready, nth(it, "up", lane, FC // 2 - 1))
                project_rows(it, "down", lane, FFN, w2, hidden, FC)

            with pe.Fori(0, TURNS) as it:
                run(it, {"ctx": ctx_T, "T": rows_T, "q": project_q, "k": project_k, "v": project_v, "max": scores_for_max,
                             "shift": shift_T, "head": scores, "weigh": weigh_values, "turn": turn, "out_T": out_T, "wo": out_project, "up": up, "down": down,
                         "final_T": final_T, "router": router, "rank": rank}, {})

        @block.scalar
        def _(act):
            load_pre(act, 0, loaded_rows)
            load_biases(act, 0, loaded_rows)
            act.wait_ge(loaded_rows, 16 * FIRST_ROWS)

            def ctx_T(it, lane, _):
                act.wait_ge(work_full, filled(it, "ctx", lane, 0))
                act.activation(cT[lane][:].rearrange("p k s -> p (k s)"), bank("ctx", lane, 0)[:], ACT.Copy).then_inc(freed("ctx", lane, 0), 1)
                act.drain()
                act.sem_inc(ctx_T_ready, 1)

            def rows_T(it, lane, stage):
                if stage == 1 and lane == 0:
                    act.wait_ge(loaded_rest, 16 * REST_ROWS)
                act.wait_ge(work_full, filled(it, "T", lane, stage))
                for k in range(KC):
                    dst, src = hT[lane % 2][:, k, :], bank("T", lane, stage)[:, k * S:(k + 1) * S]
                    if stage in pre:
                        last = act.activation(dst, src, ACT.Identity, bias=pre_shift[stage][:, k:k + 1], scale=pre_gain[stage][:, k:k + 1])
                    else:
                        last = act.activation(dst, src, ACT.Copy)
                last.then_inc(freed("T", lane, stage), 1)
                act.drain()
                act.sem_inc(hT_ready, 1)

            def final_T(it, lane, stage):
                act.wait_ge(work_full, filled(it, "final_T", lane, stage))
                act.activation(hT[lane % 2][:].rearrange("p k s -> p (k s)"), bank("final_T", lane, stage)[:], ACT.Copy).then_inc(final_T_ready, 1)
                act.drain()
                act.sem_inc(freed("final_T", lane, stage), 1)

            def hi_part(kind, dst, bias, ready):
                def step(it, lane, c):
                    act.wait_ge(work_full, filled(it, kind, lane, c))
                    for half in range(KC):
                        last = act.activation(dst[:, half, :], bank(kind, lane, c)[:, half * S:(half + 1) * S], ACT.Identity, bias=bias[:, c, half:half + 1])
                    last.then_inc(ready, 1)
                return step

            def shift_T(it, lane, c):
                act.wait_ge(work_full, filled(it, "shift", lane, c))
                act.activation(neg_max_T[:], bank("shift", lane, c)[0:H, 0:S], ACT.Copy).then_inc(shift_T_ready, 1)
                act.drain()
                act.sem_inc(freed("shift", lane, c), 1)

            def values(it, lane, c):
                act.wait_ge(work_full, filled(it, "v", lane, c))
                act.activation(v[(c * LANES + lane) % 3][:, :, :, 0:DK], bank("v", lane, c)[:].rearrange("p (t h d) -> p t h d", t=TILES, d=DK), ACT.Copy).then_inc(freed("v", lane, c), 1)
                act.drain()
                act.sem_inc(v_ready, 1)

            def out_T(it, lane, c):
                act.wait_ge(work_full, filled(it, "out_T", lane, c))
                for k in range(KC):
                    last = act.activation(oT[:, k, :], bank("out_T", lane, c)[:, k * S:(k + 1) * S], ACT.Identity, bias=bv[:, c, k:k + 1])
                last.then_inc(oT_ready, 1)
                act.drain()
                act.sem_inc(freed("out_T", lane, c), 1)

            def up(it, lane, j):
                act.wait_ge(work_full, filled(it, "up", lane, j))
                for m in range(2):
                    f = 2 * j + m
                    act.activation(hidden[:, f, :], bank("up", lane, j)[:, m * S:(m + 1) * S], ACT.Relu, bias=b1[:, f:f + 1])
                act.drain()
                act.sem_inc(freed("up", lane, j), 1)
                act.sem_inc(hidden_ready, 1)

            def exps(it, lane, arg):
                c, hd = arg
                n = c * LANES + lane
                width = S + P if CAUSAL[c] else TILES * S
                act.wait_ge(s2_full, call(it, n) * H + hd + 1)
                if hd % 4 == 0:
                    act.wait_ge(weighed[hd // 4 % 2], call(it, n) * 2 + hd // 8 + FREE_AT_FIRST)
                act.activation(probs[hd % 8][:, 0:width], s2[hd % 2][:, 0:width], ACT.Exp, scale=SCALE).then_inc(probs_ready, 1)

            with act.Fori(0, TURNS) as it:
                run(it, {"ctx": ctx_T, "v": values, "T": rows_T, "q": hi_part("q", q_hi, bq, q_hi_ready), "k": hi_part("k", k_hi, bk, k_hi_ready),
                              "shift": shift_T, "head": exps, "out_T": out_T, "up": up, "final_T": final_T}, LAG["scalar"])

        @block.vector
        def _(dve):
            for i in range(2):
                dve.memset(k_stack[i][:].bitcast(F32), 1.0)
                dve.memset(q_stack[i][:].bitcast(F32), 0.0)
            dve.drain()
            for c in range(CALLS):
                dve.wait_ge(loaded_qk[c], 16 * 2)
                for w, raw in ((wq, raw_q), (wk, raw_k)):
                    for k in range(KC):
                        for half in range(KC):
                            last = dve.tensor_copy(w[c][:, k, half * P:(half + 1) * P].rearrange("p (d i) -> p d i", d=DK),
                                                   raw[c][:, k, half * P:(half + 1) * P].rearrange("p (i d) -> p d i", d=DK))
                last.then_inc(reordered, 1)
            dve.drain()
            dve.wait_ge(loaded_rows, 16 * FIRST_ROWS)
            dve.wait_ge(consts, 1)

            def norm(it, lane, stage):
                if stage == 0:
                    dve.wait_ge(x_in[lane], 16 * (it + 1))
                src = x[lane]
                for i in range(TILES):
                    dve.bn_stats(stats[:, i, :], src[:, i, :])
                dve.drain()
                for i in range(TILES):
                    dve.bn_aggr(mean_var[:, i, :], stats[:, i, :])
                dve.drain()
                dve.sem_inc(var_ready, 1)

            def centre(it, lane, stage):
                for i in range(TILES):
                    dve.scalar_tensor_tensor(out=centred[:, i, :], in0=x[lane][:, i, :], scalar=mean_var[:, i, 0:1], in1=gain[stage][:], op0=ALU.subtract, op1=ALU.mult)
                dve.drain()

            def apply_norm(it, lane, stage):
                src = x[lane]
                dve.wait_ge(rstd_ready, nth(it, "ln", lane, stage))
                for i in range(TILES):
                    if stage in post:
                        last = dve.scalar_tensor_tensor(out=src[:, i, :], in0=centred[:, i, :], scalar=rstd[:, i:i + 1], in1=shift[stage][:], op0=ALU.mult, op1=ALU.add)
                    else:
                        last = dve.tensor_scalar(h[lane % 2][:, i, :], src[:, i, :], mean_var[:, i, 0:1], rstd[:, i:i + 1], ALU.subtract, ALU.mult)
                last.then_inc(h_ready, 1)
                dve.drain()

            def lo_part(kind, hi, dst, bias, hi_ready, ready):
                def step(it, lane, c):
                    if c == 1 and lane == 0:
                        dve.wait_ge(loaded_rest, 16 * REST_ROWS)
                    dve.wait_ge(hi_ready, nth(it, kind, lane, c))
                    for half in range(KC):
                        dve.scalar_tensor_tensor(out=dst[:, half, :], in0=bank(kind, lane, c)[:, half * S:(half + 1) * S], scalar=bias[:, c, half:half + 1],
                                                 in1=hi[:, half, :].bitcast(F32), op0=ALU.add, op1=ALU.subtract)
                    dve.drain()
                    dve.sem_inc(ready, 1)
                    dve.sem_inc(freed(kind, lane, c), 1)
                return step

            def row_max(it, lane, arg):
                c, hd = arg
                n = c * LANES + lane
                dve.wait_ge(s1_full, call(it, n) * H + hd + 1)
                src = s1[hd % 2]
                if CAUSAL[c]:
                    dve.tensor_reduce(neg_max[:, 0, hd:hd + 1], src[:, 0:P], AX_X, ALU.max, negate=True)
                    last = dve.tensor_reduce(neg_max[:, 1, hd:hd + 1], src[:, S:2 * S], AX_X, ALU.max, negate=True)
                else:
                    last = dve.tensor_reduce(neg_max[:, :, hd], src[:].rearrange("p (t s) -> p t s", t=TILES), AX_X, ALU.max, negate=True)
                last.then_inc(s1_free[hd % 2], 1)

            def copy_out(it, lane, arg):
                c, i = arg
                n = c * LANES + lane
                dve.wait_ge(weighed[1], call(it, n) * 2 + i + 1 + FREE_AT_FIRST)
                dve.tensor_copy(u[n % 2][:, 2 * i:2 * i + 2, :].rearrange("p g s -> p (g s)"), pv[i][:]).then_inc(u_ready[i], 1)

            def normalise(it, lane, c):
                for qt in range(TILES):
                    dve.wait_ge(work_full, filled(it, "turn", lane, c, qt))
                    src = bank("turn", lane, c, qt)[:].rearrange("p (h e) -> p h e", e=2 * DK)
                    dve.reciprocal(inv_sum[:, qt, :], src[:, :, DK])
                    dve.drain()
                    dve.tensor_tensor(o[:, qt, :].rearrange("p (h d) -> p h d", d=DK), src[:, :, 0:DK],
                                      inv_sum[:, qt, :].unsqueeze(2).to_broadcast([P, H, DK]), ALU.mult).then_inc(freed("turn", lane, c, qt), 1)
                dve.drain()
                dve.sem_inc(o_ready, 1)

            def residual(it, kind, lane, arg, stage):
                dve.wait_ge(work_full, filled(it, kind, lane, arg))
                dve.wait_ge(x_biased, nth(it, "T", lane, stage))
                dve.tensor_tensor(x[lane][:], x[lane][:], bank(kind, lane, arg)[:].rearrange("p (t d) -> p t d", t=TILES), ALU.add).then_inc(x_ready, 1)
                dve.drain()
                dve.sem_inc(freed(kind, lane, arg), 1)

            def choose(it, lane, stage):
                dve.wait_ge(work_full, filled(it, "router", lane, stage))
                src = bank("router", lane, stage)[:, 0:TILES * E].rearrange("p (t e) -> p t e", e=E)
                dve.tensor_tensor(logits[:], src, router_b[:].unsqueeze(1).to_broadcast([P, TILES, E]), ALU.add).then_inc(freed("router", lane, stage), 1)
                dve.drain()
                for i in range(TILES):
                    dve.max(ordered[:, i, :], logits[:, i, :])
                dve.drain()
                for i in range(TILES):
                    dve.max_index(index[:, i, :], ordered[:, i, :], logits[:, i, :])
                dve.tensor_copy(top[:, bass.ds((it * LANES + lane) * TILES, TILES), :], ordered[:])
                dve.drain()
                dve.tensor_copy(index_f[:], index[:, :, 0:TOP])
                dve.drain()
                wide = [P, TILES, E]
                for i in range(TOP):
                    dve.tensor_tensor(chosen[i][:], iota_e[:].unsqueeze(1).to_broadcast(wide), index_f[:, :, i:i + 1].to_broadcast(wide), ALU.is_equal)
                dve.drain()
                dve.tensor_tensor(both[:].rearrange("p (t e) -> p t e", e=E), chosen[0][:], chosen[1][:], ALU.add).then_inc(both_ready, 1)

            def give_slots(it, lane, stage):
                dve.wait_ge(work_full, filled(it, "rank", lane, stage))
                src = bank("rank", lane, stage)[:, 0:2 * TILES * E].rearrange("p (w t e) -> p w t e", w=2, e=E)
                for i in range(TILES):
                    dve.tensor_tensor(slot_e[:, i, :], src[:, 0, i, :], next_slot[:], ALU.add)
                    dve.drain()
                    dve.tensor_tensor(next_slot[:], src[:, 1, i, :], next_slot[:], ALU.add)
                    dve.drain()
                dve.sem_inc(freed("rank", lane, stage), 1)
                for i in range(TOP):
                    dve.tensor_tensor(slot_chosen[i][:], chosen[i][:], slot_e[:], ALU.mult)
                dve.drain()
                for i in range(TOP):
                    dve.tensor_reduce(slot_f[:, i, :], slot_chosen[i][:], AX_X, ALU.add)
                dve.drain()
                dve.tensor_copy(slots[lane][:], slot_f[:]).then_inc(slots_ready, 1)
                dve.tensor_copy(slot_of[:, :, bass.ds((it * LANES + lane) * TILES, TILES)], slot_f[:])

            with dve.Fori(0, TURNS) as it:
                run(it, {"ln": norm, "centre": centre, "apply": apply_norm, "q": lo_part("q", q_hi, q_lo, bq, q_hi_ready, q_lo_ready), "k": lo_part("k", k_hi, k_lo, bk, k_hi_ready, k_lo_ready),
                              "max": row_max, "out": copy_out, "turn": normalise,
                              "wo": lambda it, lane, c: residual(it, "wo", lane, c, c),
                              "down": lambda it, lane, _: residual(it, "down", lane, FFN, FFN),
                          "router": choose, "rank": give_slots}, LAG["vector"])


def count_residuals():
    place, n = {}, 0
    for _, kind, lane, arg in STEPS:
        if kind in ("wo", "down"):
            place[kind, lane, arg] = n
            n += 1
    return place


X_PLACE = count_residuals()

def moe_part(nc, t, out, x_rows, slots_x, zeros, ident, minus_half, top, slot_of, next_slot):
    with ExitStack() as ctx:
        def sb(name, shape, dt=F32):
            return ctx.enter_context(nc.sbuf_tensor(name, shape, dt))

        def two(name, shape, dt=F32):
            return [sb(f"{name}{i}", shape, dt) for i in range(2)]

        def sem(name):
            return ctx.enter_context(nc.semaphore(name))

        x_all = sb("x_all", [P, ALL_TILES, D])
        b1 = sb("e_b1", [P, E, FC])
        gain = sb("ln3_gain", [P, D])
        shift = sb("ln3_shift", [P, D])
        iota_e = sb("iota_e", [P, E])
        iota_s = sb("iota_s", [P, PLACES])
        counts = sb("counts", [P, E])
        free_slot = sb("free_slot", [P, E], I32)
        tiles_i = sb("tiles_i", [P, E], I32)
        tiles_f = sb("tiles_f", [P, E])
        ends = [sb(f"ends{i}", [P, E]) for i in range(2)]
        past = sb("past", [P, PLACES, E])
        tiles_past = sb("tiles_past", [P, PLACES, E])
        passed = sb("passed", [P, PLACES])
        start = sb("start", [P, PLACES])
        source_f = sb("source_f", [P, PLACES])
        tile_expert = sb("tile_expert", [P, PLACES], I32)
        tile_source = sb("tile_source", [P, PLACES], I32)
        picks = TOP * ALL_TILES
        gap = sb("gap", [P, ALL_TILES, E])
        total = sb("total", [P, ALL_TILES])
        ratio = sb("ratio", [P, ALL_TILES])
        share = sb("share", [P, ALL_TILES, TOP])
        picked_f = sb("picked_f", [P, picks])
        expert_i = sb("expert_i", [P, picks], U32)
        expert_f = sb("expert_f", [P, picks])
        moved = sb("moved", [P, E])
        is_expert = sb("is_expert", [P, picks, E])
        result_slot = sb("result_slot", [P, picks], U32)
        w1 = two("e_w1", [P, KC, FF])
        w2 = two("e_w2", [P, FC, D])
        w1_hi, w1_lo = two("e_w1_hi", [P, KC, FF], F32R), two("e_w1_lo", [P, KC, FF], F32R)
        w2_hi, w2_lo = two("e_w2_hi", [P, FC, D], F32R), two("e_w2_lo", [P, FC, D], F32R)
        b1_e = two("e_b1_", [P, FC])
        b2_e = two("e_b2_", [P, D])
        rows = two("rows", [P, GT, D])
        rows_hi, rows_lo = two("rows_hi", [P, KC, GROUP], F32R), two("rows_lo", [P, KC, GROUP], F32R)
        hidden = sb("e_hidden", [P, FC, GROUP])
        hidden_hi, hidden_lo = two("e_hidden_hi", [P, FC, GROUP], F32R), two("e_hidden_lo", [P, FC, GROUP], F32R)
        result = two("result", [P, GT, D])
        GOT = 4
        got = [sb(f"got{i}", [P, TOP, TILES, D]) for i in range(GOT)]
        stats = sb("e_stats", [P, TILES, 6])
        mean_var = sb("e_mean_var", [P, TILES, 2])
        var_eps = sb("e_var_eps", [P, TILES])
        rstd = sb("e_rstd", [P, TILES])
        centred = sb("centred_e", [P, TILES, D])
        y = two("e_y", [P, TILES, D])
        bank = [ctx.enter_context(nc.psum_tensor(f"moe{i}", [P, 512], F32)) for i in range(8)]
        up_bank, down_bank, turn_bank = bank[0:4], bank[4:6], bank[6:8]
        slots_y = nc.dram_tensor("slots_y", [SLOT_TILES * GROUP, D], F32).ap()
        x_tiles = slots_x.rearrange("(s g p) d -> p (s g) d", p=P, g=GT)
        y_tiles = slots_y.rearrange("(s g p) d -> p (s g) d", p=P, g=GT)

        gate = sem("gate")
        b1_loaded = sem("b1_loaded")
        norm_loaded = sem("norm_loaded")
        x_loaded = sem("x_loaded")
        made = sem("made")
        counted = sem("counted")
        tails_zeroed = sem("tails_zeroed")
        tails_zeroed_too = sem("tails_zeroed_too")
        gaps, exps = sem("gaps"), sem("exps")
        tiles_known = sem("tiles_known")
        results_known = sem("results_known")
        w1_loaded = [sem(f"w1_loaded{i}") for i in range(2)]
        w2_loaded = [sem(f"w2_loaded{i}") for i in range(2)]
        b2_loaded = [sem(f"b2_loaded{i}") for i in range(2)]
        rows_loaded = [sem(f"rows_loaded{i}") for i in range(2)]
        w1_hi_ready = sem("w1_hi_ready")
        w1_lo_ready = sem("w1_lo_ready")
        w2_hi_ready = sem("w2_hi_ready")
        w2_lo_ready = sem("w2_lo_ready")
        rows_T_full = sem("rows_T_full")
        rows_hi_ready = sem("rows_hi_ready")
        rows_lo_ready = sem("rows_lo_ready")
        up_full = sem("up_full")
        hidden_ready = sem("e_hidden_ready")
        hidden_hi_ready = sem("hidden_hi_ready")
        hidden_lo_ready = sem("hidden_lo_ready")
        b1_ready = sem("e_b1_ready")
        down_full = sem("down_full")
        result_ready = sem("result_ready")
        written = [sem(f"written{i}") for i in range(2)]
        gathered = [sem(f"gathered{b}") for b in range(B)]
        summed = sem("summed")
        var_ready, rstd_ready = sem("e_var_ready"), sem("e_rstd_ready")
        y_ready = sem("y_ready")
        y_out = [sem(f"y_out{i}") for i in range(2)]

        QUARTERS = FC // 2
        last_tile = SLOT_TILES - 1
        def zero_tails(engine, experts, done):
            engine.wait_ge(counted, 1)
            for e in experts:
                at = engine.value_load(free_slot[0:1, e:e + 1], min_val=0, max_val=E * REGION - GROUP)
                engine.dma_start(slots_x[bass.ds(at, GROUP), :].rearrange("(g p) d -> p g d", p=P), zeros[:].unsqueeze(1).to_broadcast([P, GT, D])).then_inc(done, 16)

        block = ctx.enter_context(nc.Block())

        @block.sync
        def _(sp):
            with nc.allow_non_contiguous_dma(reason="biases"):
                sp.dma_start(b1[:], t["L1_xattn_e_b1"].rearrange("e (f p) -> p e f", p=P)).then_inc(b1_loaded, 16)
            w1_rows = t["L1_xattn_e_w1"].rearrange("e (k p) n -> p (e k) n", p=P)
            w2_rows = t["L1_xattn_e_w2"].rearrange("e (k p) n -> p (e k) n", p=P)

            def expert(s):
                return sp.value_load(tile_expert[0:1, bass.ds(s, 1)], min_val=0, max_val=E - 1)

            def source(s):
                return sp.value_load(tile_source[0:1, bass.ds(s, 1)], min_val=0, max_val=E * EXPERT_TILES)

            def fetch_first(e, i):
                sp.dma_start(w1[i][:], w1_rows[:, bass.ds(e * KC, KC), :]).then_inc(w1_loaded[i], 16)

            def fetch_second(e, i):
                sp.dma_start(w2[i][:], w2_rows[:, bass.ds(e * FC, FC), :]).then_inc(w2_loaded[i], 16)

            def fetch_bias(e, i):
                sp.dma_start(b2_e[i][:].unsqueeze(1), t["L1_xattn_e_b2"][bass.ds(e, 1), :].partition_broadcast(P)).then_inc(b2_loaded[i], 16)

            def fetch_rows(at, i):
                sp.dma_start(rows[i][:], x_tiles[:, bass.ds(at * GT, GT), :]).then_inc(rows_loaded[i], 16)

            def write(s, i):
                sp.wait_ge(result_ready, s + 1)
                sp.dma_start(y_tiles[:, bass.ds(s * GT, GT), :], result[i][:]).then_inc(written[i], 16)

            sp.wait_ge(tiles_known, 1)
            e0, e1 = expert(0), expert(1)
            fetch_first(e0, 0)
            at0, at1 = source(0), source(1)
            sp.wait_ge(tails_zeroed, 16 * (E // 2))
            sp.wait_ge(tails_zeroed_too, 16 * (E // 2))
            fetch_rows(at0, 0)
            fetch_second(e0, 0)
            fetch_rows(at1, 1)
            fetch_bias(e0, 0)
            fetch_first(e1, 1)
            fetch_second(e1, 1)
            fetch_bias(e1, 1)
            sp.dma_start(x_all[:], x_rows.rearrange("b (t p) d -> p (b t) d", p=P)).then_inc(x_loaded, 16)
            sp.dma_start(gain[:], t["L1_xattn_ln3_g"].partition_broadcast(P)).then_inc(norm_loaded, 16)
            sp.dma_start(shift[:], t["L1_xattn_ln3_b"].partition_broadcast(P)).then_inc(norm_loaded, 16)

            def step(n, i, e, at):
                sp.wait_ge(rows_T_full, n + 1)
                fetch_rows(at, i)
                sp.wait_ge(w1_lo_ready, (n + 1) * QUARTERS)
                fetch_first(e, i)
                sp.wait_ge(w2_lo_ready, (n + 1) * QUARTERS)
                fetch_second(e, i)

            e2, at2 = expert(2), source(2)
            step(0, 0, e2, at2)
            with sp.Fori(0, PAIRS) as j:
                for i in (1, 0):
                    n = j * 2 + 2 - i
                    e, next_e, at = expert(n + 2), expert(n + 1), source(n + 2)
                    step(n, i, e, at)
                    write(n - 1, 1 - i)
                    fetch_bias(next_e, 1 - i)
            write(last_tile, 0)
            for i in range(2):
                sp.wait_ge(w1_loaded[i], 16 * (PAIRS + 2 - i))
            for i in range(2):
                sp.wait_ge(w2_loaded[i], 16 * (PAIRS + 2 - i))
            sp.wait_ge(b2_loaded[0], 16 * (PAIRS + 1))
            sp.wait_ge(b2_loaded[1], 16 * (PAIRS + 1))
            for i in range(2):
                sp.wait_ge(rows_loaded[i], 16 * (PAIRS + 2 - i))
            out_rows = out.rearrange("b (t p) d -> p (b t) d", p=P)
            for b in range(B):
                sp.wait_ge(y_ready, b + 1)
                sp.dma_start(out_rows[:, b * TILES:(b + 1) * TILES, :], y[b % 2][:]).then_inc(y_out[b % 2], 16)
            for i in range(2):
                sp.wait_ge(y_out[i], 16 * (B // 2))

        @block.gpsimd
        def _(pool):
            pool.iota(iota_e[:], pattern=[[1, E]], base=0, channel_multiplier=0, allow_small_or_imprecise_dtypes=True)
            pool.iota(iota_s[:], pattern=[[1, PLACES]], base=0, channel_multiplier=0, allow_small_or_imprecise_dtypes=True)
            pool.drain()
            pool.sem_inc(made, 1)
            zero_tails(pool, range(E // 2, E), tails_zeroed_too)

            def second_high(i, nth):
                pool.wait_ge(w2_loaded[i], 16 * nth)
                pool.sem_inc(gate, 1)
                for q in range(QUARTERS):
                    pool.tensor_copy(w2_hi[i][:, 2 * q:2 * q + 2, :], w2[i][:, 2 * q:2 * q + 2, :]).then_inc(w2_hi_ready, 1)

            second_high(0, 1)
            with pool.Fori(0, PAIRS) as j:
                for i in (1, 0):
                    n = j * 2 + 2 - i
                    pool.wait_ge(up_full, n * QUARTERS + 1)
                    second_high(i, j + 2 - i)
            for i in range(2):
                pool.wait_ge(written[i], 16 * (PAIRS + 1 - i) + WRITTEN_AT_FIRST)
            pool.wait_ge(results_known, 1)

            def inverse_root(b):
                pool.wait_ge(var_ready, b + 1)
                pool.tensor_tensor(rstd[:], var_eps[:], minus_half[:], ALU.pow).then_inc(rstd_ready, 1)

            for b in range(B):
                if b >= GOT:
                    pool.wait_ge(summed, b - GOT + 1)
                for m in range(TILES):
                    for j in range(TOP):
                        at = j * ALL_TILES + b * TILES + m
                        pool.indirect_dma_start(got[b % GOT][:, j, m, :], None, slots_y, bass.IndirectOffsetOnAxis(ap=result_slot[:, at:at + 1], axis=0)).then_inc(gathered[b], 16)
                if b >= 1:
                    inverse_root(b - 1)
            inverse_root(B - 1)

        @block.tensor
        def _(pe):
            def turn(n, i, nth):
                pe.wait_ge(rows_loaded[i], 16 * nth)
                for k in range(KC):
                    for m in range(GT):
                        last = pe.transpose(turn_bank[i][:, k * GROUP + m * P:k * GROUP + (m + 1) * P], rows[i][:, m, k * P:(k + 1) * P], ident[:])
                last.then_inc(rows_T_full, 1)

            def pair_products(dst, lhs, rhs, first, end):
                for m, (a, b) in enumerate(((0, 0), (1, 0), (0, 1))):
                    last = pe.matmul(dst, lhs[a], rhs[b], start=first and m == 0, stop=end and m == 2)
                return last

            def up(n, i):
                pe.wait_ge(rows_lo_ready, n + 1)
                for q in range(QUARTERS):
                    pe.wait_ge(w1_lo_ready, n * QUARTERS + q + 1)
                    if not isinstance(n, int):
                        pe.wait_ge(hidden_ready, (n - 1) * QUARTERS + q + 1)
                    for m in range(2):
                        f = 2 * q + m
                        for k in range(KC):
                            last = pair_products(up_bank[q][:, m * GROUP:(m + 1) * GROUP], [w[i][:, k, f * P:(f + 1) * P] for w in (w1_hi, w1_lo)],
                                                 [r[i][:, k, :] for r in (rows_hi, rows_lo)], k == 0, k == KC - 1)
                    last.then_inc(up_full, 1)

            def down(n, i):
                for m in range(GT):
                    for f in range(FC):
                        if m == 0 and f % 2 == 0:
                            pe.wait_ge(w2_lo_ready, n * QUARTERS + f // 2 + 1)
                            pe.wait_ge(hidden_lo_ready, n * QUARTERS + f // 2 + 1)
                        last = pair_products(down_bank[i][:, m * D:(m + 1) * D], [h[i][:, f, m * P:(m + 1) * P] for h in (hidden_hi, hidden_lo)],
                                             [w[i][:, f, :] for w in (w2_hi, w2_lo)], f == 0, f == FC - 1)
                last.then_inc(down_full, 1)

            turn(0, 0, 1)
            up(0, 0)
            turn(1, 1, 1)
            with pe.Fori(0, PAIRS) as j:
                for i in (1, 0):
                    n = j * 2 + 2 - i
                    up(n, i)
                    turn(n + 1, 1 - i, j + 2)
                    down(n - 1, 1 - i)
            down(last_tile, 0)

        @block.scalar
        def _(act):
            def first_high(i, nth, q):
                if q == 0:
                    act.wait_ge(w1_loaded[i], 16 * nth)
                cols = slice(q * 2 * P, (q + 1) * 2 * P)
                act.activation(w1_hi[i][:, :, cols], w1[i][:, :, cols], ACT.Copy).then_inc(w1_hi_ready, 1)

            def rows_high(n, i):
                act.wait_ge(rows_T_full, n + 1)
                act.activation(rows_hi[i][:].rearrange("p k g -> p (k g)"), turn_bank[i][:], ACT.Copy).then_inc(rows_hi_ready, 1)

            def step(n, i, nth):
                act.wait_ge(b1_ready, n + 1)
                for q in range(QUARTERS):
                    first_high(1 - i, nth, q)
                    if not isinstance(n, int):
                        act.wait_ge(hidden_lo_ready, (n - 1) * QUARTERS + q + 1)
                    act.wait_ge(up_full, n * QUARTERS + q + 1)
                    for m in range(2):
                        f = 2 * q + m
                        last = act.activation(hidden[:, f, :], up_bank[q][:, m * GROUP:(m + 1) * GROUP], ACT.Gelu, bias=b1_e[i][:, f:f + 1])
                    last.then_inc(hidden_ready, 1)
                    act.drain()
                    act.activation(hidden_hi[i][:, 2 * q:2 * q + 2, :], hidden[:, 2 * q:2 * q + 2, :], ACT.Copy).then_inc(hidden_hi_ready, 1)
                rows_high(n + 1, 1 - i)

            zero_tails(act, range(E // 2), tails_zeroed)
            act.wait_ge(gaps, 1)
            act.activation(gap[:].rearrange("p t e -> p (t e)"), gap[:].rearrange("p t e -> p (t e)"), ACT.Exp).then_inc(exps, 1)
            for q in range(QUARTERS):
                first_high(0, 1, q)
            act.wait_ge(gaps, 2)
            act.activation(ratio[:], ratio[:], ACT.Exp).then_inc(exps, 1)
            rows_high(0, 0)
            step(0, 0, 1)
            with act.Fori(0, PAIRS) as j:
                for i in (1, 0):
                    step(j * 2 + 2 - i, i, j + 2)

        @block.vector
        def _(dve):
            def then(_):
                dve.drain()

            wide = [P, ALL_TILES, E]
            then(dve.tensor_copy(free_slot[:], next_slot[:]))
            dve.sem_inc(counted, 1)
            dve.tensor_tensor(gap[:], top[:], top[:, :, 0:1].to_broadcast(wide), ALU.subtract).then_inc(gaps, 1)
            dve.wait_ge(made, 1)
            then(dve.scalar_tensor_tensor(out=counts[:], in0=iota_e[:], scalar=-float(REGION), in1=next_slot[:], op0=ALU.mult, op1=ALU.add))
            then(dve.tensor_scalar(tiles_i[:], counts[:], float(GROUP - 1), None, ALU.add))
            then(dve.tensor_scalar(tiles_i[:], tiles_i[:], GROUP.bit_length() - 1, None, ALU.logical_shift_right))
            dve.tensor_copy(tiles_f[:], tiles_i[:])
            then(dve.tensor_copy(ends[0][:], tiles_i[:]))
            at = 0
            for step in (1, 2, 4):
                dve.tensor_copy(ends[1 - at][:, 0:step], ends[at][:, 0:step])
                then(dve.tensor_tensor(ends[1 - at][:, step:], ends[at][:, step:], ends[at][:, :-step], ALU.add))
                at = 1 - at
            end = ends[at]
            then(dve.tensor_tensor(past[:], end[:].unsqueeze(1).to_broadcast([P, PLACES, E]), iota_s[:].unsqueeze(2).to_broadcast([P, PLACES, E]), ALU.is_le))
            dve.tensor_tensor(tiles_past[:], past[:], tiles_f[:].unsqueeze(1).to_broadcast([P, PLACES, E]), ALU.mult)
            then(dve.tensor_reduce(passed[:], past[:], AX_X, ALU.add))
            dve.tensor_reduce(start[:], tiles_past[:], AX_X, ALU.add)
            dve.tensor_scalar(tile_expert[:], passed[:], float(E - 1), None, ALU.min)
            then(dve.scalar_tensor_tensor(out=source_f[:], in0=passed[:], scalar=float(EXPERT_TILES), in1=iota_s[:], op0=ALU.mult, op1=ALU.add))
            then(dve.tensor_tensor(source_f[:], source_f[:], start[:], ALU.subtract))
            then(dve.tensor_scalar(tile_source[:], source_f[:], float(E * EXPERT_TILES), None, ALU.min))
            dve.sem_inc(tiles_known, 1)

            def fetch_bias(s, i):
                e = dve.value_load(tile_expert[0:1, bass.ds(s, 1)], min_val=0, max_val=E - 1)
                dve.tensor_copy(b1_e[i][:].unsqueeze(1), b1[:, bass.ds(e, 1), :]).then_inc(b1_ready, 1)

            def first_low(s, i, q):
                dve.wait_ge(w1_hi_ready, s * QUARTERS + q + 1)
                cols = slice(q * 2 * P, (q + 1) * 2 * P)
                dve.tensor_tensor(w1_lo[i][:, :, cols], w1[i][:, :, cols], w1_hi[i][:, :, cols].bitcast(F32), ALU.subtract).then_inc(w1_lo_ready, 1)

            def second_low(s, i, q):
                dve.wait_ge(w2_hi_ready, s * QUARTERS + q + 1)
                dve.tensor_tensor(w2_lo[i][:, 2 * q:2 * q + 2, :], w2[i][:, 2 * q:2 * q + 2, :], w2_hi[i][:, 2 * q:2 * q + 2, :].bitcast(F32), ALU.subtract).then_inc(w2_lo_ready, 1)

            def rows_low(n, i):
                dve.wait_ge(rows_hi_ready, n + 1)
                dve.tensor_tensor(rows_lo[i][:].rearrange("p k g -> p (k g)"), turn_bank[i][:], rows_hi[i][:].bitcast(F32).rearrange("p k g -> p (k g)"), ALU.subtract).then_inc(rows_lo_ready, 1)

            def hidden_low(n, i, q):
                dve.wait_ge(hidden_hi_ready, n * QUARTERS + q + 1)
                dve.tensor_tensor(hidden_lo[i][:, 2 * q:2 * q + 2, :], hidden[:, 2 * q:2 * q + 2, :], hidden_hi[i][:, 2 * q:2 * q + 2, :].bitcast(F32), ALU.subtract).then_inc(hidden_lo_ready, 1)

            def add_bias(n, i, nth):
                dve.wait_ge(b2_loaded[i], 16 * nth)
                dve.wait_ge(written[i], 16 * nth)
                dve.wait_ge(down_full, n + 1)
                dve.tensor_tensor(result[i][:], down_bank[i][:].rearrange("p (g d) -> p g d", g=GT), b2_e[i][:].unsqueeze(1).to_broadcast([P, GT, D]), ALU.add).then_inc(result_ready, 1)

            def shares():
                dve.wait_ge(exps, 1)
                then(dve.tensor_reduce(total[:], gap[:], AX_X, ALU.add))
                then(dve.reciprocal(total[:], total[:]))
                then(dve.tensor_tensor(gap[:, :, 0:TOP], gap[:, :, 0:TOP], total[:].unsqueeze(2).to_broadcast([P, ALL_TILES, TOP]), ALU.mult))
                dve.tensor_tensor(ratio[:], gap[:, :, 1], gap[:, :, 0], ALU.subtract).then_inc(gaps, 1)
                dve.wait_ge(exps, 2)
                then(dve.tensor_scalar(total[:], ratio[:], 1.0, None, ALU.add))
                then(dve.reciprocal(share[:, :, 0], total[:]))
                then(dve.tensor_tensor(share[:, :, 1], ratio[:], share[:, :, 0], ALU.mult))

            def result_places():
                dve.tensor_copy(picked_f[:], slot_of[:].rearrange("p j t -> p (j t)"))
                then(dve.tensor_scalar(expert_i[:], slot_of[:].rearrange("p j t -> p (j t)"), REGION.bit_length() - 1, None, ALU.logical_shift_right))
                dve.tensor_copy(expert_f[:], expert_i[:])
                then(dve.tensor_tensor(moved[:], end[:], tiles_f[:], ALU.subtract))
                then(dve.scalar_tensor_tensor(out=moved[:], in0=iota_e[:], scalar=-float(EXPERT_TILES), in1=moved[:], op0=ALU.mult, op1=ALU.add))
                shape = [P, picks, E]
                then(dve.tensor_tensor(is_expert[:], expert_f[:].unsqueeze(2).to_broadcast(shape), iota_e[:].unsqueeze(1).to_broadcast(shape), ALU.is_equal))
                then(dve.tensor_tensor(is_expert[:], is_expert[:], moved[:].unsqueeze(1).to_broadcast(shape), ALU.mult))
                then(dve.tensor_reduce(expert_f[:], is_expert[:], AX_X, ALU.add))
                then(dve.scalar_tensor_tensor(out=result_slot[:], in0=expert_f[:], scalar=float(GROUP), in1=picked_f[:], op0=ALU.mult, op1=ALU.add))
                dve.sem_inc(results_known, 1)

            def step(n, i):
                fetch_bias(n + 1, 1 - i)
                for q in range(QUARTERS):
                    first_low(n + 1, 1 - i, q)
                    hidden_low(n, i, q)
                rows_low(n + 1, 1 - i)
                for q in range(QUARTERS):
                    second_low(n, i, q)

            for i in range(2):
                dve.sem_inc(written[i], WRITTEN_AT_FIRST)
            dve.wait_ge(b1_loaded, 16)
            fetch_bias(0, 0)
            for q in range(QUARTERS):
                first_low(0, 0, q)
            shares()
            rows_low(0, 0)
            step(0, 0)
            result_places()
            with dve.Fori(0, PAIRS) as j:
                for i in (1, 0):
                    n = j * 2 + 2 - i
                    step(n, i)
                    add_bias(n - 1, 1 - i, j + 1)
            add_bias(last_tile, 0, PAIRS + 1)

            dve.wait_ge(norm_loaded, 16 * 2)
            dve.wait_ge(x_loaded, 16)
            for b in range(B):
                rows_b = range(b * TILES, (b + 1) * TILES)
                dve.wait_ge(gathered[b], 16 * TOP * TILES)
                for j in range(TOP):
                    for m in rows_b:
                        last = dve.scalar_tensor_tensor(out=x_all[:, m, :], in0=got[b % GOT][:, j, m - b * TILES, :], scalar=share[:, m, j:j + 1], in1=x_all[:, m, :], op0=ALU.mult, op1=ALU.add)
                    if j == TOP - 1:
                        last.then_inc(summed, 1)
                    then(last)
                for m in rows_b:
                    last = dve.bn_stats(stats[:, m - b * TILES, :], x_all[:, m, :])
                then(last)
                for m in range(TILES):
                    last = dve.bn_aggr(mean_var[:, m, :], stats[:, m, :])
                then(last)
                dve.tensor_scalar(var_eps[:], mean_var[:, :, 1], EPS, None, ALU.add).then_inc(var_ready, 1)
                for m in rows_b:
                    last = dve.scalar_tensor_tensor(out=centred[:, m - b * TILES, :], in0=x_all[:, m, :], scalar=mean_var[:, m - b * TILES, 0:1], in1=gain[:], op0=ALU.subtract, op1=ALU.mult)
                then(last)
                dve.wait_ge(rstd_ready, b + 1)
                if b >= 2:
                    dve.wait_ge(y_out[b % 2], 16 * (b // 2))
                for m in range(TILES):
                    last = dve.scalar_tensor_tensor(out=y[b % 2][:, m, :], in0=centred[:, m, :], scalar=rstd[:, m:m + 1], in1=shift[:], op0=ALU.mult, op1=ALU.add)
                last.then_inc(y_ready, 1)
                then(last)


_OUT = ((B, S, D), "float32")


def kernel(**inputs):
    from concourse import bacc
    from concourse.bass_utils import run_bass_kernel_spmd

    nc = bacc.Bacc("TRN2", target_bir_lowering=False, num_devices=1)
    arrays, tensors = {}, {}
    for name, value in inputs.items():
        a = np.ascontiguousarray(value)
        arrays[f"in_{name}"] = a
        tensors[name] = nc.dram_tensor(f"in_{name}", a.shape, mybir.dt.from_np(a.dtype), kind="ExternalInput").ap()
    out = nc.dram_tensor("out_0", _OUT[0], F32, kind="ExternalOutput").ap()
    build(nc, tensors, out)
    r = run_bass_kernel_spmd(nc, [arrays], core_ids=[0])
    return r.results[0]["out_0"]
```
